# Optimizing a Trainium2 kernel written in Bass

```python
import numpy as np
import jax
import jax.numpy as jnp

def _softmax(x, axis=-1):
    return jax.nn.softmax(x, axis=axis)

def _gelu(x):
    return jax.nn.gelu(x, approximate=True)

def _silu(x):
    return jax.nn.silu(x)

def _sigmoid(x):
    return jax.nn.sigmoid(x)

def _layernorm(x, axis=-1, eps=1e-05):
    m = jnp.mean(x, axis=axis, keepdims=True)
    v = jnp.var(x, axis=axis, keepdims=True)
    return (x - m) / jnp.sqrt(v + eps)

def _scatter_add(tgt, idx, src, axis=0):
    return tgt.at[idx].add(src)

def _segment_sum(src, seg, n):
    return jax.ops.segment_sum(src, seg, n)
kernel_name = 'mk_adj_preln_d1_adj_r2_1c3452'

def setup_inputs(seed: int=0):
    np.random.seed(seed)
    _w = jnp.asarray

    def _rec_inputs():
        import jax
        import jax.numpy as jnp
        _gk = jax.random.key(seed)
        x = -0.0005207 + 1.001 * jax.random.normal(jax.random.fold_in(_gk, 1), (2048, 256), jnp.float32)
        _a = jax.random.bernoulli(jax.random.fold_in(_gk, 2), 0.00195312, (2048, 2048))
        _a = jnp.logical_or(_a, jnp.swapaxes(_a, -1, -2))
        _a = jnp.logical_or(_a, jnp.eye(2048, dtype=bool))
        adj = _a.astype(jnp.int32)
        _nm = jnp.ones((2048,), dtype=bool)
        nodemask = jnp.where(_nm, 1.0, 0.0).astype(jnp.int32)
        return (x, adj, nodemask)
    x, adj, nodemask = _rec_inputs()

    def _L0_gnn_setup():
        import jax, jax.numpy as jnp
        import numpy as np
        D = 256
        H = 8
        HD = D // H
        EPS = 1e-05
        NEG = -1e+30

        def layer_norm(x, scale, bias):
            mu = jnp.mean(x, axis=-1, keepdims=True)
            var = jnp.mean(jnp.square(x - mu), axis=-1, keepdims=True)
            return (x - mu) * jax.lax.rsqrt(var + EPS) * scale + bias
        key = jax.random.key(seed)
        ks = jax.random.split(key, 16)
        S = T = 2048
        inp = {'h_source': jax.random.normal(ks[0], (S, D), jnp.float32), 'h_target': jax.random.normal(ks[1], (T, D), jnp.float32), 'edge_mask': jax.random.randint(ks[2], (T, S), 0, 2, jnp.int32), 'source_mask': jnp.ones((S,), jnp.int32), 'target_mask': jnp.ones((T,), jnp.int32), 'ln1_scale': jnp.ones((D,), jnp.float32), 'ln1_bias': jnp.zeros((D,), jnp.float32), 'Wq': jax.random.normal(ks[3], (D, D), jnp.float32) / np.sqrt(D), 'bq': jnp.zeros((D,), jnp.float32), 'Wk': jax.random.normal(ks[4], (D, D), jnp.float32) / np.sqrt(D), 'bk': jnp.zeros((D,), jnp.float32), 'Wv': jax.random.normal(ks[5], (D, D), jnp.float32) / np.sqrt(D), 'bv': jnp.zeros((D,), jnp.float32), 'Wo': jax.random.normal(ks[6], (D, D), jnp.float32) / np.sqrt(D), 'bo': jnp.zeros((D,), jnp.float32), 'ln2_scale': jnp.ones((D,), jnp.float32), 'ln2_bias': jnp.zeros((D,), jnp.float32), 'W1': jax.random.normal(ks[7], (D, 4 * D), jnp.float32) / np.sqrt(D), 'W2': jax.random.normal(ks[8], (4 * D, D), jnp.float32) / np.sqrt(4 * D)}
        return inp
    _L0_gnn_all = _L0_gnn_setup()
    _L0_gnn_in = {k: v for k, v in _L0_gnn_all.items() if k in ('h_target', 'ln1_scale', 'ln1_bias', 'Wq', 'bq', 'Wk', 'bk', 'Wv', 'bv', 'Wo', 'bo', 'ln2_scale', 'ln2_bias', 'W1', 'W2')}
    del _L0_gnn_all
    return {'x': x, 'adj': adj, 'nodemask': nodemask, 'L0_gnn_h_target': _L0_gnn_in['h_target'], 'L0_gnn_ln1_scale': _L0_gnn_in['ln1_scale'], 'L0_gnn_ln1_bias': _L0_gnn_in['ln1_bias'], 'L0_gnn_Wq': _L0_gnn_in['Wq'], 'L0_gnn_bq': _L0_gnn_in['bq'], 'L0_gnn_Wk': _L0_gnn_in['Wk'], 'L0_gnn_bk': _L0_gnn_in['bk'], 'L0_gnn_Wv': _L0_gnn_in['Wv'], 'L0_gnn_bv': _L0_gnn_in['bv'], 'L0_gnn_Wo': _L0_gnn_in['Wo'], 'L0_gnn_bo': _L0_gnn_in['bo'], 'L0_gnn_ln2_scale': _L0_gnn_in['ln2_scale'], 'L0_gnn_ln2_bias': _L0_gnn_in['ln2_bias'], 'L0_gnn_W1': _L0_gnn_in['W1'], 'L0_gnn_W2': _L0_gnn_in['W2']}

def reference(x, adj, nodemask, L0_gnn_h_target, L0_gnn_ln1_scale, L0_gnn_ln1_bias, L0_gnn_Wq, L0_gnn_bq, L0_gnn_Wk, L0_gnn_bk, L0_gnn_Wv, L0_gnn_bv, L0_gnn_Wo, L0_gnn_bo, L0_gnn_ln2_scale, L0_gnn_ln2_bias, L0_gnn_W1, L0_gnn_W2):
    import jax
    import jax.numpy as jnp

    def _L0_gnn_ref(h_source, h_target, edge_mask, source_mask, target_mask, ln1_scale, ln1_bias, Wq, bq, Wk, bk, Wv, bv, Wo, bo, ln2_scale, ln2_bias, W1, W2):
        import jax, jax.numpy as jnp
        import numpy as np
        D = 256
        H = 8
        HD = D // H
        EPS = 1e-05
        NEG = -1e+30

        def layer_norm(x, scale, bias):
            mu = jnp.mean(x, axis=-1, keepdims=True)
            var = jnp.mean(jnp.square(x - mu), axis=-1, keepdims=True)
            return (x - mu) * jax.lax.rsqrt(var + EPS) * scale + bias
        smask = (source_mask == 1)[:, None]
        tmask = (target_mask == 1)[:, None]
        hs = layer_norm(h_source, ln1_scale, ln1_bias)
        ht = layer_norm(h_target, ln1_scale, ln1_bias)
        hs = jnp.where(smask, hs, 0.0)
        ht = jnp.where(tmask, ht, 0.0)
        T, S = (ht.shape[0], hs.shape[0])
        q = (ht @ Wq + bq).reshape(T, H, HD) / jnp.sqrt(jnp.float32(HD))
        k = (hs @ Wk + bk).reshape(S, H, HD)
        v = (hs @ Wv + bv).reshape(S, H, HD)
        logits = jnp.einsum('thd,shd->hts', q, k)
        logits = jnp.where(edge_mask[None] != 0, logits, NEG)
        probs = jax.nn.softmax(logits, axis=-1)
        ctx = jnp.einsum('hts,shd->thd', probs, v).reshape(T, D)
        attn = ctx @ Wo + bo
        attn = jnp.where(tmask, attn, 0.0)
        ht = ht + attn
        ht = layer_norm(ht, ln2_scale, ln2_bias)
        ht = jnp.where(tmask, ht, 0.0)
        ff = jax.nn.gelu(ht @ W1) @ W2
        return ht + ff
    h = jnp.maximum(_layernorm(x, axis=-1), 0.0)
    x = x + _L0_gnn_ref(h, L0_gnn_h_target, adj, nodemask, nodemask, L0_gnn_ln1_scale, L0_gnn_ln1_bias, L0_gnn_Wq, L0_gnn_bq, L0_gnn_Wk, L0_gnn_bk, L0_gnn_Wv, L0_gnn_bv, L0_gnn_Wo, L0_gnn_bo, L0_gnn_ln2_scale, L0_gnn_ln2_bias, L0_gnn_W1, L0_gnn_W2)
    return x

_drawn_inputs = setup_inputs


def setup_inputs(seed=0):
    import zlib

    import numpy as np

    out = dict(_drawn_inputs(seed))
    spreads = {'L0_gnn_ln1_scale': (1.0, 0.2),
     'L0_gnn_ln1_bias': (0.0, 0.1),
     'L0_gnn_bq': (0.0, 0.411),
     'L0_gnn_bk': (0.0, 0.8),
     'L0_gnn_bv': (0.0, 0.1),
     'L0_gnn_bo': (0.0, 0.1),
     'L0_gnn_ln2_scale': (1.0, 0.2),
     'L0_gnn_ln2_bias': (0.0, 0.1)}
    factors = {}
    for name, (base, spread) in spreads.items():
        noise = np.random.default_rng([zlib.crc32(name.encode()), seed]).standard_normal(out[name].shape)
        drawn = base * np.exp(spread * noise) if base else spread * noise
        out[name] = jnp.asarray(drawn.astype(out[name].dtype))
    for name, factor in factors.items():
        out[name] = (out[name] * factor).astype(out[name].dtype)
    return out
```

```python
from contextlib import ExitStack

import concourse.bass as bass
from concourse import mybir

F32 = mybir.dt.float32
F32R = mybir.dt.float32r
BF16 = mybir.dt.bfloat16
I32 = mybir.dt.int32
ACT = mybir.ActivationFunctionType
ALU = mybir.AluOpType
AX_X = mybir.AxisListType.X

P = 128
HEADS = 8
HD = 32
EPS = 1e-5
SAFE = 60.0
MASKED = -(2.0 ** 100)
CHUNK = 512
TILES = CHUNK // P
RING = 5
SLOTS = 2
RSQRT_GUESS = 0x5F3759DF
NEWTON = 3


def graph_attention(nc, x, adj, nodemask, h_target, ln1_scale, ln1_bias, Wq, bq, Wk, bk, Wv, bv, Wo, bo,
                    ln2_scale, ln2_bias, W1, W2, out):
    S, D = x.shape
    FF = W1.shape[1]
    NCH = S // CHUNK
    ST = S // P
    DC = D // P
    FC = FF // P
    GROUPS = D // P
    PER = P // HD
    PAIRS = PER // 2
    UG = ST * PAIRS
    UNITS = GROUPS * UG
    AUX = 3 * HD
    KROWS = AUX + 2
    QSCALE = float(HD) ** -0.5
    STACKS = 16 * 3 * PER
    HALF = ST // 2
    ZROW = 64

    ADDED = [i for i in range(1, ST - 1, 2)]
    ADDS = GROUPS * PAIRS * len(ADDED)

    def add_index(g, i, pair):
        return (g * len(ADDED) + ADDED.index(i)) * PAIRS + pair

    x_rows = x.rearrange("(n p) d -> p n d", p=P)
    ht_rows = h_target.rearrange("(n p) d -> p n d", p=P)
    out_rows = out.rearrange("(n p) d -> p n d", p=P)
    adj_rows = adj.rearrange("(n p) s -> n p s", p=P)
    ht_saved = nc.dram_tensor("ht_saved", [S, D], F32).ap()
    hts_rows = ht_saved.rearrange("(n p) d -> p n d", p=P)
    ctx_saved = nc.dram_tensor("ctx_saved", [D, S], F32).ap()
    sums_saved = nc.dram_tensor("sums_saved", [HEADS, S], F32).ap()
    inverse_saved = nc.dram_tensor("inverse_saved", [HEADS, S], F32).ap()

    with ExitStack() as ctx:
        def sb(name, shape, dt, scope=ctx):
            return scope.enter_context(nc.sbuf_tensor(name, shape, dt))

        def sem(name):
            return ctx.enter_context(nc.semaphore(name))

        slot = [ctx.enter_context(nc.psum_tensor(f"slot{i}", [P, 2, CHUNK], F32)) for i in range(SLOTS)]
        acc = ctx.enter_context(nc.psum_tensor("acc", [P, 2, CHUNK], F32))
        side = ctx.enter_context(nc.psum_tensor("side", [P, 2, CHUNK], F32))
        side4 = side[:].rearrange("p a (b c) -> p (a b) c", c=D)
        acc4 = acc[:].rearrange("p a (b c) -> p (a b) c", c=D)

        ident = sb("ident", [P, P], F32)
        ones = sb("ones", [P, HD], F32)
        headsum = sb("headsum", [P, P], BF16)
        zeros = sb("zeros", [2, ZROW], F32)
        gamma1 = sb("gamma1", [P, DC], F32)
        beta1 = sb("beta1", [P, DC], F32)
        nodes = sb("nodes", [P, ST], F32)
        kbias = sb("kbias", [P, GROUPS], F32)
        qbias = sb("qbias", [P, GROUPS], F32)
        vmean = sb("vmean", [P, GROUPS], F32)
        stats = sb("stats", [P, TILES, 6], F32)
        moments = sb("moments", [P, TILES, 2], F32)
        rstd = sb("rstd", [P, TILES, 1], F32)
        variance = sb("variance", [P, HALF, 1], F32)
        newton = sb("newton", [P, HALF, 1], F32)
        kmax = sb("kmax", [P, GROUPS], F32)
        nmax = sb("nmax", [P, GROUPS], F32)
        bound = sb("bound", [P, 1], F32)
        bound1 = sb("bound1", [1, 1], F32)
        flag = sb("flag", [1, 1], I32)
        mcol = sb("mcol", [P, TILES * HEADS], F32)
        sums = sb("sums", [P, HEADS * S // P], F32)
        no_edge = sb("no_edge", [P, HEADS * S // P], F32)

        att = ctx.enter_context(ExitStack())
        kst = sb("kst", [P, HEADS, S], F32R, att)
        V = sb("V", [P, ST, D], F32, att)
        early = att.enter_context(ExitStack())
        xs = sb("xs", [P, ST, D], F32, early)
        sb("even_halves", [P, 2, ST, CHUNK], BF16, early)
        w_raw = sb("w_raw", [P, 3, DC, D], F32, early)
        wk_hi = sb("wk_hi", [P, DC, D], F32R, early)
        wk_lo = sb("wk_lo", [P, DC, D], F32R, early)
        wv_hi = sb("wv_hi", [P, DC, D], F32R, early)
        wv_lo = sb("wv_lo", [P, DC, D], F32R, early)
        vbias = sb("vbias", [P, D], F32, early)
        qbias_in = sb("qbias_in", [P, GROUPS], F32, early)
        nm_int = sb("nm_int", [P, ST], I32, early)
        early.close()
        qst = sb("qst", [P, 2, HEADS, CHUNK], F32R, att)
        maskT = sb("maskT", [P, 2, ST, CHUNK], BF16, att)
        rows = sb("rows", [P, TILES, D], F32, att)
        rT_hi = sb("rT_hi", [P, DC, CHUNK], F32R, att)
        rT_lo = sb("rT_lo", [P, DC, CHUNK], F32R, att)
        proj = sb("proj", [P, GROUPS, CHUNK], F32, att)
        proj_hi = sb("proj_hi", [P, GROUPS, CHUNK], F32, att)
        adj_raw = sb("adj_raw", [P, S], BF16, att)
        evac = sb("evac", [P, 2, CHUNK], F32, att)
        wq_hi = sb("wq_hi", [P, DC, D], F32R, att)
        wq_lo = sb("wq_lo", [P, DC, D], F32R, att)
        with ExitStack() as early2:
            proj_odd = sb("proj_odd", [P, GROUPS, CHUNK], F32, early2)
            proj_hi_odd = sb("proj_hi_odd", [P, GROUPS, CHUNK], F32, early2)
            rows_first = sb("rows_first", [P, TILES, D], F32, early2)
            node_row = sb("node_row", [P, S], BF16, early2)
            stats_s = sb("stats_s", [P, ST, 6], F32, early2)
            moments_s = sb("moments_s", [P, 2, ST, 2], F32, early2)
            rstd_s = sb("rstd_s", [P, 2, ST, 1], F32, early2)
            shift_s = sb("shift_s", [P, ST, 1], F32, early2)
        probs = sb("probs", [P, RING, 2, CHUNK], F32, att)
        psum2 = sb("added", [P, PAIRS, 2, CHUNK], F32, att)
        turned_full = rows[:].rearrange("p t d -> p (t d)").rearrange("p (d t) -> p d t", d=DC)
        squares_late = turned_full.bitcast(BF16).rearrange("p d t -> p (d t)")[:, 0:GROUPS * CHUNK].rearrange(
            "p (g t) -> p g t", g=GROUPS)
        squares_early = evac[:].bitcast(BF16).rearrange("p d t -> p (d t)")[:, 0:GROUPS * CHUNK].rearrange(
            "p (g t) -> p g t", g=GROUPS)
        mneg = proj[0:TILES * HEADS, 0, 0:P]
        mrow = proj[0:TILES * HEADS, 1, 0:2 * P].bitcast(F32R).rearrange("p (a t) -> p a t", a=2)
        mpart = evac[:, 0, 0:2 * TILES * HEADS].rearrange("p (a b) -> p a b", b=2)
        qcopy = [turned_full, proj_hi[:], rT_hi[:].bitcast(F32), rT_lo[:].bitcast(F32)]
        att.close()

        ffn = ctx.enter_context(ExitStack())
        g_hi = sb("g_hi", [P, FC, CHUNK], F32R, ffn)
        g_lo = sb("g_lo", [P, FC, CHUNK], F32R, ffn)
        dT = sb("dT", [P, DC, CHUNK], F32, ffn)
        cT = sb("cT", [P, DC, CHUNK], F32, ffn)
        cT_hi = sb("cT_hi", [P, DC, CHUNK], F32R, ffn)
        cT_lo = sb("cT_lo", [P, DC, CHUNK], F32R, ffn)
        mean_part = sb("mean_part", [P, DC, CHUNK], F32, ffn)
        ht = sb("ht", [P, TILES, D], F32, ffn)
        xr = sb("xr", [P, TILES, D], F32, ffn)
        y = sb("y", [P, TILES, D], F32, ffn)
        xy = sb("xy", [P, TILES, D], F32, ffn)
        yT_hi = sb("yT_hi", [P, DC, CHUNK], F32R, ffn)
        yT_lo = sb("yT_lo", [P, DC, CHUNK], F32R, ffn)
        g_full = sb("g_full", [P, 2, CHUNK], F32, ffn)
        result = sb("result", [P, TILES, D], F32, ffn)
        gamma1_row = sb("gamma1_row", [P, D], F32, ffn)
        gamma2 = sb("gamma2", [P, D], F32, ffn)
        beta2 = sb("beta2", [P, D], F32, ffn)
        obias = sb("obias", [P, D], F32, ffn)
        beta1_row = sb("beta1_row", [P, D], F32, ffn)
        used_by_3 = 2 * FC * CHUNK * 4 + 13 * TILES * D * 4 + 5 * D * 4
        odd_end = HEADS * S * 4 + ST * D * 4 + HEADS * CHUNK * 4
        assert used_by_3 <= odd_end
        if used_by_3 < odd_end:
            sb("gap3", [P, (odd_end - used_by_3) // 4], F32, ffn)
        w1_hi = sb("w1_hi", [P, DC, FF], F32R, ffn)
        w1_lo = sb("w1_lo", [P, DC, FF], F32R, ffn)
        w2_hi = sb("w2_hi", [P, FC, D], F32R, ffn)
        w2_lo = sb("w2_lo", [P, FC, D], F32R, ffn)
        sb("odd_mask", [P, ST, CHUNK], BF16, ffn)
        w1_raw = sb("w1_raw", [P, DC, FF], F32, ffn)
        w2_raw = sb("w2_raw", [P, FC, D], F32, ffn)
        wo_raw = sb("wo_raw", [P, DC, D], F32, ffn)
        wo_hi = sb("wo_hi", [P, DC, D], F32R, ffn)
        wo_lo = sb("wo_lo", [P, DC, D], F32R, ffn)

        params_in = sem("params_in")
        nodes_in = sem("nodes_in")
        consts = sem("consts")
        pool_made = sem("pool_made")
        keys_oned = sem("keys_oned")
        w_hi_ready = sem("w_hi_ready")
        w_lo_ready = sem("w_lo_ready")
        vmean_done = sem("vmean_done")
        vmean_ready = sem("vmean_ready")
        x_rows_in = sem("x_rows_in")
        x_rest_in = sem("x_rest_in")
        norm_a = sem("norm_a")
        rectified = sem("rectified")
        norm_b = sem("norm_b")
        k_turned = sem("k_turned")
        k_affine = sem("k_affine")
        k_masked = sem("k_masked")
        k_hi = sem("k_hi")
        k_lo = sem("k_lo")
        k_projected = sem("k_projected")
        k_out = sem("k_out")
        k_squared = sem("k_squared")
        k_split_hi = sem("k_split_hi")
        k_split_lo = sem("k_split_lo")
        k_stacked = sem("k_stacked")
        v_projected = sem("v_projected")
        v_ready = sem("v_ready")
        k_norms = sem("k_norms")
        k_norm_max = sem("k_norm_max")
        rows_in = sem("rows_in")
        norm_t = sem("norm_t")
        ht_kept = sem("ht_kept")
        turned = sem("turned")
        affine_out = sem("affine_out")
        hi_ready = sem("hi_ready")
        lo_ready = sem("lo_ready")
        projected = sem("projected")
        proj_out = sem("proj_out")
        squared = sem("squared")
        split_hi = sem("split_hi")
        split_lo = sem("split_lo")
        stacked = sem("stacked")
        q_zeroed = sem("q_zeroed")
        norms = sem("norms")
        norm_max = sem("norm_max")
        bound_col = sem("bound_col")
        bound_row = sem("bound_row")
        flag_ready = sem("flag_ready")
        flag_read = sem("flag_read")
        adj_in = sem("adj_in")
        mask_turned = sem("mask_turned")
        mask_tested = sem("mask_tested")
        q_copied = sem("q_copied")
        max_adj_in = sem("max_adj_in")
        max_tested = sem("max_tested")
        max_scored = sem("max_scored")
        max_masked = sem("max_masked")
        max_taken = sem("max_taken")
        max_col = sem("max_col")
        max_turned = sem("max_turned")
        max_split = sem("max_split")
        max_stacked = sem("max_stacked")
        scored = sem("scored")
        masked = sem("masked")
        exped = sem("exped")
        used = sem("used")
        added = sem("added")
        closed = sem("closed")
        evacuated = sem("evacuated")
        saved = sem("saved")
        sums_in = sem("sums_in")
        inverted = sem("inverted")
        inverses_out = sem("inverses_out")
        stage3 = sem("stage3")
        w3_in = sem("w3_in")
        v3_in = sem("v3_in")
        w3_hi = sem("w3_hi")
        w3_lo = sem("w3_lo")
        mix_in = sem("mix_in")
        ht_in = sem("ht_in")
        x_in = sem("x_in")
        divided = sem("divided")
        c_hi = sem("c_hi")
        c_lo = sem("c_lo")
        residual = sem("residual")
        attended = sem("attended")
        mixed = sem("mixed")
        norm_y = sem("norm_y")
        y_ready = sem("y_ready")
        xy_ready = sem("xy_ready")
        y_turned = sem("y_turned")
        y_hi = sem("y_hi")
        y_lo = sem("y_lo")
        ff1 = sem("ff1")
        gelu_out = sem("gelu_out")
        g_split = sem("g_split")
        ff2 = sem("ff2")
        summed = sem("summed")
        stored = sem("stored")
        gate = {n: sem(f"gate_{n}") for n in ("sp", "pool", "dve", "pe")}

        block = ctx.enter_context(nc.Block())

        def three(mm, dst, a_hi, a_lo, b_hi, b_lo, first, last):
            mm(dst, a_hi, b_hi, start=first, stop=False)
            mm(dst, a_hi, b_lo, start=False, stop=False)
            return mm(dst, a_lo, b_hi, start=False, stop=last)

        def stat_steps(n):
            return 2 * n + 3 + 3 * NEWTON

        LN_STEPS = stat_steps(TILES) + TILES

        def layer_stats(dve, src, st, mo, rs, n, signal, base):
            va, ne = variance[:, 0:n, :], newton[:, 0:n, :]
            for t in range(n):
                nc.vector.bn_stats(st[:, t, :], src[:, t, :]).then_inc(signal, 1)
            dve.wait_ge(signal, base + n)
            dve.sem_inc(gate["dve"], 1)
            for t in range(n):
                nc.vector.bn_aggr(mo[:, t, :], st[:, t, :]).then_inc(signal, 1)
            dve.wait_ge(signal, base + 2 * n)
            done = base + 2 * n
            nc.vector.tensor_scalar(va, mo[:, :, 1:2], EPS, None, ALU.add).then_inc(signal, 1)
            dve.wait_ge(signal, done + 1)
            nc.vector.tensor_scalar(rs.bitcast(I32), va.bitcast(I32), 1, None, ALU.arith_shift_right
                                    ).then_inc(signal, 1)
            dve.wait_ge(signal, done + 2)
            nc.vector.tensor_scalar(rs.bitcast(I32), rs.bitcast(I32), -1, RSQRT_GUESS, ALU.mult, ALU.add
                                    ).then_inc(signal, 1)
            dve.wait_ge(signal, done + 3)
            for k in range(NEWTON):
                nc.vector.tensor_tensor(ne, rs, rs, ALU.mult).then_inc(signal, 1)
                dve.wait_ge(signal, done + 4 + 3 * k)
                nc.vector.scalar_tensor_tensor(out=ne, in0=va, scalar=-0.5, in1=ne, op0=ALU.mult, op1=ALU.mult
                                               ).then_inc(signal, 1)
                dve.wait_ge(signal, done + 5 + 3 * k)
                nc.vector.scalar_tensor_tensor(out=rs, in0=ne, scalar=1.5, in1=rs, op0=ALU.add, op1=ALU.mult
                                               ).then_inc(signal, 1)
                dve.wait_ge(signal, done + 6 + 3 * k)

        def layer_apply(src, mo, rs, n, signal):
            for t in range(n):
                nc.vector.tensor_scalar(src[:, t, :], src[:, t, :], mo[:, t, 0:1], rs[:, t, :],
                                        ALU.subtract, ALU.mult).then_inc(signal, 1)

        def of_chunk(c):
            return bass.ds(c * TILES, TILES)

        def cols(c):
            return bass.ds(c * CHUNK, CHUNK)

        INV = 4
        EARLY_COLS = (NCH - 1) * CHUNK

        def packed(saved_sums, part):
            ts = slice(0, EARLY_COLS) if part == 0 else slice(EARLY_COLS, S)
            n = (EARLY_COLS if part == 0 else CHUNK) * HEADS // P
            return saved_sums[:, ts].rearrange("h (a b) -> h a b", b=n)

        def places(part):
            n = EARLY_COLS * HEADS // P
            return slice(0, n) if part == 0 else slice(n, HEADS * S // P)

        def row_vector(v):
            return v.rearrange("(o d) -> o d", o=1).to_broadcast([P, D])

        KBUF = [(proj, proj_hi), (proj_odd, proj_hi_odd)]
        qst_flat = qst[:].rearrange("p b h t -> p (b h) t")
        mask_flat = maskT[:].rearrange("p b i t -> p (b i) t")

        def qpart(c):
            return (1 - c % 2) * HEADS

        @block.sync
        def _(sp):
            def after(semaphore, value):
                sp.wait_ge(semaphore, value)
                sp.sem_inc(gate["sp"], 1)

            def turn_mask(c, t, par):
                after(adj_in, 16 * (c * TILES + t + 1))
                if isinstance(c, int) and c == 0:
                    dst = mask_flat[:, 0:ST, t * P:(t + 1) * P]
                else:
                    dst = mask_flat[:, bass.ds(par * ST, ST), t * P:(t + 1) * P]
                sp.dma_start_transpose(dst, adj_raw[:]).then_inc(mask_turned, 16)

            def keep_rows(src, c):
                after(norm_t, (c + 1) * LN_STEPS)
                sp.dma_start(hts_rows[:, of_chunk(c), :], src[:]).then_inc(ht_kept, 16)

            def stack_queries(c):
                after(split_lo, c + 1)
                base = HEADS if isinstance(c, int) else sp.snap(qpart(c))
                for j in range(PER):
                    for part in range(3):
                        src = proj if part == 2 else proj_hi
                        heads = (slice(base + j, base + HEADS, PER) if isinstance(c, int)
                                 else bass.ds(base + j, GROUPS, PER))
                        sp.dma_start(qst_flat[HD * part:HD * part + HD, heads, :].bitcast(F32),
                                     src[HD * j:HD * j + HD, :, :]).then_inc(stacked, 16)
                heads = slice(base, base + HEADS) if isinstance(c, int) else bass.ds(base, HEADS)
                dst = qst_flat[AUX:KROWS, heads, :].bitcast(F32).rearrange("r h t -> r (h t)")
                sp.dma_start(dst.rearrange("r (k z) -> r k z", z=ZROW),
                             zeros[:, None, :].to_broadcast([2, HEADS * CHUNK // ZROW, ZROW])
                             ).then_inc(q_zeroed, 16)

            def load_flag():
                return sp.value_load(flag[0:1, 0:1], min_val=0, max_val=1)

            def find_maximum(c, general):
                with sp.If(general):
                    after(stacked, STACKS * (c + 1))
                    after(norms, c + 1)
                    for k in range(HEADS // 2):
                        sp.dma_start(qcopy[k][0:AUX], qst_flat[0:AUX, bass.ds(qpart(c) + 2 * k, 2), :].bitcast(F32)
                                     ).then_inc(q_copied, 16)
                    after(max_split, 2 * c + 2)
                    after(q_zeroed, 16 * (c + 1))
                    for t in range(TILES):
                        for part in range(2):
                            sp.dma_start(
                                qst_flat[AUX + part:AUX + part + 1, bass.ds(qpart(c), HEADS),
                                         t * P:(t + 1) * P].bitcast(F32),
                                mrow[t * HEADS:(t + 1) * HEADS, part, :].bitcast(F32)).then_inc(max_stacked, 16)
                with sp.Else():
                    sp.sem_inc(q_copied, 16 * (HEADS // 2))
                    sp.sem_inc(max_stacked, 16 * 2 * TILES)

            def save_context(c, g):
                G = c * GROUPS + g
                after(evacuated, 2 * (G + 1) + 2)
                sp.dma_start(ctx_saved[g * P:(g + 1) * P, cols(c)], evac[:, 0, :]).then_inc(saved, 16)
                sp.dma_start(sums_saved[g * PER:(g + 1) * PER, cols(c)], evac[0:P:HD, 1, :]).then_inc(saved, 16)

            def load_sums(part):
                sp.dma_start(sums[:, places(part)], packed(sums_saved, part)).then_inc(sums_in, 16)

            def store_inverses(part):
                sp.wait_ge(inverted, INV * (part + 1))
                sp.dma_start(packed(inverse_saved, part), sums[:, places(part)]).then_inc(inverses_out, 16)

            def column(v):
                return v.rearrange("(g p) -> p g", p=P)

            sp.dma_start(xs[:, 0:TILES, :], x_rows[:, 0:TILES, :]).then_inc(x_rows_in, 16)
            sp.dma_start(xs[:, TILES:2 * TILES, :], x_rows[:, TILES:2 * TILES, :]).then_inc(x_rows_in, 16)
            for i, w in enumerate((Wk, Wv, Wq)):
                sp.dma_start(w_raw[:, i], w.rearrange("(c p) n -> p c n", p=P)).then_inc(params_in, 16)
            sp.dma_start(xs[:, 2 * TILES:, :], x_rows[:, 2 * TILES:, :]).then_inc(x_rest_in, 16)
            sp.dma_start(vbias[:], row_vector(bv)).then_inc(params_in, 16)
            with nc.allow_non_contiguous_dma(reason="columns of small vectors"):
                for dst, src in ((kbias, bk), (qbias_in, bq), (gamma1, ln1_scale), (beta1, ln1_bias),
                                 (nm_int, nodemask)):
                    sp.dma_start(dst[:], column(src)).then_inc(params_in, 16)
            sp.dma_start(rows_first[:], ht_rows[:, 0:TILES, :]).then_inc(rows_in, 16)
            for c in range(NCH):
                turn_mask(0, c, 0)
                sp.wait_ge(k_split_lo, c + 1)
                whole, hi = KBUF[c % 2]
                for j in range(PER):
                    for part in range(3):
                        src = whole if part == 1 else hi
                        sp.dma_start(kst[HD * part:HD * part + HD, j::PER, c * CHUNK:(c + 1) * CHUNK].bitcast(F32),
                                     src[HD * j:HD * j + HD, :, :]).then_inc(k_stacked, 16)
            keep_rows(rows_first, 0)
            stack_queries(0)
            sp.sem_inc(saved, 32)
            sp.wait_ge(flag_ready, 2)
            general = load_flag()
            sp.sem_inc(flag_read, 1)
            find_maximum(0, general)

            def front(c):
                after(norms, c)
                after(max_turned, c)
                sp.dma_start(rows[:], ht_rows[:, of_chunk(c), :]).then_inc(rows_in, 16)
                after(mask_tested, 4 * c)
                after(masked, (c - 1) * UNITS + SLOTS + 1)
                turn_mask(c, 0, c % 2)
                turn_mask(c, 1, c % 2)
                keep_rows(rows, c)
                turn_mask(c, 2, c % 2)
                after(scored, (c - 1) * UNITS + 1)
                stack_queries(c)

            with sp.Fori(0, NCH - 1) as c:
                front(c + 1)
                save_context(c, 0)
                turn_mask(c + 1, 3, (c + 1) % 2)
                after(flag_ready, 2 * (c + 1) + 2)
                general = load_flag()
                sp.sem_inc(flag_read, 1)
                save_context(c, 1)
                find_maximum(c + 1, general)

            c = NCH - 1
            sp.wait_ge(stacked, STACKS * NCH)
            sp.wait_ge(max_stacked, 16 * 2 * TILES * NCH)
            sp.wait_ge(norms, NCH)
            sp.wait_ge(ht_kept, 16 * NCH)
            sp.wait_ge(mask_turned, 16 * TILES * NCH)
            sp.wait_ge(scored, c * UNITS + 1)
            sp.wait_ge(masked, c * UNITS + SLOTS + 1)
            sp.dma_start(wo_raw[:], Wo.rearrange("(c p) n -> p c n", p=P)).then_inc(w3_in, 16)
            sp.dma_start(w1_raw[:], W1.rearrange("(c p) n -> p c n", p=P)).then_inc(w3_in, 16)
            sp.dma_start(w2_raw[:], W2.rearrange("(c p) n -> p c n", p=P)).then_inc(w3_in, 16)
            sp.wait_ge(saved, 32 * (c * GROUPS + 1))
            load_sums(0)
            store_inverses(0)
            save_context(c, 0)
            save_context(c, 1)

            sp.wait_ge(saved, 32 * (NCH * GROUPS + 1))
            sp.wait_ge(used, NCH * UNITS + RING)
            sp.wait_ge(closed, NCH * GROUPS + 1)
            sp.sem_inc(stage3, 1)

            def load_mix(c):
                sp.dma_start(ht[:], hts_rows[:, of_chunk(c), :]).then_inc(ht_in, 16)
                for g in range(GROUPS):
                    heads = inverse_saved[g * PER:(g + 1) * PER, cols(c)]
                    sp.dma_start(dT[:, g, :], heads[:, None, :].to_broadcast([PER, HD, CHUNK])).then_inc(mix_in, 16)
                sp.dma_start(cT[:], ctx_saved.rearrange("(g p) t -> p g t", p=P)[:, :, cols(c)]).then_inc(mix_in, 16)

            load_sums(1)
            sp.wait_ge(inverses_out, 16)
            load_mix(0)
            for dst, src in ((gamma1_row, ln1_scale), (beta1_row, ln1_bias), (obias, bo), (gamma2, ln2_scale),
                             (beta2, ln2_bias)):
                sp.dma_start(dst[:], row_vector(src)).then_inc(v3_in, 16)
            sp.dma_start(xr[:], x_rows[:, 0:TILES, :]).then_inc(x_in, 16)
            store_inverses(1)
            sp.wait_ge(inverses_out, 32)
            with sp.Fori(0, NCH - 1) as c:
                after(c_lo, c + 1)
                after(mixed, c + 1)
                load_mix(c + 1)
                after(xy_ready, c + 1)
                sp.dma_start(xr[:], x_rows[:, of_chunk(c + 1), :]).then_inc(x_in, 16)
                after(summed, c + 1)
                sp.dma_start(out_rows[:, of_chunk(c), :], result[:]).then_inc(stored, 16)
            sp.wait_ge(summed, NCH)
            sp.dma_start(out_rows[:, (NCH - 1) * TILES:NCH * TILES, :], result[:]).then_inc(stored, 16)
            sp.wait_ge(stored, 16 * NCH)

        @block.gpsimd
        def _(pool):
            def after(semaphore, value):
                pool.wait_ge(semaphore, value)
                pool.sem_inc(gate["pool"], 1)

            def load_adj(c, t, first=False):
                if not first:
                    after(mask_turned, 16 * (c * TILES + t))
                pool.dma_start(adj_raw[:], adj_rows[bass.ds(c * TILES + t, 1)].rearrange("o p s -> (o p) s")
                               ).then_inc(adj_in, 16)

            load_adj(0, 0, first=True)
            pool.dma_start(node_row[:], nodemask.rearrange("(o s) -> o s", o=1).to_broadcast([P, S])
                           ).then_inc(nodes_in, 16)
            nc.gpsimd.memset(ident[:], 0.0).then_inc(pool_made, 1)
            nc.gpsimd.memset(ones[:], 1.0).then_inc(pool_made, 1)
            nc.gpsimd.memset(headsum[:], 0.0).then_inc(pool_made, 1)
            pool.wait_ge(pool_made, 3)
            nc.gpsimd.affine_select(out=ident[:], in_=ident[:], compare_op=ALU.not_equal, fill=1.0, base=0,
                                    pattern=[[-1, P]], channel_multiplier=1).then_inc(pool_made, 1)
            for j in range(PER):
                pool.wait_ge(pool_made, 4 + j)
                nc.gpsimd.memset(headsum[HD * j:HD * j + HD, HD * j:HD * j + HD], 1.0).then_inc(pool_made, 1)
            pool.wait_ge(pool_made, 4 + PER)
            nc.gpsimd.memset(kst[AUX:KROWS].bitcast(F32), 1.0).then_inc(keys_oned, 1)
            pool.wait_ge(keys_oned, 1)
            pool.wait_ge(consts, 1)
            wide = turned_full
            for c in range(NCH):
                pool.wait_ge(k_affine, DC * (c + 1))
                nc.gpsimd.tensor_tensor(wide, wide, node_row[:, None, c * CHUNK:(c + 1) * CHUNK].to_broadcast(
                    [P, DC, CHUNK]), ALU.mult).then_inc(k_masked, 1)
                pool.wait_ge(k_hi, c + 1)
                if c:
                    pool.wait_ge(v_projected, c)
                nc.gpsimd.tensor_tensor(rT_lo[:], wide, rT_hi[:].bitcast(F32), ALU.subtract).then_inc(k_lo, 1)
                if c:
                    whole, hi = KBUF[(c - 1) % 2]
                    pool.wait_ge(k_split_hi, c)
                    nc.gpsimd.tensor_tensor(whole[:].bitcast(F32R), whole[:], hi[:], ALU.subtract
                                            ).then_inc(k_split_lo, 1)
                if c + 1 < TILES:
                    load_adj(0, c + 1)
            whole, hi = KBUF[(NCH - 1) % 2]
            pool.wait_ge(k_split_hi, NCH)
            nc.gpsimd.tensor_tensor(whole[:].bitcast(F32R), whole[:], hi[:], ALU.subtract).then_inc(k_split_lo, 1)

            def turned_lo(c, first=False):
                pool.wait_ge(hi_ready, c + 1)
                if first:
                    pool.wait_ge(v_projected, NCH)
                nc.gpsimd.tensor_tensor(rT_lo[:], turned_full, rT_hi[:].bitcast(F32), ALU.subtract
                                        ).then_inc(lo_ready, 1)

            def queries_lo(c):
                pool.wait_ge(squared, c + 1)
                pool.wait_ge(split_hi, c + 1)
                nc.gpsimd.tensor_tensor(proj[:].bitcast(F32R), proj[:], proj_hi[:], ALU.subtract
                                        ).then_inc(split_lo, 1)

            def find_maximum(c, general):
                with pool.If(general):
                    for t in range(TILES):
                        if t:
                            after(max_taken, (c * TILES + t) * 2 * HEADS)
                        pool.dma_start(adj_raw[:], adj_rows[bass.ds(c * TILES + t, 1)].rearrange(
                            "o p s -> (o p) s")).then_inc(max_adj_in, 16)
                    after(max_taken, (c + 1) * TILES * 2 * HEADS)
                with pool.Else():
                    pool.sem_inc(max_adj_in, 16 * TILES)

            turned_lo(0, first=True)
            queries_lo(0)
            pool.wait_ge(flag_ready, 2)
            general = pool.value_load(flag[0:1, 0:1], min_val=0, max_val=1)
            pool.sem_inc(flag_read, 1)
            after(mask_turned, 16 * TILES)
            find_maximum(0, general)

            def add_up(c, g, i, pair):
                u = (g * ST + i) * PAIRS + pair
                r = probs[:, u % RING]
                k = c * ADDS + add_index(g, i, pair)
                pool.wait_ge(exped, c * UNITS + u + 1)
                if i == ADDED[0]:
                    after(closed, c * GROUPS + g + 1)
                    nc.gpsimd.tensor_copy(psum2[:, pair], r).then_inc(added, 1)
                else:
                    after(added, k - PAIRS + 1 + 1)
                    nc.gpsimd.tensor_tensor(psum2[:, pair], psum2[:, pair], r, ALU.add).then_inc(added, 1)

            def chunk(c, last):
                todo = {
                    (0, 1): lambda: load_adj(c + 1, 0), (0, 5): lambda: load_adj(c + 1, 1),
                    (0, 11): lambda: turned_lo(c + 1), (0, 13): lambda: load_adj(c + 1, 2),
                    (1, 3): lambda: queries_lo(c + 1), (1, 7): lambda: load_adj(c + 1, 3)}
                if last:
                    todo = {(0, 5): lambda: weight_lo(0), (0, 9): lambda: weight_lo(1), (1, 3): lambda: weight_lo(2)}
                for g in range(GROUPS):
                    for i in ADDED:
                        for pair in range(PAIRS):
                            add_up(c, g, i, pair)
                        if (g, i) in todo:
                            todo[g, i]()

            def weight_lo(k):
                dst, src, hi = ((wo_lo, wo_raw, wo_hi), (w1_lo, w1_raw, w1_hi), (w2_lo, w2_raw, w2_hi))[k]
                pool.wait_ge(w3_hi, k + 1)
                nc.gpsimd.tensor_tensor(dst[:], src[:], hi[:].bitcast(F32), ALU.subtract).then_inc(w3_lo, 1)

            pool.sem_inc(added, 1)
            with pool.Fori(0, NCH - 1) as c:
                chunk(c, False)
                after(flag_ready, 2 * (c + 1) + 2)
                general = pool.value_load(flag[0:1, 0:1], min_val=0, max_val=1)
                pool.sem_inc(flag_read, 1)
                after(mask_turned, 16 * TILES * (c + 2))
                find_maximum(c + 1, general)
            chunk(NCH - 1, True)

            pool.wait_ge(stage3, 1)
            pool.wait_ge(v3_in, 16 * 5)
            wide3 = [P, TILES, D]

            def make_residual(c, first=False):
                pool.wait_ge(ht_in, 16 * (c + 1))
                nc.gpsimd.tensor_tensor(ht[:], ht[:], gamma1_row[:, None, :].to_broadcast(wide3), ALU.mult
                                        ).then_inc(residual, 1)
                pool.wait_ge(residual, 2 * c + 1 + 1)
                nc.gpsimd.tensor_tensor(ht[:], ht[:], beta1_row[:, None, :].to_broadcast(wide3), ALU.add
                                        ).then_inc(residual, 1)

            def finish_y(c):
                pool.wait_ge(norm_y, (c + 1) * LN_STEPS)
                nc.gpsimd.tensor_tensor(y[:], y[:], gamma2[:, None, :].to_broadcast(wide3), ALU.mult
                                        ).then_inc(y_ready, 1)
                pool.wait_ge(y_ready, 3 * c + 1)
                nc.gpsimd.tensor_tensor(y[:], y[:], beta2[:, None, :].to_broadcast(wide3), ALU.add
                                        ).then_inc(y_ready, 1)
                pool.wait_ge(y_ready, 3 * c + 2)
                nc.gpsimd.tensor_tensor(y[:], y[:], nodes[:, of_chunk(c)][:, :, None].to_broadcast(wide3), ALU.mult
                                        ).then_inc(y_ready, 1)

            def add_x(c, first=False):
                if not first:
                    pool.wait_ge(summed, c)
                pool.wait_ge(x_in, 16 * c + 16)
                pool.wait_ge(y_ready, 3 * c + 3)
                nc.gpsimd.tensor_tensor(xy[:], xr[:], y[:], ALU.add).then_inc(xy_ready, 1)

            nc.gpsimd.tensor_tensor(beta1_row[:], beta1_row[:], obias[:], ALU.add).then_inc(residual, 1)
            pool.wait_ge(residual, 1)
            make_residual(0)
            finish_y(0)
            add_x(0, first=True)
            with pool.Fori(1, NCH) as c:
                make_residual(c)
                finish_y(c)
                add_x(c)

        @block.scalar
        def _(act):
            act.wait_ge(params_in, 16 * 9)
            nc.scalar.mul(qbias[:], qbias_in[:], QSCALE).then_inc(w_hi_ready, 1)
            for i, dst in enumerate((wk_hi, wv_hi, wq_hi)):
                nc.scalar.copy(dst[:], w_raw[:, i]).then_inc(w_hi_ready, 1)
            for half in range(2):
                act.wait_ge(norm_a, (half + 1) * (stat_steps(HALF) + 1))
                for t in range(half * HALF, (half + 1) * HALF):
                    nc.scalar.activation(xs[:, t, :], xs[:, t, :], ACT.Relu, bias=shift_s[:, t, :],
                                         scale=rstd_s[:, 0, t, :]).then_inc(rectified, 1)

            def affine(src, signal):
                for d in range(DC):
                    nc.scalar.activation(turned_full[:, d, :], src[:, d, :], ACT.Identity, bias=beta1[:, d:d + 1],
                                         scale=gamma1[:, d:d + 1]).then_inc(signal, 1)

            def source_out(c):
                whole, hi = KBUF[c % 2]
                act.wait_ge(k_projected, c + 1)
                if c >= 2:
                    act.wait_ge(k_stacked, STACKS * (c - 1))
                for g in range(GROUPS):
                    nc.scalar.activation(whole[:, g, :], slot[1][:, g, :], ACT.Identity, bias=kbias[:, g:g + 1]
                                         ).then_inc(k_out, 1)
                act.wait_ge(k_out, GROUPS * (c + 1))
                if c:
                    act.wait_ge(k_norms, c)
                nc.scalar.activation(squares_early, whole[:], ACT.Square).then_inc(k_squared, 1)
                nc.scalar.copy(hi[:].bitcast(F32R), whole[:]).then_inc(k_split_hi, 1)

            for c in range(NCH):
                act.wait_ge(k_turned, c + 1)
                if c:
                    act.wait_ge(k_lo, c)
                affine(slot[0], k_affine)
                if c:
                    source_out(c - 1)
                act.wait_ge(k_masked, c + 1)
                if c:
                    act.wait_ge(v_projected, c)
                nc.scalar.copy(rT_hi[:], turned_full).then_inc(k_hi, 1)
            source_out(NCH - 1)

            def queries_affine(c, first=False):
                act.wait_ge(turned, c + 1)
                if first:
                    act.wait_ge(k_lo, NCH)
                else:
                    act.wait_ge(ht_kept, 16 * (c + 1))
                affine(side, affine_out)
                act.wait_ge(affine_out, DC * (c + 1))
                if first:
                    act.wait_ge(v_projected, NCH)
                nc.scalar.copy(rT_hi[:], turned_full).then_inc(hi_ready, 1)

            def queries_out(c, first=False):
                act.wait_ge(projected, c + 1)
                if first:
                    act.wait_ge(k_stacked, STACKS * NCH)
                else:
                    act.wait_ge(stacked, STACKS * c)
                    act.wait_ge(max_stacked, 16 * 2 * TILES * c)
                for g in range(GROUPS):
                    nc.scalar.activation(proj[:, g, :], side[:, g, :], ACT.Identity, bias=qbias[:, g:g + 1],
                                         scale=QSCALE).then_inc(proj_out, 1)

            def queries_split(c):
                act.wait_ge(proj_out, GROUPS * (c + 1))
                act.wait_ge(lo_ready, c + 1)
                nc.scalar.activation(squares_late, proj[:], ACT.Square).then_inc(squared, 1)
                nc.scalar.copy(proj_hi[:].bitcast(F32R), proj[:]).then_inc(split_hi, 1)

            queries_affine(0, first=True)
            queries_out(0, first=True)
            queries_split(0)
            act.wait_ge(vmean_done, 1)
            nc.scalar.mul(vmean[:], acc[:, 0, 0:GROUPS], 1.0 / S).then_inc(vmean_ready, 1)
            act.wait_ge(vmean_ready, 1)
            act.sem_inc(evacuated, 2)

            def evacuate(c, g):
                G = c * GROUPS + g
                act.wait_ge(closed, G + 2)
                act.wait_ge(saved, 32 * G + 32)
                for b in range(2):
                    nc.scalar.copy(evac[:, b, :], acc[:, b, :]).then_inc(evacuated, 1)

            def weight_hi(k):
                dst, src = ((wo_hi, wo_raw), (w1_hi, w1_raw), (w2_hi, w2_raw))[k]
                act.wait_ge(w3_in, 48)
                nc.scalar.copy(dst[:], src[:]).then_inc(w3_hi, 1)

            def chunk(c, last):
                n = c + 1
                todo = {
                    24: lambda: queries_affine(n), 36: lambda: queries_out(n), 38: lambda: queries_split(n)}
                if last:
                    todo = {10: lambda: weight_hi(0), 16: lambda: weight_hi(1), 40: lambda: weight_hi(2)}
                todo[UG + 2] = lambda: evacuate(c, 0)
                for u in range(UNITS):
                    if u in todo:
                        todo[u]()
                    act.wait_ge(masked, c * UNITS + u + 1 + SLOTS)
                    r = probs[:, u % RING]
                    nc.scalar.activation(r, r, ACT.Exp).then_inc(exped, 1)
                evacuate(c, 1)

            with act.Fori(0, NCH - 1) as c:
                chunk(c, False)
            chunk(NCH - 1, True)

            def context_hi(c):
                act.wait_ge(divided, 4 * (c + 1))
                nc.scalar.copy(cT_hi[:], cT[:]).then_inc(c_hi, 1)

            def turned_y(c):
                act.wait_ge(y_turned, c + 1)
                nc.scalar.copy(yT_hi[:], side[:]).then_inc(y_hi, 1)

            def gelu(c, first=False):
                for f in range(FC):
                    act.wait_ge(ff1, c * FC + f + 1)
                    if not (first and f < 2):
                        act.wait_ge(g_split, c * FC + f - 1)
                    h = slot[f % 2][:, f // 2 % 2, :]
                    nc.scalar.activation(g_full[:, f % 2, :], h, ACT.Gelu_apprx_tanh).then_inc(gelu_out, 1)
                    nc.scalar.activation(g_hi[:, f, :], h, ACT.Gelu_apprx_tanh).then_inc(gelu_out, 1)

            context_hi(0)
            turned_y(0)
            context_hi(1)
            gelu(0, first=True)
            turned_y(1)
            with act.Fori(1, NCH - 1) as c:
                context_hi(c + 1)
                gelu(c)
                turned_y(c + 1)
            gelu(NCH - 1)

        @block.vector
        def _(dve):
            nc.vector.memset(zeros[:], 0.0).then_inc(k_norm_max, 1)
            nc.vector.memset(kmax[:], 0.0).then_inc(k_norm_max, 1)
            MADE = 2

            def first_norm(half):
                ts = slice(half * HALF, (half + 1) * HALF)
                per = stat_steps(HALF) + 1
                layer_stats(dve, xs[:, ts], stats_s[:, ts], moments_s[:, 0, ts], rstd_s[:, 0, ts], HALF, norm_a,
                            half * per)
                nc.vector.scalar_tensor_tensor(out=shift_s[:, ts], in0=moments_s[:, 0, ts, 0:1], scalar=-1.0,
                                               in1=rstd_s[:, 0, ts], op0=ALU.mult, op1=ALU.mult).then_inc(norm_a, 1)

            def second_norm(half):
                ts = slice(half * HALF, (half + 1) * HALF)
                per = stat_steps(HALF) + HALF
                dve.wait_ge(rectified, HALF * (half + 1))
                layer_stats(dve, xs[:, ts], stats_s[:, ts], moments_s[:, 1, ts], rstd_s[:, 1, ts], HALF, norm_b,
                            half * per)
                layer_apply(xs[:, ts], moments_s[:, 1, ts], rstd_s[:, 1, ts], HALF, norm_b)

            def target_norm(src, c):
                dve.wait_ge(rows_in, 16 * (c + 1))
                layer_stats(dve, src, stats, moments, rstd[:], TILES, norm_t, c * LN_STEPS)

            dve.wait_ge(x_rows_in, 32)
            first_norm(0)
            dve.wait_ge(x_rest_in, 16)
            first_norm(1)
            dve.wait_ge(params_in, 16 * 9)
            dve.wait_ge(nodes_in, 16)
            nc.vector.tensor_scalar(nodes[:], nm_int[:], 1, None, ALU.is_equal).then_inc(k_norm_max, 1)
            nc.vector.tensor_scalar(node_row[:], node_row[:], 1.0, None, ALU.is_equal).then_inc(k_norm_max, 1)
            MADE += 2
            second_norm(0)
            dve.wait_ge(k_norm_max, MADE)
            dve.sem_inc(consts, 1)
            dve.wait_ge(w_hi_ready, 4)
            for i, (dst, hi) in enumerate(((wk_lo, wk_hi), (wv_lo, wv_hi), (wq_lo, wq_hi))):
                nc.vector.tensor_tensor(dst[:], w_raw[:, i], hi[:].bitcast(F32), ALU.subtract).then_inc(w_lo_ready, 1)
            second_norm(1)
            target_norm(rows_first, 0)
            layer_apply(rows_first, moments, rstd, TILES, norm_t)

            def test_mask(c, t):
                dve.wait_ge(mask_turned, 16 * (c * TILES + t + 1))
                if isinstance(c, int) and c == 0:
                    m = mask_flat[:, 0:ST, t * P:(t + 1) * P]
                else:
                    m = mask_flat[:, bass.ds((c % 2) * ST, ST), t * P:(t + 1) * P]
                nc.vector.tensor_scalar(m, m, 0.0, None, ALU.is_equal).then_inc(mask_tested, 1)

            for c in range(NCH):
                dve.wait_ge(v_projected, c + 1)
                nc.vector.tensor_tensor(V[:, c * TILES:(c + 1) * TILES, :], acc4,
                                        vbias[:, None, :].to_broadcast([P, TILES, D]), ALU.add).then_inc(v_ready, 1)
                dve.wait_ge(k_norms, c + 1)
                dve.wait_ge(k_norm_max, MADE + 2 * c)
                nc.vector.tensor_reduce(nmax[:], side[:], AX_X, ALU.max).then_inc(k_norm_max, 1)
                dve.wait_ge(k_norm_max, MADE + 2 * c + 1)
                nc.vector.tensor_tensor(kmax[:], kmax[:], nmax[:], ALU.max).then_inc(k_norm_max, 1)
                test_mask(0, c)
            dve.wait_ge(k_norm_max, MADE + 2 * NCH)

            def target_bound(c):
                dve.wait_ge(norms, c + 1)
                nc.vector.tensor_reduce(nmax[:], side[:], AX_X, ALU.max).then_inc(norm_max, 1)
                dve.wait_ge(norm_max, 2 * c + 1)
                nc.vector.tensor_tensor(nmax[:], nmax[:], kmax[:], ALU.mult).then_inc(norm_max, 1)
                dve.wait_ge(norm_max, 2 * c + 2)
                nc.vector.tensor_reduce(bound[:], nmax[:], AX_X, ALU.max).then_inc(bound_col, 1)

            def decide(c, first=False):
                dve.wait_ge(bound_row, c + 1)
                nc.vector.tensor_reduce(bound1[:], side[0:1, 0, 0:P], AX_X, ALU.max).then_inc(flag_ready, 1)
                dve.wait_ge(flag_ready, 2 * c + 1)
                if not first:
                    dve.wait_ge(flag_read, 4 * c)
                nc.vector.tensor_scalar(flag[:], bound1[:], SAFE * SAFE, None, ALU.is_gt).then_inc(flag_ready, 1)

            def load_flag(c):
                dve.wait_ge(flag_ready, 2 * c + 2)
                dve.sem_inc(gate["dve"], 1)
                general = dve.value_load(flag[0:1, 0:1], min_val=0, max_val=1)
                dve.sem_inc(flag_read, 1)
                return general

            def find_maximum(c, general):
                with dve.If(general):
                    dve.wait_ge(stacked, STACKS * (c + 1))
                    dve.wait_ge(saved, 32 * (c * GROUPS + 1))
                    k = 0
                    for t in range(TILES):
                        dve.wait_ge(max_adj_in, 16 * (c * TILES + t + 1))
                        nc.vector.tensor_scalar(adj_raw[:], adj_raw[:], 0.0, None, ALU.is_equal
                                                ).then_inc(max_tested, 1)
                        dve.wait_ge(max_tested, c * TILES + t + 1)
                        for h in range(HEADS):
                            for half in range(2):
                                step = c * TILES * HEADS * 2 + k
                                dve.wait_ge(max_scored, step + 1)
                                if k:
                                    dve.wait_ge(max_taken, step)
                                nc.vector.scalar_tensor_tensor(
                                    out=proj[:].rearrange("p a t -> p (a t)"),
                                    in0=adj_raw[:, half * 2 * CHUNK:(half + 1) * 2 * CHUNK], scalar=MASKED,
                                    in1=side[:].rearrange("p a t -> p (a t)"), op0=ALU.mult,
                                    op1=ALU.add).then_inc(max_masked, 1)
                                dve.wait_ge(max_masked, step + 1)
                                nc.vector.tensor_reduce(mpart[:, t * HEADS + h, half:half + 1],
                                                        proj[:].rearrange("p a t -> p (a t)"), AX_X, ALU.max
                                                        ).then_inc(max_taken, 1)
                                k += 1
                    dve.wait_ge(max_taken, (c + 1) * TILES * HEADS * 2)
                    nc.vector.tensor_reduce(mcol[:], mpart, AX_X, ALU.max).then_inc(max_col, 1)
                    dve.wait_ge(max_turned, c + 1)
                    nc.vector.tensor_scalar(mneg, side[0:TILES * HEADS, 0, 0:P], -1.0, None, ALU.mult
                                            ).then_inc(max_col, 1)
                    dve.wait_ge(max_col, 2 * c + 2)
                    nc.vector.tensor_copy(mrow[:, 0, :], mneg).then_inc(max_split, 1)
                    dve.wait_ge(max_split, 2 * c + 1)
                    nc.vector.tensor_tensor(mrow[:, 1, :], mneg, mrow[:, 0, :].bitcast(F32), ALU.subtract
                                            ).then_inc(max_split, 1)
                with dve.Else():
                    dve.sem_inc(max_tested, TILES)
                    dve.sem_inc(max_masked, TILES * HEADS * 2)
                    dve.sem_inc(max_taken, TILES * HEADS * 2)
                    dve.sem_inc(max_col, 2)
                    dve.sem_inc(max_split, 2)

            target_bound(0)
            decide(0, first=True)
            dve.sem_inc(masked, SLOTS)
            general = load_flag(0)
            find_maximum(0, general)

            def invert(part):
                at = places(part)
                base = INV * part
                dve.wait_ge(sums_in, 16 * (part + 1))
                nc.vector.tensor_scalar(no_edge[:, at], sums[:, at], 0.0, None, ALU.is_equal).then_inc(inverted, 1)
                dve.wait_ge(inverted, base + 1)
                nc.vector.tensor_tensor(sums[:, at], sums[:, at], no_edge[:, at], ALU.add).then_inc(inverted, 1)
                dve.wait_ge(inverted, base + 2)
                nc.vector.reciprocal(sums[:, at], sums[:, at]).then_inc(inverted, 1)
                dve.wait_ge(inverted, base + 3)
                nc.vector.scalar_tensor_tensor(out=sums[:, at], in0=no_edge[:, at], scalar=1.0, in1=sums[:, at],
                                               op0=ALU.is_lt, op1=ALU.mult).then_inc(inverted, 1)

            def slot_free(c, u):
                return c * UNITS + (u - RING + 1 if u >= RING else min(0, u + 1 - (UNITS - UNITS // RING * RING)))

            def chunk(c, last):
                n = c + 1
                flagged = []
                todo = {20: lambda: invert(0)} if last else {
                    6: lambda: target_norm(rows, n),
                    8: lambda: layer_apply(rows, moments, rstd, TILES, norm_t),
                    14: lambda: test_mask(n, 0), 28: lambda: test_mask(n, 1), 41: lambda: target_bound(n),
                    44: lambda: test_mask(n, 2), 46: lambda: decide(n), 56: lambda: test_mask(n, 3),
                    60: lambda: flagged.append(load_flag(n))}
                for u in range(UNITS):
                    if u in todo:
                        todo[u]()
                    i = u % UG // PAIRS
                    if u == 0:
                        dve.wait_ge(mask_tested, TILES * (c + 1))
                    dve.wait_ge(scored, c * UNITS + u + 1)
                    dve.wait_ge(used, slot_free(c, u) + RING)
                    k = [add_index(g, j, pr) + 1 for g in range(GROUPS) for j in ADDED for pr in range(PAIRS)
                         if (g * ST + j) * PAIRS + pr <= u - RING]
                    dve.wait_ge(added, c * ADDS + (k[-1] if k else 0) + 1)
                    m = mask_flat[:, bass.ds((c % 2) * ST + i, 1), :].to_broadcast([P, 2, CHUNK])
                    nc.vector.scalar_tensor_tensor(out=probs[:, u % RING], in0=m, scalar=MASKED,
                                                   in1=slot[u % SLOTS][:], op0=ALU.mult, op1=ALU.add
                                                   ).then_inc(masked, 1)
                if not last:
                    find_maximum(n, flagged[0])

            with dve.Fori(0, NCH - 1) as c:
                chunk(c, False)
            chunk(NCH - 1, True)

            dve.wait_ge(stage3, 1)
            invert(1)

            def divide(c):
                dve.wait_ge(mix_in, 48 * (c + 1))
                for g in range(GROUPS):
                    nc.vector.tensor_scalar(mean_part[:, g, :], dT[:, g, :], 0.0, vmean[:, g:g + 1],
                                            ALU.is_equal, ALU.mult).then_inc(divided, 1)
                nc.vector.tensor_tensor(cT[:], cT[:], dT[:], ALU.mult).then_inc(divided, 1)
                dve.wait_ge(divided, 4 * c + 3)
                nc.vector.tensor_tensor(cT[:], cT[:], mean_part[:], ALU.add).then_inc(divided, 1)
                dve.wait_ge(c_hi, c + 1)
                nc.vector.tensor_tensor(cT_lo[:], cT[:], cT_hi[:].bitcast(F32), ALU.subtract).then_inc(c_lo, 1)

            def mix(c, first=False):
                dve.wait_ge(attended, c + 1)
                dve.wait_ge(residual, 2 * c + 3)
                if not first:
                    dve.wait_ge(xy_ready, c)
                    dve.wait_ge(y_turned, c)
                nc.vector.tensor_tensor(y[:], side4, ht[:], ALU.add).then_inc(mixed, 1)
                dve.wait_ge(mixed, c + 1)
                layer_stats(dve, y, stats, moments, rstd[:], TILES, norm_y, c * LN_STEPS)
                layer_apply(y, moments, rstd, TILES, norm_y)

            def turned_y(c):
                dve.wait_ge(y_hi, c + 1)
                nc.vector.tensor_tensor(yT_lo[:], side[:], yT_hi[:].bitcast(F32), ALU.subtract).then_inc(y_lo, 1)

            def gelu_lo(c):
                for f in range(FC):
                    dve.wait_ge(gelu_out, 2 * (c * FC + f + 1))
                    nc.vector.tensor_tensor(g_lo[:, f, :], g_full[:, f % 2, :], g_hi[:, f, :].bitcast(F32),
                                            ALU.subtract).then_inc(g_split, 1)

            def finish(c, first=False):
                dve.wait_ge(ff2, c + 1)
                dve.wait_ge(xy_ready, c + 1)
                if not first:
                    dve.wait_ge(stored, 16 * c)
                nc.vector.tensor_tensor(result[:], acc4, xy[:], ALU.add).then_inc(summed, 1)

            divide(0)
            mix(0, first=True)
            turned_y(0)
            divide(1)
            gelu_lo(0)
            mix(1)
            finish(0, first=True)
            turned_y(1)
            with dve.Fori(1, NCH - 1) as c:
                divide(c + 1)
                gelu_lo(c)
                mix(c + 1)
                finish(c)
                turned_y(c + 1)
            gelu_lo(NCH - 1)
            finish(NCH - 1)

        @block.tensor
        def _(pe):
            def turn(dst, src, t0, signal):
                for t in range(TILES):
                    for d in range(DC):
                        mm = pe.transpose(dst[:, d, t * P:(t + 1) * P], src[:, t0 + t, d * P:(d + 1) * P], ident[:])
                mm.then_inc(signal, 1)

            def project(dst, w_hi, w_lo, signal):
                for g in range(GROUPS):
                    for d in range(DC):
                        out_cols = slice(g * P, (g + 1) * P)
                        mm = three(pe.matmul, dst[:, g, :], w_hi[:, d, out_cols], w_lo[:, d, out_cols],
                                   rT_hi[:, d, :], rT_lo[:, d, :], d == 0, d == DC - 1)
                mm.then_inc(signal, 1)

            def take_norms(squares, signal):
                for g in range(GROUPS):
                    mm = pe.matmul(side[:, g, :], headsum[:], squares[:, g, :], start=True, stop=True)
                mm.then_inc(signal, 1)

            def turn_source(c):
                half = c * TILES // HALF
                pe.wait_ge(norm_b, half * (stat_steps(HALF) + HALF) + stat_steps(HALF)
                           + (c + 1) * TILES - half * HALF)
                if c:
                    pe.wait_ge(k_affine, DC * c)
                turn(slot[0], xs, c * TILES, k_turned)

            pe.wait_ge(pool_made, 4 + PER)
            turn_source(0)
            pe.wait_ge(w_lo_ready, 3)
            for c in range(NCH):
                if c + 1 < NCH:
                    turn_source(c + 1)
                pe.wait_ge(k_lo, c + 1)
                if c:
                    pe.wait_ge(k_out, GROUPS * c)
                project(slot[1], wk_hi, wk_lo, k_projected)
                if c:
                    pe.wait_ge(v_ready, c)
                for t in range(TILES):
                    for d in range(DC):
                        ts = slice(t * P, (t + 1) * P)
                        mm = three(pe.matmul, acc4[:, t, :], rT_hi[:, d, ts], rT_lo[:, d, ts],
                                   wv_hi[:, d, :], wv_lo[:, d, :], d == 0, d == DC - 1)
                mm.then_inc(v_projected, 1)
                pe.wait_ge(k_squared, c + 1)
                if c:
                    pe.wait_ge(k_norm_max, 4 + 2 * c - 1)
                take_norms(squares_early, k_norms)

            def turn_target(c, src):
                pe.wait_ge(norm_t, (c + 1) * LN_STEPS)
                turn(side, src, 0, turned)

            def project_target(c):
                pe.wait_ge(lo_ready, c + 1)
                project(side, wq_hi, wq_lo, projected)

            def target_norms(c):
                pe.wait_ge(squared, c + 1)
                take_norms(squares_late, norms)

            def bound_to_row(c):
                pe.wait_ge(bound_col, c + 1)
                pe.transpose(side[0:1, 0, 0:P], bound[:], ident[:]).then_inc(bound_row, 1)

            pe.wait_ge(k_norm_max, 4 + 2 * NCH - 1)
            turn_target(0, rows_first)
            project_target(0)
            target_norms(0)
            pe.wait_ge(v_ready, NCH)
            for g in range(GROUPS):
                for i in range(ST):
                    mm = pe.matmul(acc[:, 0, g:g + 1], V[:, i, g * P:(g + 1) * P], ones[:, 0:1],
                                   start=(i == 0), stop=(i == ST - 1))
            mm.then_inc(vmean_done, 1)
            bound_to_row(0)
            pe.sem_inc(used, RING)
            pe.sem_inc(closed, 1)

            def load_flag(c):
                pe.wait_ge(flag_ready, 2 * c + 2)
                pe.sem_inc(gate["pe"], 1)
                general = pe.value_load(flag[0:1, 0:1], min_val=0, max_val=1)
                pe.sem_inc(flag_read, 1)
                return general

            def find_maximum(c, general):
                with pe.If(general):
                    pe.wait_ge(q_copied, 16 * (HEADS // 2) * (c + 1))
                    k = 0
                    for t in range(TILES):
                        for h in range(HEADS):
                            for half in range(2):
                                step = c * TILES * HEADS * 2 + k
                                if k:
                                    pe.wait_ge(max_masked, step)
                                for b in range(2):
                                    s0 = (2 * half + b) * CHUNK
                                    mm = pe.matmul(side[:, b, :], qcopy[h // 2][0:AUX, h % 2, t * P:(t + 1) * P],
                                                   kst[0:AUX, h, s0:s0 + CHUNK].bitcast(F32), start=True, stop=True)
                                mm.then_inc(max_scored, 1)
                                k += 1
                    pe.wait_ge(max_col, 2 * c + 1)
                    pe.transpose(side[0:TILES * HEADS, 0, 0:P], mcol[:], ident[:]).then_inc(max_turned, 1)
                with pe.Else():
                    pe.sem_inc(max_scored, TILES * HEADS * 2)
                    pe.sem_inc(max_turned, 1)

            general = load_flag(0)
            find_maximum(0, general)

            def scores(c, u):
                g, i, pair = u // UG, u % UG // PAIRS, u % PAIRS
                pe.wait_ge(masked, c * UNITS + u + 1)
                for k in range(2):
                    h = g * PER + 2 * pair + k
                    mm = pe.matmul(slot[u % SLOTS][:, k, :], kst[0:KROWS, h, i * P:(i + 1) * P],
                                   qst_flat[0:KROWS, bass.ds(qpart(c) + h, 1), :].rearrange("p o t -> p (o t)"),
                                   start=True, stop=True)
                mm.then_inc(scored, 1)

            def values(c, g, i):
                u = (g * ST + i) * PAIRS
                pe.wait_ge(exped, c * UNITS + u + PAIRS)
                if i == 0:
                    pe.wait_ge(evacuated, 2 * (c * GROUPS + g) + 1)
                for j in range(PER):
                    h = g * PER + j
                    mm = pe.matmul(acc[HD * j:HD * j + HD, 0, :], V[:, i, h * HD:(h + 1) * HD],
                                   probs[:, (u + j // 2) % RING, j % 2, :], start=(i == 0), stop=(i == ST - 1))
                if i not in ADDED:
                    if i == 0:
                        pe.wait_ge(evacuated, 2 * (c * GROUPS + g) + 2)
                    for j in range(PER):
                        mm = pe.matmul(acc[HD * j:HD * j + HD, 1, :], ones[:], probs[:, (u + j // 2) % RING, j % 2, :],
                                       start=(i == 0), stop=False)
                mm.then_inc(used, PAIRS)

            def close(c, g):
                pe.wait_ge(added, c * ADDS + (g + 1) * len(ADDED) * PAIRS + 1)
                for j in range(PER):
                    mm = pe.matmul(acc[HD * j:HD * j + HD, 1, :], ones[:], psum2[:, j // 2, j % 2, :],
                                   start=False, stop=True)
                mm.then_inc(closed, 1)

            def chunk(c, last):
                n = c + 1
                todo = {} if last else {
                    10: lambda: turn_target(n, rows), 15: lambda: project_target(n), 20: lambda: target_norms(n),
                    22: lambda: bound_to_row(n)}
                pe.wait_ge(stacked, STACKS * (c + 1))
                pe.wait_ge(q_zeroed, 16 * (c + 1))
                pe.wait_ge(max_stacked, 16 * 2 * TILES * (c + 1))
                scores(c, 0)
                scores(c, 1)
                steps = GROUPS * ST
                for k in range(steps):
                    if k in todo:
                        todo[k]()
                    if k + 1 < steps:
                        for pair in range(PAIRS):
                            scores(c, (k + 1) * PAIRS + pair)
                    values(c, k // ST, k % ST)
                    if k % ST == ST - 1:
                        close(c, k // ST)

            pe.wait_ge(keys_oned, 1)
            pe.wait_ge(k_stacked, STACKS * NCH)
            with pe.Fori(0, NCH - 1) as c:
                chunk(c, False)
                general = load_flag(c + 1)
                find_maximum(c + 1, general)
            chunk(NCH - 1, True)

            pe.wait_ge(w3_lo, 3)

            def attend(c):
                pe.wait_ge(c_lo, c + 1)
                for t in range(TILES):
                    ts = slice(t * P, (t + 1) * P)
                    for d in range(DC):
                        mm = three(pe.matmul, side4[:, t, :], cT_hi[:, d, ts], cT_lo[:, d, ts],
                                   wo_hi[:, d, :], wo_lo[:, d, :], d == 0, d == DC - 1)
                mm.then_inc(attended, 1)

            def turn_y(c):
                pe.wait_ge(y_ready, 3 * c + 3)
                turn(side, y, 0, y_turned)

            def widen(c, first=False):
                pe.wait_ge(y_lo, c + 1)
                for f in range(FC):
                    if not (first and f < 4):
                        pe.wait_ge(gelu_out, 2 * (c * FC + f - 3))
                    fs = slice(f * P, (f + 1) * P)
                    for d in range(DC):
                        mm = three(pe.matmul, slot[f % 2][:, f // 2 % 2, :], w1_hi[:, d, fs], w1_lo[:, d, fs],
                                   yT_hi[:, d, :], yT_lo[:, d, :], d == 0, d == DC - 1)
                    mm.then_inc(ff1, 1)

            def narrow(c, first=False):
                pe.wait_ge(g_split, FC * (c + 1))
                if not first:
                    pe.wait_ge(summed, c)
                for t in range(TILES):
                    ts = slice(t * P, (t + 1) * P)
                    for f in range(FC):
                        mm = three(pe.matmul, acc4[:, t, :], g_hi[:, f, ts], g_lo[:, f, ts],
                                   w2_hi[:, f, :], w2_lo[:, f, :], f == 0, f == FC - 1)
                mm.then_inc(ff2, 1)

            attend(0)
            turn_y(0)
            widen(0, first=True)
            attend(1)
            narrow(0, first=True)
            turn_y(1)
            with pe.Fori(1, NCH - 1) as c:
                widen(c)
                attend(c + 1)
                narrow(c)
                turn_y(c + 1)
            widen(NCH - 1)
            narrow(NCH - 1)


_INS = ['x', 'adj', 'nodemask', 'L0_gnn_h_target', 'L0_gnn_ln1_scale', 'L0_gnn_ln1_bias', 'L0_gnn_Wq', 'L0_gnn_bq',
        'L0_gnn_Wk', 'L0_gnn_bk', 'L0_gnn_Wv', 'L0_gnn_bv', 'L0_gnn_Wo', 'L0_gnn_bo', 'L0_gnn_ln2_scale',
        'L0_gnn_ln2_bias', 'L0_gnn_W1', 'L0_gnn_W2']


def kernel(**inputs):
    import numpy as _np
    import concourse.bacc as _bacc
    from concourse import mybir as _mybir
    from concourse.bass_utils import run_bass_kernel_spmd as _run

    nc = _bacc.Bacc("TRN2", target_bir_lowering=False, num_devices=1)
    arrays, args = {}, []
    for name in _INS:
        a = _np.ascontiguousarray(inputs[name])
        arrays[f"in_{name}"] = a
        args.append(nc.dram_tensor(f"in_{name}", a.shape, _mybir.dt.from_np(a.dtype), kind="ExternalInput").ap())
    shape = inputs['x'].shape
    args.append(nc.dram_tensor("out_0", shape, _mybir.dt.float32, kind="ExternalOutput").ap())
    graph_attention(nc, *args)
    r = _run(nc, [arrays], core_ids=[0])
    return r.results[0]["out_0"]
```

```python
from contextlib import ExitStack

import concourse.bass as bass
from concourse import mybir

F32 = mybir.dt.float32
F32R = mybir.dt.float32r
BF16 = mybir.dt.bfloat16
I32 = mybir.dt.int32
ACT = mybir.ActivationFunctionType
ALU = mybir.AluOpType
AX_X = mybir.AxisListType.X

P = 128
HEADS = 8
HD = 32
EPS = 1e-5
SAFE = 60.0
MASKED = -(2.0 ** 100)
CHUNK = 512
TILES = CHUNK // P
RING = 8
SLOTS = 2
RSQRT_GUESS = 0x5F3759DF
NEWTON = 3


def graph_attention(nc, x, adj, nodemask, h_target, ln1_scale, ln1_bias, Wq, bq, Wk, bk, Wv, bv, Wo, bo,
                    ln2_scale, ln2_bias, W1, W2, out):
    S, D = x.shape
    FF = W1.shape[1]
    NCH = S // CHUNK
    ST = S // P
    DC = D // P
    FC = FF // P
    GROUPS = D // P
    PER = P // HD
    PAIRS = PER // 2
    UG = ST * PAIRS
    UNITS = GROUPS * UG
    AUX = 3 * HD
    KROWS = AUX + 2
    QSCALE = float(HD) ** -0.5
    STACKS = 16 * 3 * PER
    HALF = ST // 2
    ZROW = 64

    ADDED = [0, 1, 3, 6, 8, 11, 13]
    AHEAD = SLOTS + 4
    TAKEN = [i for i in range(ST) if i not in ADDED]
    OPS = (len(ADDED) - 1) * PAIRS
    ADDS = GROUPS * OPS

    def add_index(g, i, pair):
        return g * OPS + max(ADDED.index(i) - 1, 0) * PAIRS + pair

    x_rows = x.rearrange("(n p) d -> p n d", p=P)
    ht_rows = h_target.rearrange("(n p) d -> p n d", p=P)
    out_rows = out.rearrange("(n p) d -> p n d", p=P)
    adj_rows = adj.rearrange("(n p) s -> n p s", p=P)
    ht_saved = nc.dram_tensor("ht_saved", [S, D], F32).ap()
    hts_rows = ht_saved.rearrange("(n p) d -> p n d", p=P)
    ctx_saved = nc.dram_tensor("ctx_saved", [D, S], F32).ap()
    sums_saved = nc.dram_tensor("sums_saved", [HEADS, S], F32).ap()
    inverse_saved = nc.dram_tensor("inverse_saved", [HEADS, S], F32).ap()

    with ExitStack() as ctx:
        def sb(name, shape, dt, scope=ctx):
            return scope.enter_context(nc.sbuf_tensor(name, shape, dt))

        def sem(name):
            return ctx.enter_context(nc.semaphore(name))

        slot = [ctx.enter_context(nc.psum_tensor(f"slot{i}", [P, 2, CHUNK], F32)) for i in range(SLOTS)]
        acc = ctx.enter_context(nc.psum_tensor("acc", [P, 2, CHUNK], F32))
        side = ctx.enter_context(nc.psum_tensor("side", [P, 2, CHUNK], F32))
        side4 = side[:].rearrange("p a (b c) -> p (a b) c", c=D)
        acc4 = acc[:].rearrange("p a (b c) -> p (a b) c", c=D)

        ident = sb("ident", [P, P], F32)
        zeros = ident[0:2, P - ZROW:P]
        ones = sb("ones", [P, HD], F32)
        headsum = sb("headsum", [P, P], BF16)
        gamma1 = sb("gamma1", [P, DC], F32)
        beta1 = sb("beta1", [P, DC], F32)
        nodes = sb("nodes", [P, ST], F32)
        kbias = sb("kbias", [P, GROUPS], F32)
        qbias = sb("qbias", [P, GROUPS], F32)
        vmean = sb("vmean", [P, GROUPS], F32)
        stats = sb("stats", [P, TILES, 6], F32)
        moments = sb("moments", [P, TILES, 2], F32)
        rstd = sb("rstd", [P, TILES, 1], F32)
        variance = sb("variance", [P, HALF, 1], F32)
        newton = sb("newton", [P, HALF, 1], F32)
        kmax = sb("kmax", [P, GROUPS], F32)
        nmax = sb("nmax", [P, GROUPS], F32)
        bound = sb("bound", [P, 1], F32)
        bound1 = sb("bound1", [1, 1], F32)
        flag = sb("flag", [1, 1], I32)
        mcol = sb("mcol", [P, TILES * HEADS], F32)
        mpart = sb("mpart", [P, TILES * HEADS, 2], F32)

        att = ctx.enter_context(ExitStack())
        kst = sb("kst", [P, HEADS, S], F32R, att)
        V = sb("V", [P, ST, D], F32, att)
        early = att.enter_context(ExitStack())
        xs = sb("xs", [P, ST, D], F32, early)
        sb("even_halves", [P, 2, ST, CHUNK], BF16, early)
        w_raw = sb("w_raw", [P, 3, DC, D], F32, early)
        wk_hi = sb("wk_hi", [P, DC, D], F32R, early)
        wk_lo = sb("wk_lo", [P, DC, D], F32R, early)
        wv_hi = sb("wv_hi", [P, DC, D], F32R, early)
        wv_lo = sb("wv_lo", [P, DC, D], F32R, early)
        vbias = sb("vbias", [P, D], F32, early)
        qbias_in = sb("qbias_in", [P, GROUPS], F32, early)
        nm_int = sb("nm_int", [P, ST], I32, early)
        early.close()
        qst = sb("qst", [P, 2, HEADS, CHUNK], F32R, att)
        maskT = sb("maskT", [P, 2, ST, CHUNK], BF16, att)
        rows = sb("rows", [P, TILES, D], F32, att)
        with ExitStack() as parts:
            late_hi = sb("late_hi", [P, DC, CHUNK], F32R, parts)
            late_lo = sb("late_lo", [P, DC, CHUNK], F32R, parts)
        proj = sb("proj", [P, GROUPS, CHUNK], F32, att)
        proj_hi = sb("proj_hi", [P, GROUPS, CHUNK], F32, att)
        adj_raw = sb("adj_raw", [P, S], BF16, att)
        evac = sb("evac", [P, CHUNK], F32, att)
        wq_hi = sb("wq_hi", [P, DC, D], F32R, att)
        wq_lo = sb("wq_lo", [P, DC, D], F32R, att)
        with ExitStack() as early2:
            proj_odd = sb("proj_odd", [P, GROUPS, CHUNK], F32, early2)
            proj_hi_odd = sb("proj_hi_odd", [P, GROUPS, CHUNK], F32, early2)
            rT_hi = sb("rT_hi", [P, DC, CHUNK], F32R, early2)
            rT_lo = sb("rT_lo", [P, DC, CHUNK], F32R, early2)
            rows_first = sb("rows_first", [P, TILES, D], F32, early2)
            node_row = sb("node_row", [P, S], BF16, early2)
            stats_s = sb("stats_s", [P, ST, 6], F32, early2)
            moments_s = sb("moments_s", [P, 2, ST, 2], F32, early2)
            rstd_s = sb("rstd_s", [P, 2, ST, 1], F32, early2)
            shift_s = sb("shift_s", [P, ST, 1], F32, early2)
        probs = sb("probs", [P, RING, 2, CHUNK], F32, att)
        psum2 = sb("added", [P, PAIRS, 2, CHUNK], F32, att)
        turned_full = rows[:].rearrange("p t d -> p (t d)").rearrange("p (d t) -> p d t", d=DC)
        squares_late = turned_full.bitcast(BF16).rearrange("p d t -> p (d t)")[:, 0:GROUPS * CHUNK].rearrange(
            "p (g t) -> p g t", g=GROUPS)
        squares_early = evac[:].bitcast(BF16).rearrange("p (g t) -> p g t", g=GROUPS)
        mneg = proj[0:TILES * HEADS, 0, 0:P]
        mrow = proj[0:TILES * HEADS, 1, 0:2 * P].bitcast(F32R).rearrange("p (a t) -> p a t", a=2)
        qcopy = [turned_full, proj_hi[:]]
        att.close()

        ffn = ctx.enter_context(ExitStack())
        g_hi = sb("g_hi", [P, FC, CHUNK], F32R, ffn)
        g_lo = sb("g_lo", [P, FC, CHUNK], F32R, ffn)
        dT = sb("dT", [P, DC, CHUNK], F32, ffn)
        cT = sb("cT", [P, DC, CHUNK], F32, ffn)
        cT_hi = sb("cT_hi", [P, DC, CHUNK], F32R, ffn)
        cT_lo = sb("cT_lo", [P, DC, CHUNK], F32R, ffn)
        mean_part = sb("mean_part", [P, DC, CHUNK], F32, ffn)
        ht = sb("ht", [P, TILES, D], F32, ffn)
        xr = sb("xr", [P, TILES, D], F32, ffn)
        y = sb("y", [P, TILES, D], F32, ffn)
        xy = sb("xy", [P, TILES, D], F32, ffn)
        yT_hi = sb("yT_hi", [P, DC, CHUNK], F32R, ffn)
        yT_lo = sb("yT_lo", [P, DC, CHUNK], F32R, ffn)
        g_full = sb("g_full", [P, 2, CHUNK], F32, ffn)
        result = sb("result", [P, TILES, D], F32, ffn)
        gamma1_row = sb("gamma1_row", [P, D], F32, ffn)
        gamma2 = sb("gamma2", [P, D], F32, ffn)
        beta2 = sb("beta2", [P, D], F32, ffn)
        obias = sb("obias", [P, D], F32, ffn)
        beta1_row = sb("beta1_row", [P, D], F32, ffn)
        used_by_3 = 2 * FC * CHUNK * 4 + 13 * TILES * D * 4 + 5 * D * 4
        odd_end = HEADS * S * 4 + ST * D * 4 + HEADS * CHUNK * 4
        assert used_by_3 <= odd_end
        if used_by_3 < odd_end:
            sb("gap3", [P, (odd_end - used_by_3) // 4], F32, ffn)
        w1_hi = sb("w1_hi", [P, DC, FF], F32R, ffn)
        w1_lo = sb("w1_lo", [P, DC, FF], F32R, ffn)
        w2_hi = sb("w2_hi", [P, FC, D], F32R, ffn)
        w2_lo = sb("w2_lo", [P, FC, D], F32R, ffn)
        sb("odd_mask", [P, ST, CHUNK], BF16, ffn)
        w1_raw = sb("w1_raw", [P, DC, FF], F32, ffn)
        w2_raw = w1_raw[:].rearrange("p c n -> p (c n)").rearrange("p (f d) -> p f d", f=FC)
        wo_raw = sb("wo_raw", [P, DC, D], F32, ffn)
        wo_hi = sb("wo_hi", [P, DC, D], F32R, ffn)
        wo_lo = sb("wo_lo", [P, DC, D], F32R, ffn)
        sums = sb("sums", [P, HEADS * S // P], F32, ffn)
        no_edge = sb("no_edge", [P, HEADS * S // P], F32, ffn)

        params_in = sem("params_in")
        nodes_in = sem("nodes_in")
        consts = sem("consts")
        pool_made = sem("pool_made")
        keys_oned = sem("keys_oned")
        w_hi_ready = sem("w_hi_ready")
        w_lo_ready = sem("w_lo_ready")
        vmean_done = sem("vmean_done")
        vmean_ready = sem("vmean_ready")
        x_rows_in = sem("x_rows_in")
        x_rest_in = sem("x_rest_in")
        norm_a = sem("norm_a")
        rectified = sem("rectified")
        norm_b = sem("norm_b")
        k_turned = sem("k_turned")
        k_affine = sem("k_affine")
        k_masked = sem("k_masked")
        k_hi = sem("k_hi")
        k_lo = sem("k_lo")
        k_projected = sem("k_projected")
        k_out = sem("k_out")
        k_squared = sem("k_squared")
        k_split_hi = sem("k_split_hi")
        k_split_lo = sem("k_split_lo")
        k_stacked = sem("k_stacked")
        v_projected = sem("v_projected")
        v_ready = sem("v_ready")
        k_norms = sem("k_norms")
        k_norm_max = sem("k_norm_max")
        rows_in = sem("rows_in")
        norm_t = sem("norm_t")
        ht_kept = sem("ht_kept")
        turned = sem("turned")
        affine_out = sem("affine_out")
        hi_ready = sem("hi_ready")
        lo_ready = sem("lo_ready")
        projected = sem("projected")
        proj_out = sem("proj_out")
        squared = sem("squared")
        split_hi = sem("split_hi")
        split_lo = sem("split_lo")
        stacked = sem("stacked")
        q_zeroed = sem("q_zeroed")
        norms = sem("norms")
        norm_max = sem("norm_max")
        bound_col = sem("bound_col")
        bound_row = sem("bound_row")
        flag_ready = sem("flag_ready")
        flag_read = sem("flag_read")
        adj_in = sem("adj_in")
        mask_turned = sem("mask_turned")
        mask_tested = sem("mask_tested")
        q_copied = [sem("q_copied_even"), sem("q_copied_odd")]
        max_adj_in = sem("max_adj_in")
        max_tested = sem("max_tested")
        max_scored = sem("max_scored")
        max_masked = sem("max_masked")
        max_taken = sem("max_taken")
        max_col = sem("max_col")
        max_turned = sem("max_turned")
        max_split = sem("max_split")
        max_stacked = sem("max_stacked")
        scored = sem("scored")
        masked = sem("masked")
        exped = sem("exped")
        used = sem("used")
        added = sem("added")
        context_done = sem("context_done")
        closed = sem("closed")
        evacuated = sem("evacuated")
        saved = sem("saved")
        sums_in = sem("sums_in")
        inverted = sem("inverted")
        inverses_out = sem("inverses_out")
        stage3 = sem("stage3")
        w3_in = sem("w3_in")
        v3_in = sem("v3_in")
        w3_hi = sem("w3_hi")
        w3_lo = sem("w3_lo")
        mix_in = sem("mix_in")
        ht_in = sem("ht_in")
        x_in = sem("x_in")
        divided = sem("divided")
        c_hi = sem("c_hi")
        c_lo = sem("c_lo")
        residual = sem("residual")
        attended = sem("attended")
        mixed = sem("mixed")
        norm_y = sem("norm_y")
        y_ready = sem("y_ready")
        xy_ready = sem("xy_ready")
        y_turned = sem("y_turned")
        y_hi = sem("y_hi")
        y_lo = sem("y_lo")
        ff1 = sem("ff1")
        gelu_out = sem("gelu_out")
        g_split = sem("g_split")
        ff2 = sem("ff2")
        summed = sem("summed")
        stored = sem("stored")
        gate = {n: sem(f"gate_{n}") for n in ("sp", "pool", "dve", "pe")}

        block = ctx.enter_context(nc.Block())

        def three(mm, dst, a_hi, a_lo, b_hi, b_lo, first, last):
            mm(dst, a_hi, b_hi, start=first, stop=False)
            mm(dst, a_hi, b_lo, start=False, stop=False)
            return mm(dst, a_lo, b_hi, start=False, stop=last)

        def stat_steps(n):
            return 2 * n + 3 + 3 * NEWTON

        LN_STEPS = stat_steps(TILES) + TILES

        def layer_stats(dve, src, st, mo, rs, n, signal, base):
            va, ne = variance[:, 0:n, :], newton[:, 0:n, :]
            for t in range(n):
                nc.vector.bn_stats(st[:, t, :], src[:, t, :]).then_inc(signal, 1)
            dve.wait_ge(signal, base + n)
            dve.sem_inc(gate["dve"], 1)
            for t in range(n):
                nc.vector.bn_aggr(mo[:, t, :], st[:, t, :]).then_inc(signal, 1)
            dve.wait_ge(signal, base + 2 * n)
            done = base + 2 * n
            nc.vector.tensor_scalar(va, mo[:, :, 1:2], EPS, None, ALU.add).then_inc(signal, 1)
            dve.wait_ge(signal, done + 1)
            nc.vector.tensor_scalar(rs.bitcast(I32), va.bitcast(I32), 1, None, ALU.arith_shift_right
                                    ).then_inc(signal, 1)
            dve.wait_ge(signal, done + 2)
            nc.vector.tensor_scalar(rs.bitcast(I32), rs.bitcast(I32), -1, RSQRT_GUESS, ALU.mult, ALU.add
                                    ).then_inc(signal, 1)
            dve.wait_ge(signal, done + 3)
            for k in range(NEWTON):
                nc.vector.tensor_tensor(ne, rs, rs, ALU.mult).then_inc(signal, 1)
                dve.wait_ge(signal, done + 4 + 3 * k)
                nc.vector.scalar_tensor_tensor(out=ne, in0=va, scalar=-0.5, in1=ne, op0=ALU.mult, op1=ALU.mult
                                               ).then_inc(signal, 1)
                dve.wait_ge(signal, done + 5 + 3 * k)
                nc.vector.scalar_tensor_tensor(out=rs, in0=ne, scalar=1.5, in1=rs, op0=ALU.add, op1=ALU.mult
                                               ).then_inc(signal, 1)
                dve.wait_ge(signal, done + 6 + 3 * k)

        def layer_apply(src, mo, rs, n, signal):
            for t in range(n):
                nc.vector.tensor_scalar(src[:, t, :], src[:, t, :], mo[:, t, 0:1], rs[:, t, :],
                                        ALU.subtract, ALU.mult).then_inc(signal, 1)

        def of_chunk(c):
            return bass.ds(c * TILES, TILES)

        def cols(c):
            return bass.ds(c * CHUNK, CHUNK)

        INV = 4
        EARLY_COLS = (NCH - 1) * CHUNK

        def packed(saved_sums, part):
            ts = slice(0, EARLY_COLS) if part == 0 else slice(EARLY_COLS, S)
            n = (EARLY_COLS if part == 0 else CHUNK) * HEADS // P
            return saved_sums[:, ts].rearrange("h (a b) -> h a b", b=n)

        def places(part):
            n = EARLY_COLS * HEADS // P
            return slice(0, n) if part == 0 else slice(n, HEADS * S // P)

        def row_vector(v):
            return v.rearrange("(o d) -> o d", o=1).to_broadcast([P, D])

        KBUF = [(proj, proj_hi), (proj_odd, proj_hi_odd)]
        qst_flat = qst[:].rearrange("p b h t -> p (b h) t")
        mask_flat = maskT[:].rearrange("p b i t -> p (b i) t")

        def qpart(c):
            return (1 - c % 2) * HEADS

        @block.sync
        def _(sp):
            def after(semaphore, value):
                sp.wait_ge(semaphore, value)
                sp.sem_inc(gate["sp"], 1)

            def turn_mask(c, t, par):
                after(adj_in, 16 * (c * TILES + t + 1))
                if isinstance(c, int) and c == 0:
                    dst = mask_flat[:, 0:ST, t * P:(t + 1) * P]
                else:
                    dst = mask_flat[:, bass.ds(par * ST, ST), t * P:(t + 1) * P]
                sp.dma_start_transpose(dst, adj_raw[:]).then_inc(mask_turned, 16)

            def keep_rows(src, c):
                after(norm_t, (c + 1) * LN_STEPS)
                sp.dma_start(hts_rows[:, of_chunk(c), :], src[:]).then_inc(ht_kept, 16)

            def stack_queries(c):
                after(split_lo, c + 1)
                base = HEADS if isinstance(c, int) else sp.snap(qpart(c))
                for j in range(PER):
                    for part in range(3):
                        src = proj if part == 2 else proj_hi
                        heads = (slice(base + j, base + HEADS, PER) if isinstance(c, int)
                                 else bass.ds(base + j, GROUPS, PER))
                        sp.dma_start(qst_flat[HD * part:HD * part + HD, heads, :].bitcast(F32),
                                     src[HD * j:HD * j + HD, :, :]).then_inc(stacked, 16)
                heads = slice(base, base + HEADS) if isinstance(c, int) else bass.ds(base, HEADS)
                dst = qst_flat[AUX:KROWS, heads, :].bitcast(F32).rearrange("r h t -> r (h t)")
                sp.dma_start(dst.rearrange("r (k z) -> r k z", z=ZROW),
                             zeros[:, None, :].to_broadcast([2, HEADS * CHUNK // ZROW, ZROW])
                             ).then_inc(q_zeroed, 16)

            def load_flag():
                return sp.value_load(flag[0:1, 0:1], min_val=0, max_val=1)

            def find_maximum(c, general):
                with sp.If(general):
                    after(stacked, STACKS * (c + 1))
                    after(norms, c + 1)
                    for k in range(HEADS // 2):
                        if k > 1:
                            after(max_masked, (c * HEADS // 2 + k - 1) * TILES * PAIRS * 2)
                        sp.dma_start(qcopy[k % 2][0:AUX],
                                     qst_flat[0:AUX, bass.ds(qpart(c) + 2 * k, 2), :].bitcast(F32)
                                     ).then_inc(q_copied[k % 2], 16)
                    after(max_split, 2 * c + 2)
                    after(q_zeroed, 16 * (c + 1))
                    for t in range(TILES):
                        for part in range(2):
                            sp.dma_start(
                                qst_flat[AUX + part:AUX + part + 1, bass.ds(qpart(c), HEADS),
                                         t * P:(t + 1) * P].bitcast(F32),
                                mrow[t * HEADS:(t + 1) * HEADS, part, :].bitcast(F32)).then_inc(max_stacked, 16)
                with sp.Else():
                    for k in range(2):
                        sp.sem_inc(q_copied[k], 16 * (HEADS // 4))
                    sp.sem_inc(max_stacked, 16 * 2 * TILES)

            def save_context(c, g):
                G = c * GROUPS + g
                after(evacuated, 2 * (G + 1) + 1)
                sp.dma_start(ctx_saved[g * P:(g + 1) * P, cols(c)], evac[:]).then_inc(saved, 16)
                after(evacuated, 2 * (G + 1) + 2)
                sp.dma_start(sums_saved[g * PER:(g + 1) * PER, cols(c)], evac[0:P:HD, :]).then_inc(saved, 16)

            def load_sums(part):
                sp.dma_start(sums[:, places(part)], packed(sums_saved, part)).then_inc(sums_in, 16)

            def store_inverses(part):
                sp.wait_ge(inverted, INV * (part + 1))
                sp.dma_start(packed(inverse_saved, part), sums[:, places(part)]).then_inc(inverses_out, 16)

            def column(v):
                return v.rearrange("(g p) -> p g", p=P)

            sp.dma_start(xs[:, 0:TILES, :], x_rows[:, 0:TILES, :]).then_inc(x_rows_in, 16)
            sp.dma_start(xs[:, TILES:2 * TILES, :], x_rows[:, TILES:2 * TILES, :]).then_inc(x_rows_in, 16)
            for i, w in enumerate((Wk, Wv, Wq)):
                sp.dma_start(w_raw[:, i], w.rearrange("(c p) n -> p c n", p=P)).then_inc(params_in, 16)
            sp.dma_start(xs[:, 2 * TILES:, :], x_rows[:, 2 * TILES:, :]).then_inc(x_rest_in, 16)
            sp.dma_start(vbias[:], row_vector(bv)).then_inc(params_in, 16)
            with nc.allow_non_contiguous_dma(reason="columns of small vectors"):
                for dst, src in ((kbias, bk), (qbias_in, bq), (gamma1, ln1_scale), (beta1, ln1_bias),
                                 (nm_int, nodemask)):
                    sp.dma_start(dst[:], column(src)).then_inc(params_in, 16)
            sp.dma_start(rows_first[:], ht_rows[:, 0:TILES, :]).then_inc(rows_in, 16)
            for c in range(NCH):
                turn_mask(0, c, 0)
                sp.wait_ge(k_split_lo, c + 1)
                whole, hi = KBUF[c % 2]
                for j in range(PER):
                    for part in range(3):
                        src = whole if part == 1 else hi
                        sp.dma_start(kst[HD * part:HD * part + HD, j::PER, c * CHUNK:(c + 1) * CHUNK].bitcast(F32),
                                     src[HD * j:HD * j + HD, :, :]).then_inc(k_stacked, 16)
            keep_rows(rows_first, 0)
            stack_queries(0)
            sp.sem_inc(saved, 32)
            sp.wait_ge(flag_ready, 2)
            general = load_flag()
            sp.sem_inc(flag_read, 1)
            find_maximum(0, general)

            def front(c):
                after(norms, c)
                after(max_turned, c)
                sp.dma_start(rows[:], ht_rows[:, of_chunk(c), :]).then_inc(rows_in, 16)
                after(mask_tested, 4 * c)
                after(masked, (c - 1) * UNITS + SLOTS + 1)
                turn_mask(c, 0, c % 2)
                keep_rows(rows, c)
                turn_mask(c, 1, c % 2)
                turn_mask(c, 2, c % 2)
                save_context(c - 1, 0)
                after(scored, (c - 1) * UNITS + 1)
                stack_queries(c)

            with sp.Fori(0, NCH - 1) as c:
                front(c + 1)
                turn_mask(c + 1, 3, (c + 1) % 2)
                after(flag_ready, 2 * (c + 1) + 2)
                general = load_flag()
                sp.sem_inc(flag_read, 1)
                find_maximum(c + 1, general)
                save_context(c, 1)

            c = NCH - 1
            sp.wait_ge(stacked, STACKS * NCH)
            sp.wait_ge(max_stacked, 16 * 2 * TILES * NCH)
            sp.wait_ge(norms, NCH)
            sp.wait_ge(ht_kept, 16 * NCH)
            sp.wait_ge(mask_turned, 16 * TILES * NCH)
            sp.wait_ge(scored, c * UNITS + 1)
            sp.wait_ge(masked, c * UNITS + SLOTS + 1)
            sp.dma_start(wo_raw[:], Wo.rearrange("(c p) n -> p c n", p=P)).then_inc(w3_in, 16)
            sp.dma_start(w1_raw[:], W1.rearrange("(c p) n -> p c n", p=P)).then_inc(w3_in, 16)
            sp.wait_ge(saved, 32 * (c * GROUPS + 1))
            load_sums(0)
            store_inverses(0)
            save_context(c, 0)
            sp.wait_ge(w3_lo, 2)
            sp.dma_start(w2_raw, W2.rearrange("(c p) n -> p c n", p=P)).then_inc(w3_in, 16)
            save_context(c, 1)

            sp.wait_ge(saved, 32 * (NCH * GROUPS + 1))
            sp.wait_ge(used, NCH * UNITS + RING)
            sp.wait_ge(closed, NCH * GROUPS + 1)
            sp.sem_inc(stage3, 1)

            def load_mix(c):
                sp.dma_start(ht[:], hts_rows[:, of_chunk(c), :]).then_inc(ht_in, 16)
                for g in range(GROUPS):
                    heads = inverse_saved[g * PER:(g + 1) * PER, cols(c)]
                    sp.dma_start(dT[:, g, :], heads[:, None, :].to_broadcast([PER, HD, CHUNK])).then_inc(mix_in, 16)
                sp.dma_start(cT[:], ctx_saved.rearrange("(g p) t -> p g t", p=P)[:, :, cols(c)]).then_inc(mix_in, 16)

            load_sums(1)
            sp.wait_ge(inverses_out, 16)
            load_mix(0)
            for dst, src in ((gamma1_row, ln1_scale), (beta1_row, ln1_bias), (obias, bo), (gamma2, ln2_scale),
                             (beta2, ln2_bias)):
                sp.dma_start(dst[:], row_vector(src)).then_inc(v3_in, 16)
            sp.dma_start(xr[:], x_rows[:, 0:TILES, :]).then_inc(x_in, 16)
            store_inverses(1)
            sp.wait_ge(inverses_out, 32)
            with sp.Fori(0, NCH - 1) as c:
                after(c_lo, c + 1)
                after(mixed, c + 1)
                load_mix(c + 1)
                after(xy_ready, c + 1)
                sp.dma_start(xr[:], x_rows[:, of_chunk(c + 1), :]).then_inc(x_in, 16)
                after(summed, c + 1)
                sp.dma_start(out_rows[:, of_chunk(c), :], result[:]).then_inc(stored, 16)
            sp.wait_ge(summed, NCH)
            sp.dma_start(out_rows[:, (NCH - 1) * TILES:NCH * TILES, :], result[:]).then_inc(stored, 16)
            sp.wait_ge(stored, 16 * NCH)

        @block.gpsimd
        def _(pool):
            def after(semaphore, value):
                pool.wait_ge(semaphore, value)
                pool.sem_inc(gate["pool"], 1)

            def load_adj(c, t, first=False):
                if not first:
                    after(mask_turned, 16 * (c * TILES + t))
                pool.dma_start(adj_raw[:], adj_rows[bass.ds(c * TILES + t, 1)].rearrange("o p s -> (o p) s")
                               ).then_inc(adj_in, 16)

            load_adj(0, 0, first=True)
            pool.dma_start(node_row[:], nodemask.rearrange("(o s) -> o s", o=1).to_broadcast([P, S])
                           ).then_inc(nodes_in, 16)
            nc.gpsimd.memset(ident[:], 0.0).then_inc(pool_made, 1)
            nc.gpsimd.memset(ones[:], 1.0).then_inc(pool_made, 1)
            nc.gpsimd.memset(headsum[:], 0.0).then_inc(pool_made, 1)
            pool.wait_ge(pool_made, 3)
            nc.gpsimd.affine_select(out=ident[:], in_=ident[:], compare_op=ALU.not_equal, fill=1.0, base=0,
                                    pattern=[[-1, P]], channel_multiplier=1).then_inc(pool_made, 1)
            for j in range(PER):
                pool.wait_ge(pool_made, 4 + j)
                nc.gpsimd.memset(headsum[HD * j:HD * j + HD, HD * j:HD * j + HD], 1.0).then_inc(pool_made, 1)
            pool.wait_ge(pool_made, 4 + PER)
            nc.gpsimd.memset(kst[AUX:KROWS].bitcast(F32), 1.0).then_inc(keys_oned, 1)
            pool.wait_ge(keys_oned, 1)
            pool.wait_ge(consts, 1)
            wide = turned_full
            for c in range(NCH):
                pool.wait_ge(k_affine, DC * (c + 1))
                nc.gpsimd.tensor_tensor(wide, wide, node_row[:, None, c * CHUNK:(c + 1) * CHUNK].to_broadcast(
                    [P, DC, CHUNK]), ALU.mult).then_inc(k_masked, 1)
                pool.wait_ge(k_hi, c + 1)
                if c:
                    pool.wait_ge(v_projected, c)
                nc.gpsimd.tensor_tensor(rT_lo[:], wide, rT_hi[:].bitcast(F32), ALU.subtract).then_inc(k_lo, 1)
                if c:
                    whole, hi = KBUF[(c - 1) % 2]
                    pool.wait_ge(k_split_hi, c)
                    nc.gpsimd.tensor_tensor(whole[:].bitcast(F32R), whole[:], hi[:], ALU.subtract
                                            ).then_inc(k_split_lo, 1)
                if c + 1 < TILES:
                    load_adj(0, c + 1)
            whole, hi = KBUF[(NCH - 1) % 2]
            pool.wait_ge(k_split_hi, NCH)
            nc.gpsimd.tensor_tensor(whole[:].bitcast(F32R), whole[:], hi[:], ALU.subtract).then_inc(k_split_lo, 1)

            def turned_lo(c, hi, lo):
                pool.wait_ge(hi_ready, c + 1)
                nc.gpsimd.tensor_tensor(lo, turned_full, hi.bitcast(F32), ALU.subtract).then_inc(lo_ready, 1)

            def queries_lo(c):
                pool.wait_ge(squared, c + 1)
                pool.wait_ge(split_hi, c + 1)
                nc.gpsimd.tensor_tensor(proj[:].bitcast(F32R), proj[:], proj_hi[:], ALU.subtract
                                        ).then_inc(split_lo, 1)

            def find_maximum(c, general):
                with pool.If(general):
                    for k in range(HEADS // 2):
                        for t in range(TILES):
                            if k or t:
                                after(max_masked, ((c * HEADS // 2 + k) * TILES + t) * 2 * 2)
                            pool.dma_start(adj_raw[:], adj_rows[bass.ds(c * TILES + t, 1)].rearrange(
                                "o p s -> (o p) s")).then_inc(max_adj_in, 16)
                    after(max_masked, (c + 1) * TILES * 2 * HEADS)
                with pool.Else():
                    pool.sem_inc(max_adj_in, 16 * TILES * HEADS // 2)

            pool.wait_ge(v_projected, NCH)
            turned_lo(0, rT_hi[:], rT_lo[:])
            queries_lo(0)
            pool.wait_ge(flag_ready, 2)
            general = pool.value_load(flag[0:1, 0:1], min_val=0, max_val=1)
            pool.sem_inc(flag_read, 1)
            after(mask_turned, 16 * TILES)
            find_maximum(0, general)

            def add_up(c, g, i, pair):
                def at(tile):
                    return probs[:, ((g * ST + tile) * PAIRS + pair) % RING]
                k = c * ADDS + add_index(g, i, pair)
                pool.wait_ge(exped, c * UNITS + (g * ST + i) * PAIRS + pair + 1)
                if i == ADDED[1]:
                    after(closed, c * GROUPS + g + 1)
                    nc.gpsimd.tensor_tensor(psum2[:, pair], at(ADDED[0]), at(i), ALU.add).then_inc(added, 1)
                else:
                    after(added, k - PAIRS + 1 + 1)
                    nc.gpsimd.tensor_tensor(psum2[:, pair], psum2[:, pair], at(i), ALU.add).then_inc(added, 1)

            def chunk(c, last):
                todo = {
                    (0, 1): lambda: load_adj(c + 1, 0), (0, 6): lambda: load_adj(c + 1, 1),
                    (0, 11): lambda: turned_lo(c + 1, late_hi[:], late_lo[:]), (0, 13): lambda: load_adj(c + 1, 2),
                    (1, 1): lambda: queries_lo(c + 1), (1, 3): lambda: load_adj(c + 1, 3)}
                if last:
                    todo = {(0, 6): lambda: weight_lo(0), (0, 11): lambda: weight_lo(1), (1, 11): lambda: weight_lo(2)}
                for g in range(GROUPS):
                    for i in ADDED[1:]:
                        for pair in range(PAIRS):
                            add_up(c, g, i, pair)
                        if (g, i) in todo:
                            todo[g, i]()

            def weight_lo(k):
                dst, src, hi = ((wo_lo, wo_raw[:], wo_hi), (w1_lo, w1_raw[:], w1_hi), (w2_lo, w2_raw, w2_hi))[k]
                pool.wait_ge(w3_hi, k + 1)
                nc.gpsimd.tensor_tensor(dst[:], src, hi[:].bitcast(F32), ALU.subtract).then_inc(w3_lo, 1)

            pool.sem_inc(added, 1)
            with pool.Fori(0, NCH - 1) as c:
                chunk(c, False)
                after(flag_ready, 2 * (c + 1) + 2)
                general = pool.value_load(flag[0:1, 0:1], min_val=0, max_val=1)
                pool.sem_inc(flag_read, 1)
                after(mask_turned, 16 * TILES * (c + 2))
                find_maximum(c + 1, general)
            chunk(NCH - 1, True)

            pool.wait_ge(stage3, 1)
            pool.wait_ge(v3_in, 16 * 5)
            wide3 = [P, TILES, D]

            def make_residual(c, first=False):
                pool.wait_ge(ht_in, 16 * (c + 1))
                nc.gpsimd.tensor_tensor(ht[:], ht[:], gamma1_row[:, None, :].to_broadcast(wide3), ALU.mult
                                        ).then_inc(residual, 1)
                pool.wait_ge(residual, 2 * c + 1 + 1)
                nc.gpsimd.tensor_tensor(ht[:], ht[:], beta1_row[:, None, :].to_broadcast(wide3), ALU.add
                                        ).then_inc(residual, 1)

            def finish_y(c):
                pool.wait_ge(norm_y, (c + 1) * LN_STEPS)
                nc.gpsimd.tensor_tensor(y[:], y[:], gamma2[:, None, :].to_broadcast(wide3), ALU.mult
                                        ).then_inc(y_ready, 1)
                pool.wait_ge(y_ready, 3 * c + 1)
                nc.gpsimd.tensor_tensor(y[:], y[:], beta2[:, None, :].to_broadcast(wide3), ALU.add
                                        ).then_inc(y_ready, 1)
                pool.wait_ge(y_ready, 3 * c + 2)
                nc.gpsimd.tensor_tensor(y[:], y[:], nodes[:, of_chunk(c)][:, :, None].to_broadcast(wide3), ALU.mult
                                        ).then_inc(y_ready, 1)

            def add_x(c, first=False):
                if not first:
                    pool.wait_ge(summed, c)
                pool.wait_ge(x_in, 16 * c + 16)
                pool.wait_ge(y_ready, 3 * c + 3)
                nc.gpsimd.tensor_tensor(xy[:], xr[:], y[:], ALU.add).then_inc(xy_ready, 1)

            nc.gpsimd.tensor_tensor(beta1_row[:], beta1_row[:], obias[:], ALU.add).then_inc(residual, 1)
            pool.wait_ge(residual, 1)
            make_residual(0)
            finish_y(0)
            add_x(0, first=True)
            with pool.Fori(1, NCH) as c:
                make_residual(c)
                finish_y(c)
                add_x(c)

        @block.scalar
        def _(act):
            act.wait_ge(params_in, 16 * 9)
            nc.scalar.mul(qbias[:], qbias_in[:], QSCALE).then_inc(w_hi_ready, 1)
            for i, dst in enumerate((wk_hi, wv_hi, wq_hi)):
                nc.scalar.copy(dst[:], w_raw[:, i]).then_inc(w_hi_ready, 1)
            for half in range(2):
                act.wait_ge(norm_a, (half + 1) * (stat_steps(HALF) + 1))
                for t in range(half * HALF, (half + 1) * HALF):
                    nc.scalar.activation(xs[:, t, :], xs[:, t, :], ACT.Relu, bias=shift_s[:, t, :],
                                         scale=rstd_s[:, 0, t, :]).then_inc(rectified, 1)

            def affine(src, signal):
                for d in range(DC):
                    nc.scalar.activation(turned_full[:, d, :], src[:, d, :], ACT.Identity, bias=beta1[:, d:d + 1],
                                         scale=gamma1[:, d:d + 1]).then_inc(signal, 1)

            def source_out(c):
                whole, hi = KBUF[c % 2]
                act.wait_ge(k_projected, c + 1)
                if c >= 2:
                    act.wait_ge(k_stacked, STACKS * (c - 1))
                for g in range(GROUPS):
                    nc.scalar.activation(whole[:, g, :], slot[1][:, g, :], ACT.Identity, bias=kbias[:, g:g + 1]
                                         ).then_inc(k_out, 1)
                act.wait_ge(k_out, GROUPS * (c + 1))
                if c:
                    act.wait_ge(k_norms, c)
                nc.scalar.activation(squares_early, whole[:], ACT.Square).then_inc(k_squared, 1)
                nc.scalar.copy(hi[:].bitcast(F32R), whole[:]).then_inc(k_split_hi, 1)

            for c in range(NCH):
                act.wait_ge(k_turned, c + 1)
                if c:
                    act.wait_ge(k_lo, c)
                affine(slot[0], k_affine)
                if c:
                    source_out(c - 1)
                act.wait_ge(k_masked, c + 1)
                if c:
                    act.wait_ge(v_projected, c)
                nc.scalar.copy(rT_hi[:], turned_full).then_inc(k_hi, 1)
            source_out(NCH - 1)

            def queries_affine(c, hi, first=False):
                act.wait_ge(turned, c + 1)
                if first:
                    act.wait_ge(k_lo, NCH)
                    act.wait_ge(v_projected, NCH)
                else:
                    act.wait_ge(ht_kept, 16 * (c + 1))
                    act.wait_ge(stacked, STACKS * c)
                    act.wait_ge(max_stacked, 16 * 2 * TILES * c)
                affine(side, affine_out)
                act.wait_ge(affine_out, DC * (c + 1))
                nc.scalar.copy(hi, turned_full).then_inc(hi_ready, 1)

            def queries_out(c, first=False):
                act.wait_ge(projected, GROUPS * (c + 1))
                if first:
                    act.wait_ge(k_stacked, STACKS * NCH)
                for g in range(GROUPS):
                    nc.scalar.activation(proj[:, g, :], side[:, g, :], ACT.Identity, bias=qbias[:, g:g + 1],
                                         scale=QSCALE).then_inc(proj_out, 1)

            def queries_split(c):
                act.wait_ge(proj_out, GROUPS * (c + 1))
                act.wait_ge(lo_ready, c + 1)
                nc.scalar.activation(squares_late, proj[:], ACT.Square).then_inc(squared, 1)
                nc.scalar.copy(proj_hi[:].bitcast(F32R), proj[:]).then_inc(split_hi, 1)

            queries_affine(0, rT_hi[:], first=True)
            queries_out(0, first=True)
            queries_split(0)
            act.wait_ge(vmean_done, 1)
            nc.scalar.mul(vmean[:], acc[:, 0, 0:GROUPS], 1.0 / S).then_inc(vmean_ready, 1)
            act.wait_ge(vmean_ready, 1)
            act.sem_inc(evacuated, 2)

            def evacuate(c, g, b):
                G = c * GROUPS + g
                act.wait_ge(closed if b else context_done, G + 2 if b else G + 1)
                act.wait_ge(saved, 16 * (2 * G + b) + 32)
                nc.scalar.copy(evac[:], acc[:, b, :]).then_inc(evacuated, 1)

            START = AHEAD + 2

            def exponentials(c, u):
                act.wait_ge(masked, c * UNITS + u + 1 + SLOTS)
                r = probs[:, u % RING]
                nc.scalar.activation(r, r, ACT.Exp).then_inc(exped, 1)

            def weight_hi(k):
                dst, src = ((wo_hi, wo_raw[:]), (w1_hi, w1_raw[:]), (w2_hi, w2_raw))[k]
                act.wait_ge(w3_in, 32 if k < 2 else 48)
                nc.scalar.copy(dst[:], src).then_inc(w3_hi, 1)

            def chunk(c, last):
                n = c + 1
                todo = {
                    17: lambda: queries_affine(n, late_hi[:]), 33: lambda: queries_out(n), 34: lambda: queries_split(n)}
                if last:
                    todo = {10: lambda: weight_hi(0), 16: lambda: weight_hi(1), 50: lambda: weight_hi(2)}
                for g in range(GROUPS):
                    todo[(g + 1) * UG + AHEAD - 2] = lambda g=g: evacuate(c, g, 0)
                    todo[(g + 1) * UG + AHEAD + 1] = lambda g=g: evacuate(c, g, 1)
                for u in range(START, UNITS + START):
                    if u in todo:
                        todo[u]()
                    if u < UNITS:
                        exponentials(c, u)
                    elif not last:
                        exponentials(n, u - UNITS)

            for u in range(START):
                exponentials(0, u)
            with act.Fori(0, NCH - 1) as c:
                chunk(c, False)
            chunk(NCH - 1, True)

            def context_hi(c):
                act.wait_ge(divided, 4 * (c + 1))
                nc.scalar.copy(cT_hi[:], cT[:]).then_inc(c_hi, 1)

            def turned_y(c):
                act.wait_ge(y_turned, c + 1)
                nc.scalar.copy(yT_hi[:], side[:]).then_inc(y_hi, 1)

            def gelu(c, first=False):
                for f in range(FC):
                    act.wait_ge(ff1, c * FC + f + 1)
                    if not (first and f < 2):
                        act.wait_ge(g_split, c * FC + f - 1)
                    h = slot[f % 2][:, f // 2 % 2, :]
                    nc.scalar.activation(g_full[:, f % 2, :], h, ACT.Gelu_apprx_tanh).then_inc(gelu_out, 1)
                    nc.scalar.activation(g_hi[:, f, :], h, ACT.Gelu_apprx_tanh).then_inc(gelu_out, 1)

            context_hi(0)
            turned_y(0)
            context_hi(1)
            gelu(0, first=True)
            turned_y(1)
            with act.Fori(1, NCH - 1) as c:
                context_hi(c + 1)
                gelu(c)
                turned_y(c + 1)
            gelu(NCH - 1)

        @block.vector
        def _(dve):
            nc.vector.memset(kmax[:], 0.0).then_inc(k_norm_max, 1)
            MADE = 1

            def first_norm(half):
                ts = slice(half * HALF, (half + 1) * HALF)
                per = stat_steps(HALF) + 1
                layer_stats(dve, xs[:, ts], stats_s[:, ts], moments_s[:, 0, ts], rstd_s[:, 0, ts], HALF, norm_a,
                            half * per)
                nc.vector.scalar_tensor_tensor(out=shift_s[:, ts], in0=moments_s[:, 0, ts, 0:1], scalar=-1.0,
                                               in1=rstd_s[:, 0, ts], op0=ALU.mult, op1=ALU.mult).then_inc(norm_a, 1)

            def second_norm(half):
                ts = slice(half * HALF, (half + 1) * HALF)
                per = stat_steps(HALF) + HALF
                dve.wait_ge(rectified, HALF * (half + 1))
                layer_stats(dve, xs[:, ts], stats_s[:, ts], moments_s[:, 1, ts], rstd_s[:, 1, ts], HALF, norm_b,
                            half * per)
                layer_apply(xs[:, ts], moments_s[:, 1, ts], rstd_s[:, 1, ts], HALF, norm_b)

            def target_norm(src, c):
                dve.wait_ge(rows_in, 16 * (c + 1))
                layer_stats(dve, src, stats, moments, rstd[:], TILES, norm_t, c * LN_STEPS)

            dve.wait_ge(x_rows_in, 32)
            first_norm(0)
            dve.wait_ge(x_rest_in, 16)
            first_norm(1)
            dve.wait_ge(params_in, 16 * 9)
            dve.wait_ge(nodes_in, 16)
            nc.vector.tensor_scalar(nodes[:], nm_int[:], 1, None, ALU.is_equal).then_inc(k_norm_max, 1)
            nc.vector.tensor_scalar(node_row[:], node_row[:], 1.0, None, ALU.is_equal).then_inc(k_norm_max, 1)
            MADE += 2
            second_norm(0)
            dve.wait_ge(k_norm_max, MADE)
            dve.sem_inc(consts, 1)
            dve.wait_ge(w_hi_ready, 4)
            for i, (dst, hi) in enumerate(((wk_lo, wk_hi), (wv_lo, wv_hi), (wq_lo, wq_hi))):
                nc.vector.tensor_tensor(dst[:], w_raw[:, i], hi[:].bitcast(F32), ALU.subtract).then_inc(w_lo_ready, 1)
            second_norm(1)
            target_norm(rows_first, 0)
            layer_apply(rows_first, moments, rstd, TILES, norm_t)

            def test_mask(c, t):
                dve.wait_ge(mask_turned, 16 * (c * TILES + t + 1))
                if isinstance(c, int) and c == 0:
                    m = mask_flat[:, 0:ST, t * P:(t + 1) * P]
                else:
                    m = mask_flat[:, bass.ds((c % 2) * ST, ST), t * P:(t + 1) * P]
                nc.vector.tensor_scalar(m, m, 0.0, None, ALU.is_equal).then_inc(mask_tested, 1)

            for c in range(NCH):
                dve.wait_ge(v_projected, c + 1)
                nc.vector.tensor_tensor(V[:, c * TILES:(c + 1) * TILES, :], acc4,
                                        vbias[:, None, :].to_broadcast([P, TILES, D]), ALU.add).then_inc(v_ready, 1)
                dve.wait_ge(k_norms, c + 1)
                dve.wait_ge(k_norm_max, MADE + 2 * c)
                nc.vector.tensor_reduce(nmax[:], side[:], AX_X, ALU.max).then_inc(k_norm_max, 1)
                dve.wait_ge(k_norm_max, MADE + 2 * c + 1)
                nc.vector.tensor_tensor(kmax[:], kmax[:], nmax[:], ALU.max).then_inc(k_norm_max, 1)
                test_mask(0, c)
            dve.wait_ge(k_norm_max, MADE + 2 * NCH)

            def target_bound(c):
                dve.wait_ge(norms, c + 1)
                nc.vector.tensor_reduce(nmax[:], side[:], AX_X, ALU.max).then_inc(norm_max, 1)
                dve.wait_ge(norm_max, 2 * c + 1)
                nc.vector.tensor_tensor(nmax[:], nmax[:], kmax[:], ALU.mult).then_inc(norm_max, 1)
                dve.wait_ge(norm_max, 2 * c + 2)
                nc.vector.tensor_reduce(bound[:], nmax[:], AX_X, ALU.max).then_inc(bound_col, 1)

            def decide(c, first=False):
                dve.wait_ge(bound_row, c + 1)
                nc.vector.tensor_reduce(bound1[:], side[0:1, 0, 0:P], AX_X, ALU.max).then_inc(flag_ready, 1)
                dve.wait_ge(flag_ready, 2 * c + 1)
                if not first:
                    dve.wait_ge(flag_read, 4 * c)
                nc.vector.tensor_scalar(flag[:], bound1[:], SAFE * SAFE, None, ALU.is_gt).then_inc(flag_ready, 1)

            def load_flag(c):
                dve.wait_ge(flag_ready, 2 * c + 2)
                dve.sem_inc(gate["dve"], 1)
                general = dve.value_load(flag[0:1, 0:1], min_val=0, max_val=1)
                dve.sem_inc(flag_read, 1)
                return general

            def find_maximum(c, general):
                with dve.If(general):
                    dve.wait_ge(stacked, STACKS * (c + 1))
                    n = 0
                    for k in range(HEADS // 2):
                        for t in range(TILES):
                            dve.wait_ge(max_adj_in, 16 * ((c * HEADS // 2 + k) * TILES + t + 1))
                            nc.vector.tensor_scalar(adj_raw[:], adj_raw[:], 0.0, None, ALU.is_equal
                                                    ).then_inc(max_tested, 1)
                            dve.wait_ge(max_tested, (c * HEADS // 2 + k) * TILES + t + 1)
                            for h in (2 * k, 2 * k + 1):
                                for half in range(2):
                                    step = c * TILES * HEADS * 2 + n
                                    dve.wait_ge(max_scored, step + 1)
                                    if n:
                                        dve.wait_ge(max_taken, step)
                                    nc.vector.scalar_tensor_tensor(
                                        out=proj[:].rearrange("p a t -> p (a t)"),
                                        in0=adj_raw[:, half * 2 * CHUNK:(half + 1) * 2 * CHUNK], scalar=MASKED,
                                        in1=side[:].rearrange("p a t -> p (a t)"), op0=ALU.mult,
                                        op1=ALU.add).then_inc(max_masked, 1)
                                    dve.wait_ge(max_masked, step + 1)
                                    nc.vector.tensor_reduce(mpart[:, t * HEADS + h, half:half + 1],
                                                            proj[:].rearrange("p a t -> p (a t)"), AX_X, ALU.max
                                                            ).then_inc(max_taken, 1)
                                    n += 1
                    dve.wait_ge(max_taken, (c + 1) * TILES * HEADS * 2)
                    nc.vector.tensor_reduce(mcol[:], mpart[:], AX_X, ALU.max).then_inc(max_col, 1)
                    dve.wait_ge(max_turned, c + 1)
                    nc.vector.tensor_scalar(mneg, side[0:TILES * HEADS, 0, 0:P], -1.0, None, ALU.mult
                                            ).then_inc(max_col, 1)
                    dve.wait_ge(max_col, 2 * c + 2)
                    nc.vector.tensor_copy(mrow[:, 0, :], mneg).then_inc(max_split, 1)
                    dve.wait_ge(max_split, 2 * c + 1)
                    nc.vector.tensor_tensor(mrow[:, 1, :], mneg, mrow[:, 0, :].bitcast(F32), ALU.subtract
                                            ).then_inc(max_split, 1)
                with dve.Else():
                    dve.sem_inc(max_tested, TILES * HEADS // 2)
                    dve.sem_inc(max_masked, TILES * HEADS * 2)
                    dve.sem_inc(max_taken, TILES * HEADS * 2)
                    dve.sem_inc(max_col, 2)
                    dve.sem_inc(max_split, 2)

            target_bound(0)
            decide(0, first=True)
            dve.sem_inc(masked, SLOTS)
            general = load_flag(0)
            find_maximum(0, general)

            def invert(part):
                at = places(part)
                base = INV * part
                dve.wait_ge(sums_in, 16 * (part + 1))
                nc.vector.tensor_scalar(no_edge[:, at], sums[:, at], 0.0, None, ALU.is_equal).then_inc(inverted, 1)
                dve.wait_ge(inverted, base + 1)
                nc.vector.tensor_tensor(sums[:, at], sums[:, at], no_edge[:, at], ALU.add).then_inc(inverted, 1)
                dve.wait_ge(inverted, base + 2)
                nc.vector.reciprocal(sums[:, at], sums[:, at]).then_inc(inverted, 1)
                dve.wait_ge(inverted, base + 3)
                nc.vector.scalar_tensor_tensor(out=sums[:, at], in0=no_edge[:, at], scalar=1.0, in1=sums[:, at],
                                               op0=ALU.is_lt, op1=ALU.mult).then_inc(inverted, 1)

            def ring_free(c, u):
                if u >= RING:
                    return c * UNITS + u - RING + 1
                before = u + (UNITS - 1 - u) // RING * RING
                return c * UNITS + before + 1 - UNITS

            def chunk(c, last):
                n = c + 1
                flagged = []
                todo = {20: lambda: invert(0)} if last else {
                    10: lambda: target_norm(rows, n),
                    12: lambda: layer_apply(rows, moments, rstd, TILES, norm_t),
                    16: lambda: test_mask(n, 0), 24: lambda: test_mask(n, 1), 47: lambda: target_bound(n),
                    40: lambda: test_mask(n, 2), 51: lambda: decide(n), 57: lambda: test_mask(n, 3),
                    60: lambda: flagged.append(load_flag(n))}
                for u in range(UNITS):
                    if u in todo:
                        todo[u]()
                    i = u % UG // PAIRS
                    if u == 0:
                        dve.wait_ge(mask_tested, TILES * (c + 1))
                    dve.wait_ge(scored, c * UNITS + u + 1)
                    dve.wait_ge(used, ring_free(c, u) + RING)
                    k = [add_index(g, j, pr) + 1 for g in range(GROUPS) for j in ADDED for pr in range(PAIRS)
                         if (g * ST + j) * PAIRS + pr <= u - RING]
                    dve.wait_ge(added, c * ADDS + (k[-1] if k else 0) + 1)
                    m = mask_flat[:, bass.ds((c % 2) * ST + i, 1), :].to_broadcast([P, 2, CHUNK])
                    nc.vector.scalar_tensor_tensor(out=probs[:, u % RING], in0=m, scalar=MASKED,
                                                   in1=slot[u % SLOTS][:], op0=ALU.mult, op1=ALU.add
                                                   ).then_inc(masked, 1)
                if not last:
                    find_maximum(n, flagged[0])

            with dve.Fori(0, NCH - 1) as c:
                chunk(c, False)
            chunk(NCH - 1, True)

            dve.wait_ge(stage3, 1)
            invert(1)

            def divide(c):
                dve.wait_ge(mix_in, 48 * (c + 1))
                for g in range(GROUPS):
                    nc.vector.tensor_scalar(mean_part[:, g, :], dT[:, g, :], 0.0, vmean[:, g:g + 1],
                                            ALU.is_equal, ALU.mult).then_inc(divided, 1)
                nc.vector.tensor_tensor(cT[:], cT[:], dT[:], ALU.mult).then_inc(divided, 1)
                dve.wait_ge(divided, 4 * c + 3)
                nc.vector.tensor_tensor(cT[:], cT[:], mean_part[:], ALU.add).then_inc(divided, 1)
                dve.wait_ge(c_hi, c + 1)
                nc.vector.tensor_tensor(cT_lo[:], cT[:], cT_hi[:].bitcast(F32), ALU.subtract).then_inc(c_lo, 1)

            def mix(c, first=False):
                dve.wait_ge(attended, c + 1)
                dve.wait_ge(residual, 2 * c + 3)
                if not first:
                    dve.wait_ge(xy_ready, c)
                    dve.wait_ge(y_turned, c)
                nc.vector.tensor_tensor(y[:], side4, ht[:], ALU.add).then_inc(mixed, 1)
                dve.wait_ge(mixed, c + 1)
                layer_stats(dve, y, stats, moments, rstd[:], TILES, norm_y, c * LN_STEPS)
                layer_apply(y, moments, rstd, TILES, norm_y)

            def turned_y(c):
                dve.wait_ge(y_hi, c + 1)
                nc.vector.tensor_tensor(yT_lo[:], side[:], yT_hi[:].bitcast(F32), ALU.subtract).then_inc(y_lo, 1)

            def gelu_lo(c):
                for f in range(FC):
                    dve.wait_ge(gelu_out, 2 * (c * FC + f + 1))
                    nc.vector.tensor_tensor(g_lo[:, f, :], g_full[:, f % 2, :], g_hi[:, f, :].bitcast(F32),
                                            ALU.subtract).then_inc(g_split, 1)

            def finish(c, first=False):
                dve.wait_ge(ff2, c + 1)
                dve.wait_ge(xy_ready, c + 1)
                if not first:
                    dve.wait_ge(stored, 16 * c)
                nc.vector.tensor_tensor(result[:], acc4, xy[:], ALU.add).then_inc(summed, 1)

            divide(0)
            mix(0, first=True)
            turned_y(0)
            divide(1)
            gelu_lo(0)
            mix(1)
            finish(0, first=True)
            turned_y(1)
            with dve.Fori(1, NCH - 1) as c:
                divide(c + 1)
                gelu_lo(c)
                mix(c + 1)
                finish(c)
                turned_y(c + 1)
            gelu_lo(NCH - 1)
            finish(NCH - 1)

        @block.tensor
        def _(pe):
            def turn(dst, src, t0, signal):
                for t in range(TILES):
                    for d in range(DC):
                        mm = pe.transpose(dst[:, d, t * P:(t + 1) * P], src[:, t0 + t, d * P:(d + 1) * P], ident[:])
                mm.then_inc(signal, 1)

            def project(dst, w_hi, w_lo, hi, lo, signal, groups):
                for g in groups:
                    for d in range(DC):
                        out_cols = slice(g * P, (g + 1) * P)
                        mm = three(pe.matmul, dst[:, g, :], w_hi[:, d, out_cols], w_lo[:, d, out_cols],
                                   hi[:, d, :], lo[:, d, :], d == 0, d == DC - 1)
                mm.then_inc(signal, 1)

            def take_norms(squares, signal):
                for g in range(GROUPS):
                    mm = pe.matmul(side[:, g, :], headsum[:], squares[:, g, :], start=True, stop=True)
                mm.then_inc(signal, 1)

            def turn_source(c):
                half = c * TILES // HALF
                pe.wait_ge(norm_b, half * (stat_steps(HALF) + HALF) + stat_steps(HALF)
                           + (c + 1) * TILES - half * HALF)
                if c:
                    pe.wait_ge(k_affine, DC * c)
                turn(slot[0], xs, c * TILES, k_turned)

            pe.wait_ge(pool_made, 4 + PER)
            turn_source(0)
            pe.wait_ge(w_lo_ready, 3)
            for c in range(NCH):
                if c + 1 < NCH:
                    turn_source(c + 1)
                pe.wait_ge(k_lo, c + 1)
                if c:
                    pe.wait_ge(k_out, GROUPS * c)
                project(slot[1], wk_hi, wk_lo, rT_hi, rT_lo, k_projected, range(GROUPS))
                if c:
                    pe.wait_ge(v_ready, c)
                for t in range(TILES):
                    for d in range(DC):
                        ts = slice(t * P, (t + 1) * P)
                        mm = three(pe.matmul, acc4[:, t, :], rT_hi[:, d, ts], rT_lo[:, d, ts],
                                   wv_hi[:, d, :], wv_lo[:, d, :], d == 0, d == DC - 1)
                mm.then_inc(v_projected, 1)
                pe.wait_ge(k_squared, c + 1)
                if c:
                    pe.wait_ge(k_norm_max, 3 + 2 * c - 1)
                take_norms(squares_early, k_norms)

            def turn_target(c, src):
                pe.wait_ge(norm_t, (c + 1) * LN_STEPS)
                turn(side, src, 0, turned)

            def project_target(c, hi, lo, g):
                pe.wait_ge(lo_ready, c + 1)
                project(side, wq_hi, wq_lo, hi, lo, projected, [g])

            def target_norms(c):
                pe.wait_ge(squared, c + 1)
                take_norms(squares_late, norms)

            def bound_to_row(c):
                pe.wait_ge(bound_col, c + 1)
                pe.transpose(side[0:1, 0, 0:P], bound[:], ident[:]).then_inc(bound_row, 1)

            pe.wait_ge(k_norm_max, 3 + 2 * NCH - 1)
            turn_target(0, rows_first)
            for g in range(GROUPS):
                project_target(0, rT_hi, rT_lo, g)
            target_norms(0)
            pe.wait_ge(v_ready, NCH)
            for g in range(GROUPS):
                for i in range(ST):
                    mm = pe.matmul(acc[:, 0, g:g + 1], V[:, i, g * P:(g + 1) * P], ones[:, 0:1],
                                   start=(i == 0), stop=(i == ST - 1))
            mm.then_inc(vmean_done, 1)
            bound_to_row(0)
            pe.sem_inc(used, RING)
            pe.sem_inc(closed, 1)

            def load_flag(c):
                pe.wait_ge(flag_ready, 2 * c + 2)
                pe.sem_inc(gate["pe"], 1)
                general = pe.value_load(flag[0:1, 0:1], min_val=0, max_val=1)
                pe.sem_inc(flag_read, 1)
                return general

            def find_maximum(c, general):
                with pe.If(general):
                    n = 0
                    for k in range(HEADS // 2):
                        pe.wait_ge(q_copied[k % 2], 16 * (HEADS // 4 * c + k // 2 + 1))
                        for t in range(TILES):
                            for h in range(2):
                                for half in range(2):
                                    if n:
                                        pe.wait_ge(max_masked, c * TILES * HEADS * 2 + n)
                                    for b in range(2):
                                        s0 = (2 * half + b) * CHUNK
                                        mm = pe.matmul(side[:, b, :], qcopy[k % 2][0:AUX, h, t * P:(t + 1) * P],
                                                       kst[0:AUX, 2 * k + h, s0:s0 + CHUNK].bitcast(F32),
                                                       start=True, stop=True)
                                    mm.then_inc(max_scored, 1)
                                    n += 1
                    pe.wait_ge(max_col, 2 * c + 1)
                    pe.transpose(side[0:TILES * HEADS, 0, 0:P], mcol[:], ident[:]).then_inc(max_turned, 1)
                with pe.Else():
                    pe.sem_inc(max_scored, TILES * HEADS * 2)
                    pe.sem_inc(max_turned, 1)

            general = load_flag(0)
            find_maximum(0, general)

            def scores(c, u):
                g, i, pair = u // UG, u % UG // PAIRS, u % PAIRS
                pe.wait_ge(masked, c * UNITS + u + 1)
                for k in range(2):
                    h = g * PER + 2 * pair + k
                    mm = pe.matmul(slot[u % SLOTS][:, k, :], kst[0:KROWS, h, i * P:(i + 1) * P],
                                   qst_flat[0:KROWS, bass.ds(qpart(c) + h, 1), :].rearrange("p o t -> p (o t)"),
                                   start=True, stop=True)
                mm.then_inc(scored, 1)

            def context(c, g, i):
                u = (g * ST + i) * PAIRS
                pe.wait_ge(exped, c * UNITS + u + PAIRS)
                if i == 0:
                    pe.wait_ge(evacuated, 2 * (c * GROUPS + g) + 1)
                for j in range(PER):
                    h = g * PER + j
                    mm = pe.matmul(acc[HD * j:HD * j + HD, 0, :], V[:, i, h * HD:(h + 1) * HD],
                                   probs[:, (u + j // 2) % RING, j % 2, :], start=(i == 0), stop=(i == ST - 1))
                if i == ST - 1:
                    mm.then_inc(context_done, 1)
                elif i in ADDED:
                    mm.then_inc(used, PAIRS)

            def add_sums(c, g, i):
                u = (g * ST + i) * PAIRS
                first = i == TAKEN[0]
                if first:
                    pe.wait_ge(evacuated, 2 * (c * GROUPS + g) + 2)
                for j in range(PER):
                    mm = pe.matmul(acc[HD * j:HD * j + HD, 1, :], ones[:], probs[:, (u + j // 2) % RING, j % 2, :],
                                   start=first, stop=False)
                mm.then_inc(used, PAIRS)

            def close(c, g):
                pe.wait_ge(added, c * ADDS + (g + 1) * OPS + 1)
                for j in range(PER):
                    mm = pe.matmul(acc[HD * j:HD * j + HD, 1, :], ones[:], psum2[:, j // 2, j % 2, :],
                                   start=False, stop=True)
                mm.then_inc(closed, 1)

            def queries_ready(c):
                pe.wait_ge(stacked, STACKS * (c + 1))
                pe.wait_ge(q_zeroed, 16 * (c + 1))
                pe.wait_ge(max_stacked, 16 * 2 * TILES * (c + 1))

            def chunk(c, last):
                n = c + 1
                todo = {} if last else {
                    14: lambda: turn_target(n, rows), 25: lambda: project_target(n, late_hi, late_lo, 0),
                    27: lambda: project_target(n, late_hi, late_lo, 1), 37: lambda: target_norms(n),
                    41: lambda: bound_to_row(n), UNITS - AHEAD: lambda: find_maximum(n, load_flag(n))}
                for u in range(UNITS):
                    if u in todo:
                        todo[u]()
                    if u + AHEAD < UNITS:
                        scores(c, u + AHEAD)
                    elif not last:
                        if u == UNITS - AHEAD:
                            queries_ready(n)
                        scores(n, u + AHEAD - UNITS)
                    k = u // PAIRS
                    if u % PAIRS == 0:
                        context(c, k // ST, k % ST)
                    elif k % ST not in ADDED:
                        add_sums(c, k // ST, k % ST)
                    if u == UG:
                        close(c, 0)
                close(c, GROUPS - 1)

            pe.wait_ge(keys_oned, 1)
            pe.wait_ge(k_stacked, STACKS * NCH)
            queries_ready(0)
            for u in range(AHEAD):
                scores(0, u)
            with pe.Fori(0, NCH - 1) as c:
                chunk(c, False)
            chunk(NCH - 1, True)

            pe.wait_ge(w3_lo, 3)

            def attend(c):
                pe.wait_ge(c_lo, c + 1)
                for t in range(TILES):
                    ts = slice(t * P, (t + 1) * P)
                    for d in range(DC):
                        mm = three(pe.matmul, side4[:, t, :], cT_hi[:, d, ts], cT_lo[:, d, ts],
                                   wo_hi[:, d, :], wo_lo[:, d, :], d == 0, d == DC - 1)
                mm.then_inc(attended, 1)

            def turn_y(c):
                pe.wait_ge(y_ready, 3 * c + 3)
                turn(side, y, 0, y_turned)

            def widen(c, first=False):
                pe.wait_ge(y_lo, c + 1)
                for f in range(FC):
                    if not (first and f < 4):
                        pe.wait_ge(gelu_out, 2 * (c * FC + f - 3))
                    fs = slice(f * P, (f + 1) * P)
                    for d in range(DC):
                        mm = three(pe.matmul, slot[f % 2][:, f // 2 % 2, :], w1_hi[:, d, fs], w1_lo[:, d, fs],
                                   yT_hi[:, d, :], yT_lo[:, d, :], d == 0, d == DC - 1)
                    mm.then_inc(ff1, 1)

            def narrow(c, first=False):
                pe.wait_ge(g_split, FC * (c + 1))
                if not first:
                    pe.wait_ge(summed, c)
                for t in range(TILES):
                    ts = slice(t * P, (t + 1) * P)
                    for f in range(FC):
                        mm = three(pe.matmul, acc4[:, t, :], g_hi[:, f, ts], g_lo[:, f, ts],
                                   w2_hi[:, f, :], w2_lo[:, f, :], f == 0, f == FC - 1)
                mm.then_inc(ff2, 1)

            attend(0)
            turn_y(0)
            widen(0, first=True)
            attend(1)
            narrow(0, first=True)
            turn_y(1)
            with pe.Fori(1, NCH - 1) as c:
                widen(c)
                attend(c + 1)
                narrow(c)
                turn_y(c + 1)
            widen(NCH - 1)
            narrow(NCH - 1)


_INS = ['x', 'adj', 'nodemask', 'L0_gnn_h_target', 'L0_gnn_ln1_scale', 'L0_gnn_ln1_bias', 'L0_gnn_Wq', 'L0_gnn_bq',
        'L0_gnn_Wk', 'L0_gnn_bk', 'L0_gnn_Wv', 'L0_gnn_bv', 'L0_gnn_Wo', 'L0_gnn_bo', 'L0_gnn_ln2_scale',
        'L0_gnn_ln2_bias', 'L0_gnn_W1', 'L0_gnn_W2']


def kernel(**inputs):
    import numpy as _np
    import concourse.bacc as _bacc
    from concourse import mybir as _mybir
    from concourse.bass_utils import run_bass_kernel_spmd as _run

    nc = _bacc.Bacc("TRN2", target_bir_lowering=False, num_devices=1)
    arrays, args = {}, []
    for name in _INS:
        a = _np.ascontiguousarray(inputs[name])
        arrays[f"in_{name}"] = a
        args.append(nc.dram_tensor(f"in_{name}", a.shape, _mybir.dt.from_np(a.dtype), kind="ExternalInput").ap())
    shape = inputs['x'].shape
    args.append(nc.dram_tensor("out_0", shape, _mybir.dt.float32, kind="ExternalOutput").ap())
    graph_attention(nc, *args)
    r = _run(nc, [arrays], core_ids=[0])
    return r.results[0]["out_0"]
```

```python
from contextlib import ExitStack

import concourse.bass as bass
from concourse import mybir

F32 = mybir.dt.float32
F32R = mybir.dt.float32r
BF16 = mybir.dt.bfloat16
I32 = mybir.dt.int32
ACT = mybir.ActivationFunctionType
ALU = mybir.AluOpType
AX_X = mybir.AxisListType.X

P = 128
HEADS = 8
HD = 32
EPS = 1e-5
SAFE = 60.0
MASKED = -(2.0 ** 100)
CHUNK = 512
TILES = CHUNK // P
RING = 8
SLOTS = 3
RSQRT_GUESS = 0x5F3759DF
NEWTON = 3


def graph_attention(nc, x, adj, nodemask, h_target, ln1_scale, ln1_bias, Wq, bq, Wk, bk, Wv, bv, Wo, bo,
                    ln2_scale, ln2_bias, W1, W2, out):
    S, D = x.shape
    FF = W1.shape[1]
    NCH = S // CHUNK
    ST = S // P
    DC = D // P
    FC = FF // P
    GROUPS = D // P
    PER = P // HD
    PAIRS = PER // 2
    UG = ST * PAIRS
    UNITS = GROUPS * UG
    AUX = 3 * HD
    KROWS = AUX + 2
    QSCALE = float(HD) ** -0.5
    STACKS = 16 * 3 * PER
    HALF = ST // 2
    ZROW = 64

    ADDED = [0, 1, 3, 6, 8, 11, 13]
    AHEAD = 6
    BORROWED = {20: "turned", 31: "projected 0", 32: "projected 1", 43: "norms", 49: "bound"}
    assert (UNITS + len(BORROWED)) % SLOTS == 0

    def slot_order(last):
        order = []
        for u in range(UNITS):
            if u in BORROWED and not last:
                order.append(BORROWED[u])
            order.append(u)
        return order

    def place(what, last=False):
        return slot_order(last).index(what) % SLOTS

    def place_before(what, last=False):
        at = slot_order(last).index(what) - SLOTS
        return at if at < 0 else slot_order(last)[at]

    TAKEN = [i for i in range(ST) if i not in ADDED]
    OPS = (len(ADDED) - 1) * PAIRS
    ADDS = GROUPS * OPS

    def add_index(g, i, pair):
        return g * OPS + max(ADDED.index(i) - 1, 0) * PAIRS + pair

    x_rows = x.rearrange("(n p) d -> p n d", p=P)
    ht_rows = h_target.rearrange("(n p) d -> p n d", p=P)
    out_rows = out.rearrange("(n p) d -> p n d", p=P)
    adj_rows = adj.rearrange("(n p) s -> n p s", p=P)
    ht_saved = nc.dram_tensor("ht_saved", [S, D], F32).ap()
    hts_rows = ht_saved.rearrange("(n p) d -> p n d", p=P)
    ctx_saved = nc.dram_tensor("ctx_saved", [D, S], F32).ap()
    sums_saved = nc.dram_tensor("sums_saved", [HEADS, S], F32).ap()
    inverse_saved = nc.dram_tensor("inverse_saved", [HEADS, S], F32).ap()

    with ExitStack() as ctx:
        def sb(name, shape, dt, scope=ctx):
            return scope.enter_context(nc.sbuf_tensor(name, shape, dt))

        def sem(name):
            return ctx.enter_context(nc.semaphore(name))

        slot = [ctx.enter_context(nc.psum_tensor(f"slot{i}", [P, 2, CHUNK], F32)) for i in range(SLOTS)]
        acc = ctx.enter_context(nc.psum_tensor("acc", [P, 2, CHUNK], F32))
        side = slot[SLOTS - 1]
        side4 = side[:].rearrange("p a (b c) -> p (a b) c", c=D)
        acc4 = acc[:].rearrange("p a (b c) -> p (a b) c", c=D)

        ident = sb("ident", [P, P], F32)
        zeros = ident[0:2, P - ZROW:P]
        ones = sb("ones", [P, HD], F32)
        headsum = sb("headsum", [P, P], BF16)
        gamma1 = sb("gamma1", [P, DC], F32)
        beta1 = sb("beta1", [P, DC], F32)
        nodes = sb("nodes", [P, ST], F32)
        kbias = sb("kbias", [P, GROUPS], F32)
        qbias = sb("qbias", [P, GROUPS], F32)
        vmean = sb("vmean", [P, GROUPS], F32)
        stats = sb("stats", [P, TILES, 6], F32)
        moments = sb("moments", [P, TILES, 2], F32)
        rstd = sb("rstd", [P, TILES, 1], F32)
        variance = sb("variance", [P, HALF, 1], F32)
        newton = sb("newton", [P, HALF, 1], F32)
        kmax = sb("kmax", [P, GROUPS], F32)
        nmax = sb("nmax", [P, GROUPS], F32)
        bound = sb("bound", [P, 1], F32)
        bound1 = sb("bound1", [1, 1], F32)
        flag = sb("flag", [1, 1], I32)
        mcol = sb("mcol", [P, TILES * HEADS], F32)
        mpart = sb("mpart", [P, TILES * HEADS, 2], F32)

        att = ctx.enter_context(ExitStack())
        kst = sb("kst", [P, HEADS, S], F32R, att)
        V = sb("V", [P, ST, D], F32, att)
        early = att.enter_context(ExitStack())
        xs = sb("xs", [P, ST, D], F32, early)
        sb("even_halves", [P, 2, ST, CHUNK], BF16, early)
        w_raw = sb("w_raw", [P, 3, DC, D], F32, early)
        wk_hi = sb("wk_hi", [P, DC, D], F32R, early)
        wk_lo = sb("wk_lo", [P, DC, D], F32R, early)
        wv_hi = sb("wv_hi", [P, DC, D], F32R, early)
        wv_lo = sb("wv_lo", [P, DC, D], F32R, early)
        vbias = sb("vbias", [P, D], F32, early)
        qbias_in = sb("qbias_in", [P, GROUPS], F32, early)
        nm_int = sb("nm_int", [P, ST], I32, early)
        early.close()
        qst = sb("qst", [P, 2, HEADS, CHUNK], F32R, att)
        maskT = sb("maskT", [P, 2, ST, CHUNK], BF16, att)
        rows = sb("rows", [P, TILES, D], F32, att)
        with ExitStack() as parts:
            late_hi = sb("late_hi", [P, DC, CHUNK], F32R, parts)
            late_lo = sb("late_lo", [P, DC, CHUNK], F32R, parts)
        proj = sb("proj", [P, GROUPS, CHUNK], F32, att)
        proj_hi = sb("proj_hi", [P, GROUPS, CHUNK], F32, att)
        adj_raw = sb("adj_raw", [P, S], BF16, att)
        evac = sb("evac", [P, CHUNK], F32, att)
        wq_hi = sb("wq_hi", [P, DC, D], F32R, att)
        wq_lo = sb("wq_lo", [P, DC, D], F32R, att)
        with ExitStack() as early2:
            proj_odd = sb("proj_odd", [P, GROUPS, CHUNK], F32, early2)
            proj_hi_odd = sb("proj_hi_odd", [P, GROUPS, CHUNK], F32, early2)
            RT = [(sb(f"rT_hi{i}", [P, DC, CHUNK], F32R, early2), sb(f"rT_lo{i}", [P, DC, CHUNK], F32R, early2))
                  for i in range(2)]
            wide_odd = sb("wide_odd", [P, DC, CHUNK], F32, early2)
            vsum = sb("vsum", [P, D], F32, early2)
            rows_first = sb("rows_first", [P, TILES, D], F32, early2)
            node_row = sb("node_row", [P, S], BF16, early2)
            stats_s = sb("stats_s", [P, ST, 6], F32, early2)
            moments_s = sb("moments_s", [P, 2, ST, 2], F32, early2)
            rstd_s = sb("rstd_s", [P, 2, ST, 1], F32, early2)
            shift_s = sb("shift_s", [P, ST, 1], F32, early2)
        probs = sb("probs", [P, RING, 2, CHUNK], F32, att)
        psum2 = sb("added", [P, PAIRS, 2, CHUNK], F32, att)
        turned_full = rows[:].rearrange("p t d -> p (t d)").rearrange("p (d t) -> p d t", d=DC)
        WIDE = [turned_full, wide_odd[:]]
        squares_late = turned_full.bitcast(BF16).rearrange("p d t -> p (d t)")[:, 0:GROUPS * CHUNK].rearrange(
            "p (g t) -> p g t", g=GROUPS)
        squares_early = evac[:].bitcast(BF16).rearrange("p (g t) -> p g t", g=GROUPS)
        mneg = proj[0:TILES * HEADS, 0, 0:P]
        mrow = proj[0:TILES * HEADS, 1, 0:2 * P].bitcast(F32R).rearrange("p (a t) -> p a t", a=2)
        qcopy = [turned_full, proj_hi[:]]
        att.close()

        ffn = ctx.enter_context(ExitStack())
        g_hi = sb("g_hi", [P, FC, CHUNK], F32R, ffn)
        g_lo = sb("g_lo", [P, FC, CHUNK], F32R, ffn)
        dT = sb("dT", [P, DC, CHUNK], F32, ffn)
        cT = sb("cT", [P, DC, CHUNK], F32, ffn)
        cT_hi = sb("cT_hi", [P, DC, CHUNK], F32R, ffn)
        cT_lo = sb("cT_lo", [P, DC, CHUNK], F32R, ffn)
        mean_part = sb("mean_part", [P, DC, CHUNK], F32, ffn)
        ht = sb("ht", [P, TILES, D], F32, ffn)
        gamma1_row = sb("gamma1_row", [P, D], F32, ffn)
        beta1_row = sb("beta1_row", [P, D], F32, ffn)
        obias = sb("obias", [P, D], F32, ffn)
        gamma2 = sb("gamma2", [P, D], F32, ffn)
        beta2 = sb("beta2", [P, D], F32, ffn)
        gamma2_col = sb("gamma2_col", [P, DC], F32, ffn)
        beta2_col = sb("beta2_col", [P, DC], F32, ffn)
        over_keys = (2 * FC * CHUNK + 6 * TILES * D + 5 * D + 2 * DC) * 4
        assert over_keys <= HEADS * S * 4
        xr = sb("xr", [P, TILES, D], F32, ffn)
        y = sb("y", [P, TILES, D], F32, ffn)
        xy = sb("xy", [P, TILES, D], F32, ffn)
        yT = sb("yT", [P, DC, CHUNK], F32, ffn)
        yT_hi = sb("yT_hi", [P, DC, CHUNK], F32R, ffn)
        yT_lo = sb("yT_lo", [P, DC, CHUNK], F32R, ffn)
        g_full = sb("g_full", [P, 2, CHUNK], F32, ffn)
        result = sb("result", [P, TILES, D], F32, ffn)
        used_by_3 = over_keys + 8 * TILES * D * 4
        odd_end = HEADS * S * 4 + ST * D * 4 + HEADS * CHUNK * 4
        assert used_by_3 <= odd_end
        if used_by_3 < odd_end:
            sb("gap3", [P, (odd_end - used_by_3) // 4], F32, ffn)
        w1_hi = sb("w1_hi", [P, DC, FF], F32R, ffn)
        w1_lo = sb("w1_lo", [P, DC, FF], F32R, ffn)
        w2_hi = sb("w2_hi", [P, FC, D], F32R, ffn)
        w2_lo = sb("w2_lo", [P, FC, D], F32R, ffn)
        sb("odd_mask", [P, ST, CHUNK], BF16, ffn)
        w1_raw = sb("w1_raw", [P, DC, FF], F32, ffn)
        w2_raw = w1_raw[:].rearrange("p c n -> p (c n)").rearrange("p (f d) -> p f d", f=FC)
        wo_raw = sb("wo_raw", [P, DC, D], F32, ffn)
        wo_hi = sb("wo_hi", [P, DC, D], F32R, ffn)
        wo_lo = sb("wo_lo", [P, DC, D], F32R, ffn)
        sums = sb("sums", [P, HEADS * S // P], F32, ffn)
        no_edge = sb("no_edge", [P, HEADS * S // P], F32, ffn)

        params_in = sem("params_in")
        nodes_in = sem("nodes_in")
        consts = sem("consts")
        pool_made = sem("pool_made")
        keys_oned = sem("keys_oned")
        w_hi_ready = sem("w_hi_ready")
        w_lo_ready = sem("w_lo_ready")
        vsum_ready = sem("vsum_ready")
        vmean_done = sem("vmean_done")
        vmean_ready = sem("vmean_ready")
        x_rows_in = sem("x_rows_in")
        x_rest_in = sem("x_rest_in")
        norm_a = sem("norm_a")
        rectified = sem("rectified")
        norm_b = sem("norm_b")
        k_turned = sem("k_turned")
        k_affine = sem("k_affine")
        k_masked = sem("k_masked")
        k_hi = sem("k_hi")
        k_lo = sem("k_lo")
        k_projected = sem("k_projected")
        k_out = sem("k_out")
        k_squared = sem("k_squared")
        k_split_hi = sem("k_split_hi")
        k_split_lo = sem("k_split_lo")
        last_k_lo = sem("last_k_lo")
        first_q_lo = sem("first_q_lo")
        k_stacked = [sem("k_stacked_even"), sem("k_stacked_odd")]
        v_projected = sem("v_projected")
        v_ready = sem("v_ready")
        k_norms = sem("k_norms")
        k_norm_max = sem("k_norm_max")
        rows_in = sem("rows_in")
        norm_t = sem("norm_t")
        ht_kept = sem("ht_kept")
        turned = sem("turned")
        affine_out = sem("affine_out")
        hi_ready = sem("hi_ready")
        lo_ready = sem("lo_ready")
        projected = sem("projected")
        proj_out = sem("proj_out")
        squared = sem("squared")
        split_hi = sem("split_hi")
        split_lo = sem("split_lo")
        stacked = sem("stacked")
        q_zeroed = sem("q_zeroed")
        norms = sem("norms")
        norm_max = sem("norm_max")
        bound_col = sem("bound_col")
        bound_row = sem("bound_row")
        flag_ready = sem("flag_ready")
        flag_read = sem("flag_read")
        adj_in = sem("adj_in")
        mask_turned = sem("mask_turned")
        mask_tested = sem("mask_tested")
        q_copied = [sem("q_copied_even"), sem("q_copied_odd")]
        max_adj_in = sem("max_adj_in")
        max_tested = sem("max_tested")
        max_scored = sem("max_scored")
        max_masked = sem("max_masked")
        max_taken = sem("max_taken")
        max_col = sem("max_col")
        max_turned = sem("max_turned")
        max_split = sem("max_split")
        max_stacked = sem("max_stacked")
        scored = sem("scored")
        masked = sem("masked")
        exped = sem("exped")
        used = sem("used")
        added = sem("added")
        context_done = sem("context_done")
        closed = sem("closed")
        evacuated = sem("evacuated")
        saved = sem("saved")
        sums_in = sem("sums_in")
        inverted = sem("inverted")
        inverses_out = sem("inverses_out")
        stage3 = sem("stage3")
        w3_in = sem("w3_in")
        v3_in = sem("v3_in")
        w3_hi = sem("w3_hi")
        w3_lo = sem("w3_lo")
        mix_in = sem("mix_in")
        ht_in = sem("ht_in")
        x_in = sem("x_in")
        divided = sem("divided")
        c_hi = sem("c_hi")
        c_lo = sem("c_lo")
        residual = sem("residual")
        attended = sem("attended")
        mixed = sem("mixed")
        norm_y = sem("norm_y")
        y_ready = sem("y_ready")
        xy_ready = sem("xy_ready")
        y_turned = sem("y_turned")
        y_affine = sem("y_affine")
        y_hi = sem("y_hi")
        y_lo = sem("y_lo")
        ff1 = sem("ff1")
        gelu_out = sem("gelu_out")
        g_split = sem("g_split")
        ff2 = sem("ff2")
        summed = sem("summed")
        stored = sem("stored")
        gate = {n: sem(f"gate_{n}") for n in ("sp", "pool", "dve", "pe")}

        block = ctx.enter_context(nc.Block())

        def three(mm, dst, a_hi, a_lo, b_hi, b_lo, first, last):
            mm(dst, a_hi, b_hi, start=first, stop=False)
            mm(dst, a_hi, b_lo, start=False, stop=False)
            return mm(dst, a_lo, b_hi, start=False, stop=last)

        def stat_steps(n):
            return 2 * n + 3 + 3 * NEWTON

        LN_STEPS = stat_steps(TILES) + TILES

        def layer_stats(dve, src, st, mo, rs, n, signal, base):
            va, ne = variance[:, 0:n, :], newton[:, 0:n, :]
            for t in range(n):
                nc.vector.bn_stats(st[:, t, :], src[:, t, :]).then_inc(signal, 1)
            dve.wait_ge(signal, base + n)
            dve.sem_inc(gate["dve"], 1)
            for t in range(n):
                nc.vector.bn_aggr(mo[:, t, :], st[:, t, :]).then_inc(signal, 1)
            dve.wait_ge(signal, base + 2 * n)
            done = base + 2 * n
            nc.vector.tensor_scalar(va, mo[:, :, 1:2], EPS, None, ALU.add).then_inc(signal, 1)
            dve.wait_ge(signal, done + 1)
            nc.vector.tensor_scalar(rs.bitcast(I32), va.bitcast(I32), 1, None, ALU.arith_shift_right
                                    ).then_inc(signal, 1)
            dve.wait_ge(signal, done + 2)
            nc.vector.tensor_scalar(rs.bitcast(I32), rs.bitcast(I32), -1, RSQRT_GUESS, ALU.mult, ALU.add
                                    ).then_inc(signal, 1)
            dve.wait_ge(signal, done + 3)
            for k in range(NEWTON):
                nc.vector.tensor_tensor(ne, rs, rs, ALU.mult).then_inc(signal, 1)
                dve.wait_ge(signal, done + 4 + 3 * k)
                nc.vector.scalar_tensor_tensor(out=ne, in0=va, scalar=-0.5, in1=ne, op0=ALU.mult, op1=ALU.mult
                                               ).then_inc(signal, 1)
                dve.wait_ge(signal, done + 5 + 3 * k)
                nc.vector.scalar_tensor_tensor(out=rs, in0=ne, scalar=1.5, in1=rs, op0=ALU.add, op1=ALU.mult
                                               ).then_inc(signal, 1)
                dve.wait_ge(signal, done + 6 + 3 * k)

        def layer_apply(src, mo, rs, n, signal):
            for t in range(n):
                nc.vector.tensor_scalar(src[:, t, :], src[:, t, :], mo[:, t, 0:1], rs[:, t, :],
                                        ALU.subtract, ALU.mult).then_inc(signal, 1)

        def of_chunk(c):
            return bass.ds(c * TILES, TILES)

        def cols(c):
            return bass.ds(c * CHUNK, CHUNK)

        INV = 4
        EARLY_COLS = (NCH - 1) * CHUNK

        def packed(saved_sums, part):
            ts = slice(0, EARLY_COLS) if part == 0 else slice(EARLY_COLS, S)
            n = (EARLY_COLS if part == 0 else CHUNK) * HEADS // P
            return saved_sums[:, ts].rearrange("h (a b) -> h a b", b=n)

        def places(part):
            n = EARLY_COLS * HEADS // P
            return slice(0, n) if part == 0 else slice(n, HEADS * S // P)

        def stack_keys_lo(queue, c, signal):
            queue.wait_ge(k_split_lo, c + 1)
            for j in range(PER):
                queue.dma_start(kst[HD:2 * HD, j::PER, c * CHUNK:(c + 1) * CHUNK].bitcast(F32),
                                KBUF[c % 2][0][HD * j:HD * j + HD, :, :]).then_inc(signal, 16)

        def row_vector(v):
            return v.rearrange("(o d) -> o d", o=1).to_broadcast([P, D])

        KBUF = [(proj, proj_hi), (proj_odd, proj_hi_odd)]
        qst_flat = qst[:].rearrange("p b h t -> p (b h) t")
        mask_flat = maskT[:].rearrange("p b i t -> p (b i) t")

        def qpart(c):
            return (1 - c % 2) * HEADS

        @block.sync
        def _(sp):
            def after(semaphore, value):
                sp.wait_ge(semaphore, value)
                sp.sem_inc(gate["sp"], 1)

            def turn_mask(c, t, par):
                after(adj_in, 16 * (c * TILES + t + 1))
                if isinstance(c, int) and c == 0:
                    dst = mask_flat[:, 0:ST, t * P:(t + 1) * P]
                else:
                    dst = mask_flat[:, bass.ds(par * ST, ST), t * P:(t + 1) * P]
                sp.dma_start_transpose(dst, adj_raw[:]).then_inc(mask_turned, 16)

            def keep_rows(src, c):
                after(norm_t, (c + 1) * LN_STEPS)
                sp.dma_start(hts_rows[:, of_chunk(c), :], src[:]).then_inc(ht_kept, 16)

            def stack_queries(c):
                after(split_hi, c + 1)
                base = HEADS if isinstance(c, int) else sp.snap(qpart(c))
                for part in range(3):
                    if part == 2:
                        if isinstance(c, int):
                            break
                        after(split_lo, c + 1)
                    for j in range(PER):
                        src = proj if part == 2 else proj_hi
                        heads = (slice(base + j, base + HEADS, PER) if isinstance(c, int)
                                 else bass.ds(base + j, GROUPS, PER))
                        sp.dma_start(qst_flat[HD * part:HD * part + HD, heads, :].bitcast(F32),
                                     src[HD * j:HD * j + HD, :, :]).then_inc(stacked, 16)
                if not isinstance(c, int):
                    no_shift(c, base)

            def no_shift(c, base):
                heads = slice(base, base + HEADS) if isinstance(c, int) else bass.ds(base, HEADS)
                dst = qst_flat[AUX:KROWS, heads, :].bitcast(F32).rearrange("r h t -> r (h t)")
                sp.dma_start(dst.rearrange("r (k z) -> r k z", z=ZROW),
                             zeros[:, None, :].to_broadcast([2, HEADS * CHUNK // ZROW, ZROW])
                             ).then_inc(q_zeroed, 16)

            def load_flag():
                return sp.value_load(flag[0:1, 0:1], min_val=0, max_val=1)

            def find_maximum(c, general):
                with sp.If(general):
                    after(stacked, STACKS * (c + 1))
                    after(norms, c + 1)
                    for k in range(HEADS // 2):
                        if k > 1:
                            after(max_masked, (c * HEADS // 2 + k - 1) * TILES * PAIRS * 2)
                        sp.dma_start(qcopy[k % 2][0:AUX],
                                     qst_flat[0:AUX, bass.ds(qpart(c) + 2 * k, 2), :].bitcast(F32)
                                     ).then_inc(q_copied[k % 2], 16)
                    after(max_split, 2 * c + 2)
                    after(q_zeroed, 16 * (c + 1))
                    for t in range(TILES):
                        for part in range(2):
                            sp.dma_start(
                                qst_flat[AUX + part:AUX + part + 1, bass.ds(qpart(c), HEADS),
                                         t * P:(t + 1) * P].bitcast(F32),
                                mrow[t * HEADS:(t + 1) * HEADS, part, :].bitcast(F32)).then_inc(max_stacked, 16)
                with sp.Else():
                    for k in range(2):
                        sp.sem_inc(q_copied[k], 16 * (HEADS // 4))
                    sp.sem_inc(max_stacked, 16 * 2 * TILES)

            def save_context(c, g):
                G = c * GROUPS + g
                after(evacuated, 2 * (G + 1) + 1)
                sp.dma_start(ctx_saved[g * P:(g + 1) * P, cols(c)], evac[:]).then_inc(saved, 16)
                after(evacuated, 2 * (G + 1) + 2)
                sp.dma_start(sums_saved[g * PER:(g + 1) * PER, cols(c)], evac[0:P:HD, :]).then_inc(saved, 16)

            def load_sums(part):
                sp.dma_start(sums[:, places(part)], packed(sums_saved, part)).then_inc(sums_in, 16)

            def store_inverses(part):
                sp.wait_ge(inverted, INV * (part + 1))
                sp.dma_start(packed(inverse_saved, part), sums[:, places(part)]).then_inc(inverses_out, 16)

            def column(v):
                return v.rearrange("(g p) -> p g", p=P)

            sp.dma_start(xs[:, 0:TILES, :], x_rows[:, 0:TILES, :]).then_inc(x_rows_in, 16)
            sp.dma_start(xs[:, TILES:2 * TILES, :], x_rows[:, TILES:2 * TILES, :]).then_inc(x_rows_in, 16)
            sp.dma_start(xs[:, 2 * TILES:, :], x_rows[:, 2 * TILES:, :]).then_inc(x_rest_in, 16)
            for i, w in enumerate((Wk, Wv, Wq)):
                sp.dma_start(w_raw[:, i], w.rearrange("(c p) n -> p c n", p=P)).then_inc(params_in, 16)
            sp.dma_start(vbias[:], row_vector(bv)).then_inc(params_in, 16)
            with nc.allow_non_contiguous_dma(reason="columns of small vectors"):
                for dst, src in ((kbias, bk), (qbias_in, bq), (gamma1, ln1_scale), (beta1, ln1_bias),
                                 (nm_int, nodemask)):
                    sp.dma_start(dst[:], column(src)).then_inc(params_in, 16)
            sp.dma_start(rows_first[:], ht_rows[:, 0:TILES, :]).then_inc(rows_in, 16)
            turn_mask(0, 0, 0)
            sp.wait_ge(pool_made, 4)
            no_shift(0, HEADS)
            for c in range(NCH):
                if c + 1 < TILES:
                    turn_mask(0, c + 1, 0)
                if c == 1:
                    keep_rows(rows_first, 0)
                sp.wait_ge(k_split_hi, c + 1)
                for part in (0, 2):
                    for j in range(PER):
                        sp.dma_start(kst[HD * part:HD * part + HD, j::PER, c * CHUNK:(c + 1) * CHUNK].bitcast(F32),
                                     KBUF[c % 2][1][HD * j:HD * j + HD, :, :]).then_inc(k_stacked[c % 2], 16)
                if c + 1 < NCH:
                    stack_keys_lo(sp, c, k_stacked[c % 2])
            stack_queries(0)
            sp.wait_ge(last_k_lo, 16 * PER)
            sp.sem_inc(k_stacked[(NCH - 1) % 2], 16 * PER)
            sp.wait_ge(first_q_lo, 16 * PER)
            sp.sem_inc(stacked, 16 * PER)
            sp.sem_inc(saved, 32)
            sp.wait_ge(flag_ready, 2)
            general = load_flag()
            sp.sem_inc(flag_read, 1)
            find_maximum(0, general)

            def front(c):
                after(norms, c)
                after(max_turned, c)
                sp.dma_start(rows[:], ht_rows[:, of_chunk(c), :]).then_inc(rows_in, 16)
                after(mask_tested, 4 * c)
                after(masked, (c - 1) * UNITS + SLOTS + 1)
                turn_mask(c, 0, c % 2)
                keep_rows(rows, c)
                turn_mask(c, 1, c % 2)
                turn_mask(c, 2, c % 2)
                save_context(c - 1, 0)
                after(scored, (c - 1) * UNITS + 1)
                stack_queries(c)

            with sp.Fori(0, NCH - 1) as c:
                front(c + 1)
                turn_mask(c + 1, 3, (c + 1) % 2)
                after(flag_ready, 2 * (c + 1) + 2)
                general = load_flag()
                sp.sem_inc(flag_read, 1)
                find_maximum(c + 1, general)
                save_context(c, 1)

            c = NCH - 1
            sp.wait_ge(stacked, STACKS * NCH)
            sp.wait_ge(max_stacked, 16 * 2 * TILES * NCH)
            sp.wait_ge(norms, NCH)
            sp.wait_ge(ht_kept, 16 * NCH)
            sp.wait_ge(mask_turned, 16 * TILES * NCH)
            sp.wait_ge(scored, c * UNITS + 1)
            sp.wait_ge(masked, c * UNITS + SLOTS + 1)
            sp.dma_start(wo_raw[:], Wo.rearrange("(c p) n -> p c n", p=P)).then_inc(w3_in, 16)
            sp.dma_start(w1_raw[:], W1.rearrange("(c p) n -> p c n", p=P)).then_inc(w3_in, 16)
            sp.wait_ge(saved, 32 * (c * GROUPS + 1))
            load_sums(0)
            store_inverses(0)
            save_context(c, 0)
            sp.wait_ge(w3_lo, 2)
            sp.dma_start(w2_raw, W2.rearrange("(c p) n -> p c n", p=P)).then_inc(w3_in, 16)

            def load_mix(c):
                for g in range(GROUPS):
                    heads = inverse_saved[g * PER:(g + 1) * PER, cols(c)]
                    sp.dma_start(dT[:, g, :], heads[:, None, :].to_broadcast([PER, HD, CHUNK])).then_inc(mix_in, 16)
                sp.dma_start(cT[:], ctx_saved.rearrange("(g p) t -> p g t", p=P)[:, :, cols(c)]).then_inc(mix_in, 16)

            def load_targets(c):
                sp.dma_start(ht[:], hts_rows[:, of_chunk(c), :]).then_inc(ht_in, 16)

            sp.wait_ge(inverses_out, 16)
            sp.wait_ge(scored, NCH * UNITS)
            load_mix(0)
            load_targets(0)
            for dst, src in ((gamma1_row, ln1_scale), (beta1_row, ln1_bias), (obias, bo), (gamma2, ln2_scale),
                             (beta2, ln2_bias)):
                sp.dma_start(dst[:], row_vector(src)).then_inc(v3_in, 16)
            with nc.allow_non_contiguous_dma(reason="columns of small vectors"):
                for dst, src in ((gamma2_col, ln2_scale), (beta2_col, ln2_bias)):
                    sp.dma_start(dst[:], column(src)).then_inc(v3_in, 16)
            save_context(c, 1)

            sp.wait_ge(used, NCH * UNITS + RING)
            sp.wait_ge(closed, NCH * GROUPS + 1)
            sp.sem_inc(stage3, 1)
            sp.dma_start(xr[:], x_rows[:, 0:TILES, :]).then_inc(x_in, 16)
            sp.wait_ge(saved, 32 * (NCH * GROUPS + 1))
            load_sums(1)
            store_inverses(1)
            sp.wait_ge(inverses_out, 32)

            def load_next(c):
                after(c_lo, c)
                load_mix(c)
                after(mixed, c)
                load_targets(c)

            def load_x(c):
                after(xy_ready, c)
                sp.dma_start(xr[:], x_rows[:, of_chunk(c), :]).then_inc(x_in, 16)

            def store(c):
                after(summed, TILES * (c + 1))
                sp.dma_start(out_rows[:, of_chunk(c), :], result[:]).then_inc(stored, 16)

            load_next(1)
            with sp.Fori(1, NCH - 1) as c:
                load_x(c)
                load_next(c + 1)
                store(c - 1)
            load_x(NCH - 1)
            store(NCH - 2)
            store(NCH - 1)
            sp.wait_ge(stored, 16 * NCH)

        @block.gpsimd
        def _(pool):
            def after(semaphore, value):
                pool.wait_ge(semaphore, value)
                pool.sem_inc(gate["pool"], 1)

            def load_adj(c, t, first=False):
                if not first:
                    after(mask_turned, 16 * (c * TILES + t))
                pool.dma_start(adj_raw[:], adj_rows[bass.ds(c * TILES + t, 1)].rearrange("o p s -> (o p) s")
                               ).then_inc(adj_in, 16)

            load_adj(0, 0, first=True)
            pool.dma_start(node_row[:], nodemask.rearrange("(o s) -> o s", o=1).to_broadcast([P, S])
                           ).then_inc(nodes_in, 16)
            nc.gpsimd.memset(ident[:], 0.0).then_inc(pool_made, 1)
            nc.gpsimd.memset(ones[:], 1.0).then_inc(pool_made, 1)
            nc.gpsimd.memset(headsum[:], 0.0).then_inc(pool_made, 1)
            pool.wait_ge(pool_made, 3)
            nc.gpsimd.affine_select(out=ident[:], in_=ident[:], compare_op=ALU.not_equal, fill=1.0, base=0,
                                    pattern=[[-1, P]], channel_multiplier=1).then_inc(pool_made, 1)
            for j in range(PER):
                pool.wait_ge(pool_made, 4 + j)
                nc.gpsimd.memset(headsum[HD * j:HD * j + HD, HD * j:HD * j + HD], 1.0).then_inc(pool_made, 1)
            pool.wait_ge(pool_made, 4 + PER)
            nc.gpsimd.memset(kst[AUX:KROWS].bitcast(F32), 1.0).then_inc(keys_oned, 1)
            pool.wait_ge(keys_oned, 1)
            pool.wait_ge(consts, 1)
            for c in range(NCH):
                wide, (hi, lo) = WIDE[c % 2], RT[c % 2]
                pool.wait_ge(k_affine, DC * (c + 1))
                nc.gpsimd.tensor_tensor(wide, wide, node_row[:, None, c * CHUNK:(c + 1) * CHUNK].to_broadcast(
                    [P, DC, CHUNK]), ALU.mult).then_inc(k_masked, 1)
                pool.wait_ge(k_hi, c + 1)
                if c >= 2:
                    pool.wait_ge(v_projected, c - 1)
                nc.gpsimd.tensor_tensor(lo[:], wide, hi[:].bitcast(F32), ALU.subtract).then_inc(k_lo, 1)
                if c + 1 < TILES:
                    load_adj(0, c + 1)

            def turned_lo(c, hi, lo):
                pool.wait_ge(hi_ready, c + 1)
                nc.gpsimd.tensor_tensor(lo, turned_full, hi.bitcast(F32), ALU.subtract).then_inc(lo_ready, 1)

            def queries_lo(c):
                pool.wait_ge(squared, c + 1)
                pool.wait_ge(split_hi, c + 1)
                nc.gpsimd.tensor_tensor(proj[:].bitcast(F32R), proj[:], proj_hi[:], ALU.subtract
                                        ).then_inc(split_lo, 1)

            def find_maximum(c, general):
                with pool.If(general):
                    for k in range(HEADS // 2):
                        for t in range(TILES):
                            if k or t:
                                after(max_masked, ((c * HEADS // 2 + k) * TILES + t) * 2 * 2)
                            pool.dma_start(adj_raw[:], adj_rows[bass.ds(c * TILES + t, 1)].rearrange(
                                "o p s -> (o p) s")).then_inc(max_adj_in, 16)
                    after(max_masked, (c + 1) * TILES * 2 * HEADS)
                with pool.Else():
                    pool.sem_inc(max_adj_in, 16 * TILES * HEADS // 2)

            pool.wait_ge(v_projected, NCH - 1)
            turned_lo(0, RT[0][0][:], RT[0][1][:])
            stack_keys_lo(pool, NCH - 1, last_k_lo)
            queries_lo(0)
            pool.wait_ge(split_lo, 1)
            for j in range(PER):
                pool.dma_start(qst_flat[2 * HD:3 * HD, HEADS + j:2 * HEADS:PER, :].bitcast(F32),
                               proj[HD * j:HD * j + HD, :, :]).then_inc(first_q_lo, 16)
            pool.wait_ge(flag_ready, 2)
            general = pool.value_load(flag[0:1, 0:1], min_val=0, max_val=1)
            pool.sem_inc(flag_read, 1)
            after(mask_turned, 16 * TILES)
            find_maximum(0, general)

            def add_up(c, g, i, pair):
                def at(tile):
                    return probs[:, ((g * ST + tile) * PAIRS + pair) % RING]
                k = c * ADDS + add_index(g, i, pair)
                pool.wait_ge(exped, c * UNITS + (g * ST + i) * PAIRS + pair + 1)
                if i == ADDED[1]:
                    after(closed, c * GROUPS + g + 1)
                    nc.gpsimd.tensor_tensor(psum2[:, pair], at(ADDED[0]), at(i), ALU.add).then_inc(added, 1)
                else:
                    after(added, k - PAIRS + 1 + 1)
                    nc.gpsimd.tensor_tensor(psum2[:, pair], psum2[:, pair], at(i), ALU.add).then_inc(added, 1)

            def chunk(c, last):
                todo = {
                    (0, 1): lambda: load_adj(c + 1, 0), (0, 6): lambda: load_adj(c + 1, 1),
                    (0, 11): lambda: turned_lo(c + 1, late_hi[:], late_lo[:]), (0, 13): lambda: load_adj(c + 1, 2),
                    (1, 1): lambda: queries_lo(c + 1), (1, 3): lambda: load_adj(c + 1, 3)}
                if last:
                    todo = {(0, 6): lambda: weight_lo(0), (0, 11): lambda: weight_lo(1), (1, 11): lambda: weight_lo(2)}
                for g in range(GROUPS):
                    for i in ADDED[1:]:
                        for pair in range(PAIRS):
                            add_up(c, g, i, pair)
                        if (g, i) in todo:
                            todo[g, i]()

            def weight_lo(k):
                dst, src, hi = ((wo_lo, wo_raw[:], wo_hi), (w1_lo, w1_raw[:], w1_hi), (w2_lo, w2_raw, w2_hi))[k]
                pool.wait_ge(w3_hi, k + 1)
                nc.gpsimd.tensor_tensor(dst[:], src, hi[:].bitcast(F32), ALU.subtract).then_inc(w3_lo, 1)

            pool.sem_inc(added, 1)
            with pool.Fori(0, NCH - 1) as c:
                chunk(c, False)
                after(flag_ready, 2 * (c + 1) + 2)
                general = pool.value_load(flag[0:1, 0:1], min_val=0, max_val=1)
                pool.sem_inc(flag_read, 1)
                after(mask_turned, 16 * TILES * (c + 2))
                find_maximum(c + 1, general)
            chunk(NCH - 1, True)

            pool.wait_ge(v3_in, 16 * 7)
            wide3 = [P, TILES, D]

            def make_residual(c):
                pool.wait_ge(ht_in, 16 * (c + 1))
                nc.gpsimd.tensor_tensor(ht[:], ht[:], gamma1_row[:, None, :].to_broadcast(wide3), ALU.mult
                                        ).then_inc(residual, 1)
                pool.wait_ge(residual, 2 * c + 1 + 1)
                nc.gpsimd.tensor_tensor(ht[:], ht[:], beta1_row[:, None, :].to_broadcast(wide3), ALU.add
                                        ).then_inc(residual, 1)

            def finish_y(c, first=False):
                pool.wait_ge(norm_y, (c + 1) * LN_STEPS)
                pool.wait_ge(y_turned, c + 1)
                nc.gpsimd.tensor_tensor(y[:], y[:], gamma2[:, None, :].to_broadcast(wide3), ALU.mult
                                        ).then_inc(y_ready, 1)
                pool.wait_ge(y_ready, 3 * c + 1)
                nc.gpsimd.tensor_tensor(y[:], y[:], beta2[:, None, :].to_broadcast(wide3), ALU.add
                                        ).then_inc(y_ready, 1)
                pool.wait_ge(y_ready, 3 * c + 2)
                nc.gpsimd.tensor_tensor(y[:], y[:], nodes[:, of_chunk(c)][:, :, None].to_broadcast(wide3), ALU.mult
                                        ).then_inc(y_ready, 1)
                if not first:
                    pool.wait_ge(summed, c * TILES)
                pool.wait_ge(x_in, 16 * c + 16)
                pool.wait_ge(y_ready, 3 * c + 3)
                nc.gpsimd.tensor_tensor(xy[:], xr[:], y[:], ALU.add).then_inc(xy_ready, 1)

            nc.gpsimd.tensor_tensor(beta1_row[:], beta1_row[:], obias[:], ALU.add).then_inc(residual, 1)
            pool.wait_ge(residual, 1)
            make_residual(0)
            finish_y(0, first=True)
            with pool.Fori(1, NCH) as c:
                make_residual(c)
                finish_y(c)

        @block.scalar
        def _(act):
            for half in range(2):
                act.wait_ge(norm_a, (half + 1) * (stat_steps(HALF) + 1))
                for t in range(half * HALF, (half + 1) * HALF):
                    nc.scalar.activation(xs[:, t, :], xs[:, t, :], ACT.Relu, bias=shift_s[:, t, :],
                                         scale=rstd_s[:, 0, t, :]).then_inc(rectified, 1)
                if half == 0:
                    act.wait_ge(params_in, 16 * 9)
                    nc.scalar.mul(qbias[:], qbias_in[:], QSCALE).then_inc(w_hi_ready, 1)
                    for i, dst in enumerate((wk_hi, wv_hi, wq_hi)):
                        nc.scalar.copy(dst[:], w_raw[:, i]).then_inc(w_hi_ready, 1)

            def affine(dst, src, signal):
                for d in range(DC):
                    nc.scalar.activation(dst[:, d, :], src[:, d, :], ACT.Identity, bias=beta1[:, d:d + 1],
                                         scale=gamma1[:, d:d + 1]).then_inc(signal, 1)

            def source_out(c):
                whole, hi = KBUF[c % 2]
                act.wait_ge(k_projected, c + 1)
                if c >= 2:
                    act.wait_ge(k_stacked[c % 2], STACKS * (c // 2))
                for g in range(GROUPS):
                    nc.scalar.activation(whole[:, g, :], slot[1][:, g, :], ACT.Identity, bias=kbias[:, g:g + 1]
                                         ).then_inc(k_out, 1)
                act.wait_ge(k_out, GROUPS * (c + 1))
                if c:
                    act.wait_ge(k_norms, c)
                nc.scalar.activation(squares_early, whole[:], ACT.Square).then_inc(k_squared, 1)
                nc.scalar.copy(hi[:].bitcast(F32R), whole[:]).then_inc(k_split_hi, 1)

            for c in range(NCH):
                act.wait_ge(k_turned, c + 1)
                if c >= 2:
                    act.wait_ge(k_lo, c - 1)
                affine(WIDE[c % 2], slot[0], k_affine)
                act.wait_ge(k_masked, c + 1)
                if c >= 2:
                    act.wait_ge(v_projected, c - 1)
                nc.scalar.copy(RT[c % 2][0][:], WIDE[c % 2]).then_inc(k_hi, 1)
                if c:
                    source_out(c - 1)

            def queries_affine(c, src, hi, first=False):
                act.wait_ge(turned, c + 1)
                if first:
                    act.wait_ge(k_lo, NCH - 1)
                    act.wait_ge(v_projected, NCH - 1)
                else:
                    act.wait_ge(ht_kept, 16 * (c + 1))
                    act.wait_ge(stacked, STACKS * c)
                    act.wait_ge(max_stacked, 16 * 2 * TILES * c)
                affine(turned_full, src, affine_out)
                act.wait_ge(affine_out, DC * (c + 1))
                nc.scalar.copy(hi, turned_full).then_inc(hi_ready, 1)

            def queries_out(c, src, g):
                if g == 0:
                    act.wait_ge(projected, GROUPS * (c + 1))
                nc.scalar.activation(proj[:, g, :], src[:, g, :], ACT.Identity, bias=qbias[:, g:g + 1],
                                     scale=QSCALE).then_inc(proj_out, 1)

            def queries_split(c):
                act.wait_ge(proj_out, GROUPS * (c + 1))
                act.wait_ge(lo_ready, c + 1)
                nc.scalar.activation(squares_late, proj[:], ACT.Square).then_inc(squared, 1)
                nc.scalar.copy(proj_hi[:].bitcast(F32R), proj[:]).then_inc(split_hi, 1)

            queries_affine(0, slot[0], RT[0][0][:], first=True)
            source_out(NCH - 1)
            act.wait_ge(k_stacked[0], STACKS * NCH // 2)
            for g in range(GROUPS):
                queries_out(0, slot[0], g)
            queries_split(0)
            act.wait_ge(vmean_done, 1)
            nc.scalar.mul(vmean[:], acc[:, 0, 0:GROUPS], 1.0 / S).then_inc(vmean_ready, 1)
            act.wait_ge(vmean_ready, 1)
            act.sem_inc(evacuated, 2)

            def evacuate(c, g, b):
                G = c * GROUPS + g
                act.wait_ge(closed if b else context_done, G + 2 if b else G + 1)
                act.wait_ge(saved, 16 * (2 * G + b) + 32)
                nc.scalar.copy(evac[:], acc[:, b, :]).then_inc(evacuated, 1)

            START = AHEAD + 2

            def exponentials(c, u):
                act.wait_ge(masked, c * UNITS + u + 1 + SLOTS)
                r = probs[:, u % RING]
                nc.scalar.activation(r, r, ACT.Exp).then_inc(exped, 1)

            def weight_hi(k):
                dst, src = ((wo_hi, wo_raw[:]), (w1_hi, w1_raw[:]), (w2_hi, w2_raw))[k]
                act.wait_ge(w3_in, 32 if k < 2 else 48)
                nc.scalar.copy(dst[:], src).then_inc(w3_hi, 1)

            def chunk(c, last):
                n = c + 1
                todo = {
                    20: lambda: queries_affine(n, slot[place("turned")], late_hi[:]),
                    31: lambda: queries_out(n, slot[place("projected 0")], 0),
                    32: lambda: queries_out(n, slot[place("projected 1")], 1),
                    35: lambda: queries_split(n)}
                if last:
                    todo = {10: lambda: weight_hi(0), 16: lambda: weight_hi(1), 50: lambda: weight_hi(2)}
                for g in range(GROUPS):
                    todo[(g + 1) * UG + AHEAD - 2] = lambda g=g: evacuate(c, g, 0)
                    todo[(g + 1) * UG + AHEAD + 1] = lambda g=g: evacuate(c, g, 1)
                for u in range(START, UNITS + START):
                    if u in todo:
                        todo[u]()
                    if u < UNITS:
                        exponentials(c, u)
                    elif not last:
                        exponentials(n, u - UNITS)

            for u in range(START):
                exponentials(0, u)
            with act.Fori(0, NCH - 1) as c:
                chunk(c, False)
            chunk(NCH - 1, True)

            def context_hi(c):
                act.wait_ge(divided, 4 * (c + 1))
                nc.scalar.copy(cT_hi[:], cT[:]).then_inc(c_hi, 1)

            def turned_y(c):
                act.wait_ge(y_turned, c + 1)
                for d in range(DC):
                    nc.scalar.activation(yT[:, d, :], side[:, d, :], ACT.Identity, bias=beta2_col[:, d:d + 1],
                                         scale=gamma2_col[:, d:d + 1]).then_inc(y_affine, 1)
                act.wait_ge(y_affine, DC * (c + 1))
                nc.scalar.copy(yT_hi[:], yT[:]).then_inc(y_hi, 1)

            def gelu(c, first=False):
                for f in range(FC):
                    act.wait_ge(ff1, c * FC + f + 1)
                    if not (first and f < 2):
                        act.wait_ge(g_split, c * FC + f - 1)
                    h = slot[f % 2][:, f // 2 % 2, :]
                    nc.scalar.activation(g_full[:, f % 2, :], h, ACT.Gelu_apprx_tanh).then_inc(gelu_out, 1)
                    nc.scalar.activation(g_hi[:, f, :], h, ACT.Gelu_apprx_tanh).then_inc(gelu_out, 1)

            context_hi(0)
            turned_y(0)
            context_hi(1)
            gelu(0, first=True)
            turned_y(1)
            with act.Fori(1, NCH - 1) as c:
                context_hi(c + 1)
                gelu(c)
                turned_y(c + 1)
            gelu(NCH - 1)

        @block.vector
        def _(dve):
            nc.vector.memset(kmax[:], 0.0).then_inc(k_norm_max, 1)
            MADE = 1

            def first_norm(half):
                ts = slice(half * HALF, (half + 1) * HALF)
                per = stat_steps(HALF) + 1
                layer_stats(dve, xs[:, ts], stats_s[:, ts], moments_s[:, 0, ts], rstd_s[:, 0, ts], HALF, norm_a,
                            half * per)
                nc.vector.scalar_tensor_tensor(out=shift_s[:, ts], in0=moments_s[:, 0, ts, 0:1], scalar=-1.0,
                                               in1=rstd_s[:, 0, ts], op0=ALU.mult, op1=ALU.mult).then_inc(norm_a, 1)

            def second_norm(half):
                ts = slice(half * HALF, (half + 1) * HALF)
                per = stat_steps(HALF) + HALF
                dve.wait_ge(rectified, HALF * (half + 1))
                layer_stats(dve, xs[:, ts], stats_s[:, ts], moments_s[:, 1, ts], rstd_s[:, 1, ts], HALF, norm_b,
                            half * per)
                layer_apply(xs[:, ts], moments_s[:, 1, ts], rstd_s[:, 1, ts], HALF, norm_b)

            def target_norm(src, c):
                dve.wait_ge(rows_in, 16 * (c + 1))
                layer_stats(dve, src, stats, moments, rstd[:], TILES, norm_t, c * LN_STEPS)

            dve.wait_ge(x_rows_in, 32)
            first_norm(0)
            dve.wait_ge(x_rest_in, 16)
            first_norm(1)
            dve.wait_ge(params_in, 16 * 9)
            dve.wait_ge(nodes_in, 16)
            nc.vector.tensor_scalar(nodes[:], nm_int[:], 1, None, ALU.is_equal).then_inc(k_norm_max, 1)
            nc.vector.tensor_scalar(node_row[:], node_row[:], 1.0, None, ALU.is_equal).then_inc(k_norm_max, 1)
            MADE += 2
            second_norm(0)
            dve.wait_ge(k_norm_max, MADE)
            dve.sem_inc(consts, 1)
            dve.wait_ge(w_hi_ready, 4)
            for i, (dst, hi) in enumerate(((wk_lo, wk_hi), (wv_lo, wv_hi), (wq_lo, wq_hi))):
                nc.vector.tensor_tensor(dst[:], w_raw[:, i], hi[:].bitcast(F32), ALU.subtract).then_inc(w_lo_ready, 1)
            second_norm(1)
            target_norm(rows_first, 0)
            layer_apply(rows_first, moments, rstd, TILES, norm_t)

            def test_mask(c, t):
                dve.wait_ge(mask_turned, 16 * (c * TILES + t + 1))
                if isinstance(c, int) and c == 0:
                    m = mask_flat[:, 0:ST, t * P:(t + 1) * P]
                else:
                    m = mask_flat[:, bass.ds((c % 2) * ST, ST), t * P:(t + 1) * P]
                nc.vector.tensor_scalar(m, m, 0.0, None, ALU.is_equal).then_inc(mask_tested, 1)

            for c in range(NCH):
                dve.wait_ge(v_projected, c + 1)
                nc.vector.tensor_tensor(V[:, c * TILES:(c + 1) * TILES, :], acc4,
                                        vbias[:, None, :].to_broadcast([P, TILES, D]), ALU.add).then_inc(v_ready, 1)
                whole, hi = KBUF[c % 2]
                dve.wait_ge(k_squared, c + 1)
                dve.wait_ge(k_split_hi, c + 1)
                nc.vector.tensor_tensor(whole[:].bitcast(F32R), whole[:], hi[:], ALU.subtract).then_inc(k_split_lo, 1)
                dve.wait_ge(k_norms, c + 1)
                dve.wait_ge(k_norm_max, MADE + 2 * c)
                nc.vector.tensor_reduce(nmax[:], side[:], AX_X, ALU.max).then_inc(k_norm_max, 1)
                dve.wait_ge(k_norm_max, MADE + 2 * c + 1)
                nc.vector.tensor_tensor(kmax[:], kmax[:], nmax[:], ALU.max).then_inc(k_norm_max, 1)
                test_mask(0, c)
            dve.wait_ge(k_norm_max, MADE + 2 * NCH)

            def target_bound(c, src):
                dve.wait_ge(norms, c + 1)
                nc.vector.tensor_reduce(nmax[:], src[:], AX_X, ALU.max).then_inc(norm_max, 1)
                dve.wait_ge(norm_max, 2 * c + 1)
                nc.vector.tensor_tensor(nmax[:], nmax[:], kmax[:], ALU.mult).then_inc(norm_max, 1)
                dve.wait_ge(norm_max, 2 * c + 2)
                nc.vector.tensor_reduce(bound[:], nmax[:], AX_X, ALU.max).then_inc(bound_col, 1)

            def decide(c, src, first=False):
                dve.wait_ge(bound_row, c + 1)
                nc.vector.tensor_reduce(bound1[:], src[0:1, 0, 0:P], AX_X, ALU.max).then_inc(flag_ready, 1)
                dve.wait_ge(flag_ready, 2 * c + 1)
                if not first:
                    dve.wait_ge(flag_read, 4 * c)
                nc.vector.tensor_scalar(flag[:], bound1[:], SAFE * SAFE, None, ALU.is_gt).then_inc(flag_ready, 1)

            def load_flag(c):
                dve.wait_ge(flag_ready, 2 * c + 2)
                dve.sem_inc(gate["dve"], 1)
                general = dve.value_load(flag[0:1, 0:1], min_val=0, max_val=1)
                dve.sem_inc(flag_read, 1)
                return general

            def find_maximum(c, general):
                with dve.If(general):
                    dve.wait_ge(stacked, STACKS * (c + 1))
                    n = 0
                    for k in range(HEADS // 2):
                        for t in range(TILES):
                            dve.wait_ge(max_adj_in, 16 * ((c * HEADS // 2 + k) * TILES + t + 1))
                            nc.vector.tensor_scalar(adj_raw[:], adj_raw[:], 0.0, None, ALU.is_equal
                                                    ).then_inc(max_tested, 1)
                            dve.wait_ge(max_tested, (c * HEADS // 2 + k) * TILES + t + 1)
                            for h in (2 * k, 2 * k + 1):
                                for half in range(2):
                                    step = c * TILES * HEADS * 2 + n
                                    dve.wait_ge(max_scored, step + 1)
                                    if n:
                                        dve.wait_ge(max_taken, step)
                                    nc.vector.scalar_tensor_tensor(
                                        out=proj[:].rearrange("p a t -> p (a t)"),
                                        in0=adj_raw[:, half * 2 * CHUNK:(half + 1) * 2 * CHUNK], scalar=MASKED,
                                        in1=side[:].rearrange("p a t -> p (a t)"), op0=ALU.mult,
                                        op1=ALU.add).then_inc(max_masked, 1)
                                    dve.wait_ge(max_masked, step + 1)
                                    nc.vector.tensor_reduce(mpart[:, t * HEADS + h, half:half + 1],
                                                            proj[:].rearrange("p a t -> p (a t)"), AX_X, ALU.max
                                                            ).then_inc(max_taken, 1)
                                    n += 1
                    dve.wait_ge(max_taken, (c + 1) * TILES * HEADS * 2)
                    nc.vector.tensor_reduce(mcol[:], mpart[:], AX_X, ALU.max).then_inc(max_col, 1)
                    dve.wait_ge(max_turned, c + 1)
                    nc.vector.tensor_scalar(mneg, side[0:TILES * HEADS, 0, 0:P], -1.0, None, ALU.mult
                                            ).then_inc(max_col, 1)
                    dve.wait_ge(max_col, 2 * c + 2)
                    nc.vector.tensor_copy(mrow[:, 0, :], mneg).then_inc(max_split, 1)
                    dve.wait_ge(max_split, 2 * c + 1)
                    nc.vector.tensor_tensor(mrow[:, 1, :], mneg, mrow[:, 0, :].bitcast(F32), ALU.subtract
                                            ).then_inc(max_split, 1)
                with dve.Else():
                    dve.sem_inc(max_tested, TILES * HEADS // 2)
                    dve.sem_inc(max_masked, TILES * HEADS * 2)
                    dve.sem_inc(max_taken, TILES * HEADS * 2)
                    dve.sem_inc(max_col, 2)
                    dve.sem_inc(max_split, 2)

            target_bound(0, side)
            decide(0, side, first=True)
            dve.wait_ge(v_ready, NCH)
            nc.vector.tensor_reduce(vsum[:], V[:].rearrange("p i d -> p d i"), AX_X, ALU.add).then_inc(vsum_ready, 1)
            dve.sem_inc(masked, SLOTS)
            general = load_flag(0)
            find_maximum(0, general)

            def invert(part):
                at = places(part)
                base = INV * part
                dve.wait_ge(sums_in, 16 * (part + 1))
                nc.vector.tensor_scalar(no_edge[:, at], sums[:, at], 0.0, None, ALU.is_equal).then_inc(inverted, 1)
                dve.wait_ge(inverted, base + 1)
                nc.vector.tensor_tensor(sums[:, at], sums[:, at], no_edge[:, at], ALU.add).then_inc(inverted, 1)
                dve.wait_ge(inverted, base + 2)
                nc.vector.reciprocal(sums[:, at], sums[:, at]).then_inc(inverted, 1)
                dve.wait_ge(inverted, base + 3)
                nc.vector.scalar_tensor_tensor(out=sums[:, at], in0=no_edge[:, at], scalar=1.0, in1=sums[:, at],
                                               op0=ALU.is_lt, op1=ALU.mult).then_inc(inverted, 1)

            def ring_free(c, u):
                if u >= RING:
                    return c * UNITS + u - RING + 1
                before = u + (UNITS - 1 - u) // RING * RING
                return c * UNITS + before + 1 - UNITS

            def chunk(c, last):
                n = c + 1
                flagged = []
                todo = {20: lambda: invert(0)} if last else {
                    11: lambda: target_norm(rows, n),
                    13: lambda: layer_apply(rows, moments, rstd, TILES, norm_t),
                    16: lambda: test_mask(n, 0), 24: lambda: test_mask(n, 1), 44: lambda: target_bound(n, slot[place("norms")]),
                    40: lambda: test_mask(n, 2), 51: lambda: decide(n, slot[place("bound")]), 57: lambda: test_mask(n, 3),
                    60: lambda: flagged.append(load_flag(n))}
                for u in range(UNITS):
                    if u in todo:
                        todo[u]()
                    i = u % UG // PAIRS
                    if u == 0:
                        dve.wait_ge(mask_tested, TILES * (c + 1))
                    dve.wait_ge(scored, c * UNITS + u + 1)
                    dve.wait_ge(used, ring_free(c, u) + RING)
                    k = [add_index(g, j, pr) + 1 for g in range(GROUPS) for j in ADDED for pr in range(PAIRS)
                         if (g * ST + j) * PAIRS + pr <= u - RING]
                    dve.wait_ge(added, c * ADDS + (k[-1] if k else 0) + 1)
                    m = mask_flat[:, bass.ds((c % 2) * ST + i, 1), :].to_broadcast([P, 2, CHUNK])
                    nc.vector.scalar_tensor_tensor(out=probs[:, u % RING], in0=m, scalar=MASKED,
                                                   in1=slot[place(u, last)][:], op0=ALU.mult, op1=ALU.add
                                                   ).then_inc(masked, 1)
                if not last:
                    find_maximum(n, flagged[0])

            with dve.Fori(0, NCH - 1) as c:
                chunk(c, False)
            chunk(NCH - 1, True)

            def divide(c):
                dve.wait_ge(mix_in, 48 * (c + 1))
                for g in range(GROUPS):
                    nc.vector.tensor_scalar(mean_part[:, g, :], dT[:, g, :], 0.0, vmean[:, g:g + 1],
                                            ALU.is_equal, ALU.mult).then_inc(divided, 1)
                nc.vector.tensor_tensor(cT[:], cT[:], dT[:], ALU.mult).then_inc(divided, 1)
                dve.wait_ge(divided, 4 * c + 3)
                nc.vector.tensor_tensor(cT[:], cT[:], mean_part[:], ALU.add).then_inc(divided, 1)
                dve.wait_ge(c_hi, c + 1)
                nc.vector.tensor_tensor(cT_lo[:], cT[:], cT_hi[:].bitcast(F32), ALU.subtract).then_inc(c_lo, 1)

            def mix(c, first=False):
                dve.wait_ge(attended, c + 1)
                dve.wait_ge(residual, 2 * c + 3)
                if not first:
                    dve.wait_ge(xy_ready, c)
                    dve.wait_ge(y_turned, c)
                nc.vector.tensor_tensor(y[:], side4, ht[:], ALU.add).then_inc(mixed, 1)
                dve.wait_ge(mixed, c + 1)
                layer_stats(dve, y, stats, moments, rstd[:], TILES, norm_y, c * LN_STEPS)
                layer_apply(y, moments, rstd, TILES, norm_y)

            def turned_y(c):
                dve.wait_ge(y_hi, c + 1)
                nc.vector.tensor_tensor(yT_lo[:], yT[:], yT_hi[:].bitcast(F32), ALU.subtract).then_inc(y_lo, 1)

            def gelu_lo(c):
                for f in range(FC):
                    dve.wait_ge(gelu_out, 2 * (c * FC + f + 1))
                    nc.vector.tensor_tensor(g_lo[:, f, :], g_full[:, f % 2, :], g_hi[:, f, :].bitcast(F32),
                                            ALU.subtract).then_inc(g_split, 1)

            def finish(c, first=False):
                dve.wait_ge(ff2, c + 1)
                dve.wait_ge(xy_ready, c + 1)
                if not first:
                    dve.wait_ge(stored, 16 * c)
                for t in range(TILES):
                    node = nodes[:, t:t + 1] if first else nodes[:, bass.ds(c * TILES + t, 1)]
                    nc.vector.scalar_tensor_tensor(out=result[:, t, :], in0=acc4[:, t, :], scalar=node,
                                                   in1=xy[:, t, :], op0=ALU.mult, op1=ALU.add).then_inc(summed, 1)

            divide(0)
            dve.wait_ge(stage3, 1)
            invert(1)
            mix(0, first=True)
            turned_y(0)
            divide(1)
            gelu_lo(0)
            mix(1)
            turned_y(1)
            finish(0, first=True)
            with dve.Fori(1, NCH - 1) as c:
                divide(c + 1)
                gelu_lo(c)
                mix(c + 1)
                turned_y(c + 1)
                finish(c)
            gelu_lo(NCH - 1)
            finish(NCH - 1)

        @block.tensor
        def _(pe):
            def turn(dst, src, t0, signal):
                for t in range(TILES):
                    for d in range(DC):
                        mm = pe.transpose(dst[:, d, t * P:(t + 1) * P], src[:, t0 + t, d * P:(d + 1) * P], ident[:])
                mm.then_inc(signal, 1)

            def project(dst, w_hi, w_lo, hi, lo, signal, groups):
                for g in groups:
                    for d in range(DC):
                        out_cols = slice(g * P, (g + 1) * P)
                        mm = three(pe.matmul, dst[:, g, :], w_hi[:, d, out_cols], w_lo[:, d, out_cols],
                                   hi[:, d, :], lo[:, d, :], d == 0, d == DC - 1)
                mm.then_inc(signal, 1)

            def take_norms(squares, dst, signal):
                for g in range(GROUPS):
                    mm = pe.matmul(dst[:, g, :], headsum[:], squares[:, g, :], start=True, stop=True)
                mm.then_inc(signal, 1)

            def turn_source(c):
                half = c * TILES // HALF
                pe.wait_ge(norm_b, half * (stat_steps(HALF) + HALF) + stat_steps(HALF)
                           + (c + 1) * TILES - half * HALF)
                if c:
                    pe.wait_ge(k_affine, DC * c)
                turn(slot[0], xs, c * TILES, k_turned)

            def turn_target(c, src, dst):
                pe.wait_ge(norm_t, (c + 1) * LN_STEPS)
                turn(dst, src, 0, turned)

            def project_target(c, hi, lo, dst, g):
                pe.wait_ge(lo_ready, c + 1)
                project(dst, wq_hi, wq_lo, hi, lo, projected, [g])

            def target_norms(c, dst):
                pe.wait_ge(squared, c + 1)
                take_norms(squares_late, dst, norms)

            def bound_to_row(c, dst):
                pe.wait_ge(bound_col, c + 1)
                pe.transpose(dst[0:1, 0, 0:P], bound[:], ident[:]).then_inc(bound_row, 1)

            pe.wait_ge(pool_made, 4 + PER)
            turn_source(0)
            pe.wait_ge(w_lo_ready, 3)
            for c in range(NCH):
                hi, lo = RT[c % 2]
                if c + 1 < NCH:
                    turn_source(c + 1)
                else:
                    pe.wait_ge(k_affine, DC * NCH)
                    turn_target(0, rows_first, slot[0])
                pe.wait_ge(k_lo, c + 1)
                if c:
                    pe.wait_ge(k_out, GROUPS * c)
                project(slot[1], wk_hi, wk_lo, hi, lo, k_projected, range(GROUPS))
                if c:
                    pe.wait_ge(v_ready, c)
                for t in range(TILES):
                    for d in range(DC):
                        ts = slice(t * P, (t + 1) * P)
                        mm = three(pe.matmul, acc4[:, t, :], hi[:, d, ts], lo[:, d, ts],
                                   wv_hi[:, d, :], wv_lo[:, d, :], d == 0, d == DC - 1)
                mm.then_inc(v_projected, 1)
                if c + 1 == NCH:
                    for g in range(GROUPS):
                        project_target(0, *RT[0], slot[0], g)
                pe.wait_ge(k_squared, c + 1)
                if c:
                    pe.wait_ge(k_norm_max, 3 + 2 * c - 1)
                take_norms(squares_early, side, k_norms)

            pe.wait_ge(k_norm_max, 3 + 2 * NCH - 1)
            target_norms(0, side)
            bound_to_row(0, side)
            pe.wait_ge(vsum_ready, 1)
            for g in range(GROUPS):
                mm = pe.matmul(acc[:, 0, g:g + 1], vsum[:, g * P:(g + 1) * P], ones[:, 0:1], start=True, stop=True)
            mm.then_inc(vmean_done, 1)
            pe.sem_inc(used, RING)
            pe.sem_inc(closed, 1)

            def load_flag(c):
                pe.wait_ge(flag_ready, 2 * c + 2)
                pe.sem_inc(gate["pe"], 1)
                general = pe.value_load(flag[0:1, 0:1], min_val=0, max_val=1)
                pe.sem_inc(flag_read, 1)
                return general

            def find_maximum(c, general):
                with pe.If(general):
                    pe.wait_ge(masked, c * UNITS + SLOTS)
                    pe.sem_inc(gate["pe"], 1)
                    n = 0
                    for k in range(HEADS // 2):
                        pe.wait_ge(q_copied[k % 2], 16 * (HEADS // 4 * c + k // 2 + 1))
                        for t in range(TILES):
                            for h in range(2):
                                for half in range(2):
                                    if n:
                                        pe.wait_ge(max_masked, c * TILES * HEADS * 2 + n)
                                    for b in range(2):
                                        s0 = (2 * half + b) * CHUNK
                                        mm = pe.matmul(side[:, b, :], qcopy[k % 2][0:AUX, h, t * P:(t + 1) * P],
                                                       kst[0:AUX, 2 * k + h, s0:s0 + CHUNK].bitcast(F32),
                                                       start=True, stop=True)
                                    mm.then_inc(max_scored, 1)
                                    n += 1
                    pe.wait_ge(max_col, 2 * c + 1)
                    pe.transpose(side[0:TILES * HEADS, 0, 0:P], mcol[:], ident[:]).then_inc(max_turned, 1)
                with pe.Else():
                    pe.sem_inc(max_scored, TILES * HEADS * 2)
                    pe.sem_inc(max_turned, 1)

            general = load_flag(0)
            find_maximum(0, general)

            def slot_free(c, what, last=False):
                before = place_before(what, last)
                if not isinstance(before, str):
                    pe.wait_ge(masked, c * UNITS + before + 1 + SLOTS)
                elif before == "turned":
                    pe.wait_ge(affine_out, DC * (c + 2))
                elif before == "norms":
                    pe.wait_ge(norm_max, 2 * (c + 1) + 1)
                elif before == "bound":
                    pe.wait_ge(flag_ready, 2 * (c + 1) + 1)
                else:
                    pe.wait_ge(proj_out, GROUPS * (c + 1) + int(before[-1]) + 1)

            def scores(c, u, last=False):
                g, i, pair = u // UG, u % UG // PAIRS, u % PAIRS
                slot_free(c, u, last)
                for k in range(2):
                    h = g * PER + 2 * pair + k
                    mm = pe.matmul(slot[place(u, last)][:, k, :], kst[0:KROWS, h, i * P:(i + 1) * P],
                                   qst_flat[0:KROWS, bass.ds(qpart(c) + h, 1), :].rearrange("p o t -> p (o t)"),
                                   start=True, stop=True)
                mm.then_inc(scored, 1)

            def context(c, g, i):
                u = (g * ST + i) * PAIRS
                pe.wait_ge(exped, c * UNITS + u + PAIRS)
                if i == 0:
                    pe.wait_ge(evacuated, 2 * (c * GROUPS + g) + 1)
                for j in range(PER):
                    h = g * PER + j
                    mm = pe.matmul(acc[HD * j:HD * j + HD, 0, :], V[:, i, h * HD:(h + 1) * HD],
                                   probs[:, (u + j // 2) % RING, j % 2, :], start=(i == 0), stop=(i == ST - 1))
                if i == ST - 1:
                    mm.then_inc(context_done, 1)
                elif i in ADDED:
                    mm.then_inc(used, PAIRS)

            def add_sums(c, g, i):
                u = (g * ST + i) * PAIRS
                first = i == TAKEN[0]
                if first:
                    pe.wait_ge(evacuated, 2 * (c * GROUPS + g) + 2)
                for j in range(PER):
                    mm = pe.matmul(acc[HD * j:HD * j + HD, 1, :], ones[:], probs[:, (u + j // 2) % RING, j % 2, :],
                                   start=first, stop=False)
                mm.then_inc(used, PAIRS)

            def close(c, g):
                pe.wait_ge(added, c * ADDS + (g + 1) * OPS + 1)
                for j in range(PER):
                    mm = pe.matmul(acc[HD * j:HD * j + HD, 1, :], ones[:], psum2[:, j // 2, j % 2, :],
                                   start=False, stop=True)
                mm.then_inc(closed, 1)

            def queries_ready(c):
                pe.wait_ge(stacked, STACKS * (c + 1))
                pe.wait_ge(q_zeroed, 16 * (c + 1))
                pe.wait_ge(max_stacked, 16 * 2 * TILES * (c + 1))

            def chunk(c, last):
                n = c + 1
                steps = {
                    "turned": lambda dst: turn_target(n, rows, dst),
                    "projected 0": lambda dst: project_target(n, late_hi, late_lo, dst, 0),
                    "projected 1": lambda dst: project_target(n, late_hi, late_lo, dst, 1),
                    "norms": lambda dst: target_norms(n, dst),
                    "bound": lambda dst: bound_to_row(n, dst)}
                for u in range(UNITS):
                    if not last and u + AHEAD in BORROWED:
                        step = BORROWED[u + AHEAD]
                        slot_free(c, step)
                        steps[step](slot[place(step)])
                    if not last and u == UNITS - AHEAD:
                        find_maximum(n, load_flag(n))
                    if u + AHEAD < UNITS:
                        scores(c, u + AHEAD, last)
                    elif not last:
                        if u == UNITS - AHEAD:
                            queries_ready(n)
                        scores(n, u + AHEAD - UNITS)
                    k = u // PAIRS
                    if u == UG:
                        close(c, 0)
                    if u % PAIRS == 0:
                        context(c, k // ST, k % ST)
                    elif k % ST not in ADDED:
                        add_sums(c, k // ST, k % ST)
                close(c, GROUPS - 1)

            pe.wait_ge(keys_oned, 1)
            for k in range(2):
                pe.wait_ge(k_stacked[k], STACKS * NCH // 2)
            queries_ready(0)
            for u in range(AHEAD):
                scores(0, u)
            with pe.Fori(0, NCH - 1) as c:
                chunk(c, False)
            chunk(NCH - 1, True)

            pe.wait_ge(w3_lo, 3)

            def attend(c):
                pe.wait_ge(c_lo, c + 1)
                for t in range(TILES):
                    ts = slice(t * P, (t + 1) * P)
                    for d in range(DC):
                        mm = three(pe.matmul, side4[:, t, :], cT_hi[:, d, ts], cT_lo[:, d, ts],
                                   wo_hi[:, d, :], wo_lo[:, d, :], d == 0, d == DC - 1)
                mm.then_inc(attended, 1)

            def turn_y(c):
                pe.wait_ge(norm_y, (c + 1) * LN_STEPS)
                turn(side, y, 0, y_turned)

            def widen(c, first=False):
                pe.wait_ge(y_lo, c + 1)
                for f in range(FC):
                    if not (first and f < 4):
                        pe.wait_ge(gelu_out, 2 * (c * FC + f - 3))
                    fs = slice(f * P, (f + 1) * P)
                    for d in range(DC):
                        mm = three(pe.matmul, slot[f % 2][:, f // 2 % 2, :], w1_hi[:, d, fs], w1_lo[:, d, fs],
                                   yT_hi[:, d, :], yT_lo[:, d, :], d == 0, d == DC - 1)
                    mm.then_inc(ff1, 1)

            def narrow(c, first=False, last=False):
                pe.wait_ge(g_split, FC * (c + 1))
                if not first:
                    pe.wait_ge(summed, TILES * c)
                for t in range(TILES):
                    if t == TILES - 1 and not last:
                        turn_y(c + 1)
                    ts = slice(t * P, (t + 1) * P)
                    for f in range(FC):
                        mm = three(pe.matmul, acc4[:, t, :], g_hi[:, f, ts], g_lo[:, f, ts],
                                   w2_hi[:, f, :], w2_lo[:, f, :], f == 0, f == FC - 1)
                mm.then_inc(ff2, 1)

            attend(0)
            turn_y(0)
            widen(0, first=True)
            attend(1)
            narrow(0, first=True)
            with pe.Fori(1, NCH - 1) as c:
                widen(c)
                attend(c + 1)
                narrow(c)
            widen(NCH - 1)
            narrow(NCH - 1, last=True)


_INS = ['x', 'adj', 'nodemask', 'L0_gnn_h_target', 'L0_gnn_ln1_scale', 'L0_gnn_ln1_bias', 'L0_gnn_Wq', 'L0_gnn_bq',
        'L0_gnn_Wk', 'L0_gnn_bk', 'L0_gnn_Wv', 'L0_gnn_bv', 'L0_gnn_Wo', 'L0_gnn_bo', 'L0_gnn_ln2_scale',
        'L0_gnn_ln2_bias', 'L0_gnn_W1', 'L0_gnn_W2']


def kernel(**inputs):
    import numpy as _np
    import concourse.bacc as _bacc
    from concourse import mybir as _mybir
    from concourse.bass_utils import run_bass_kernel_spmd as _run

    nc = _bacc.Bacc("TRN2", target_bir_lowering=False, num_devices=1)
    arrays, args = {}, []
    for name in _INS:
        a = _np.ascontiguousarray(inputs[name])
        arrays[f"in_{name}"] = a
        args.append(nc.dram_tensor(f"in_{name}", a.shape, _mybir.dt.from_np(a.dtype), kind="ExternalInput").ap())
    shape = inputs['x'].shape
    args.append(nc.dram_tensor("out_0", shape, _mybir.dt.float32, kind="ExternalOutput").ap())
    graph_attention(nc, *args)
    r = _run(nc, [arrays], core_ids=[0])
    return r.results[0]["out_0"]
```
